# Optimizing a Trainium2 kernel written in Bass

```python
import numpy as np
import jax
import jax.numpy as jnp

def _softmax(x, axis=-1):
    return jax.nn.softmax(x, axis=axis)

def _gelu(x):
    return jax.nn.gelu(x, approximate=True)

def _silu(x):
    return jax.nn.silu(x)

def _sigmoid(x):
    return jax.nn.sigmoid(x)

def _layernorm(x, axis=-1, eps=1e-05):
    m = jnp.mean(x, axis=axis, keepdims=True)
    v = jnp.var(x, axis=axis, keepdims=True)
    return (x - m) / jnp.sqrt(v + eps)

def _scatter_add(tgt, idx, src, axis=0):
    return tgt.at[idx].add(src)

def _segment_sum(src, seg, n):
    return jax.ops.segment_sum(src, seg, n)
kernel_name = 'mk_hybrid_d1_jaxref_r4_0f58e4'

def setup_inputs(seed: int=0):
    np.random.seed(seed)
    _w = jnp.asarray

    def _L0_attn_a_setup():
        import jax, jax.numpy as jnp
        import numpy as np
        N_HEAD = 16
        BUCKET = 64
        HIDDEN = 256
        EPS = 1e-05

        def _ln(x, g, b):
            m = x.mean(-1, keepdims=True)
            v = x.var(-1, keepdims=True)
            return (x - m) * jax.lax.rsqrt(v + EPS) * g + b
        key = jax.random.key(seed)
        ks = jax.random.split(key, 6)

        def w(k, shape, s=0.02):
            return jax.random.normal(k, shape, jnp.float32) * s
        C = HIDDEN
        return {'x': jax.random.normal(ks[0], (4, 2048, C), jnp.float32), 'ln1_g': jnp.ones((C,), jnp.float32), 'ln1_b': jnp.zeros((C,), jnp.float32), 'w_qkv': w(ks[1], (C, 3 * C)), 'b_qkv': jnp.zeros((3 * C,), jnp.float32), 'w_out': w(ks[2], (C, C)), 'b_out': jnp.zeros((C,), jnp.float32), 'ln2_g': jnp.ones((C,), jnp.float32), 'ln2_b': jnp.zeros((C,), jnp.float32), 'w1': w(ks[3], (C, 4 * C)), 'b1': jnp.zeros((4 * C,), jnp.float32), 'w2': w(ks[4], (4 * C, C)), 'b2': jnp.zeros((C,), jnp.float32)}
    _L0_attn_a_in = _L0_attn_a_setup()

    def _L0_attn_b_setup():
        import jax, jax.numpy as jnp
        import numpy as np
        D_MODEL = 256
        N_HEADS = 16
        HEAD_DIM = D_MODEL // N_HEADS
        BATCH = 2
        SEQ = 512

        def _alibi_bias(seq_len, n_heads, dtype):
            slopes = 1.0 / 2.0 ** (jnp.arange(n_heads, dtype=dtype) / n_heads)
            rel = jnp.arange(seq_len, dtype=dtype)[None, :] - jnp.arange(seq_len, dtype=dtype)[:, None]
            return slopes[:, None, None] * rel[None, :, :]
        key = jax.random.key(seed)
        ks = jax.random.split(key, 9)
        s = 0.02
        return {'x': jax.random.normal(ks[0], (BATCH, SEQ, D_MODEL), dtype=jnp.float32), 'Wq': jax.random.normal(ks[1], (D_MODEL, D_MODEL), dtype=jnp.float32) * s, 'bq': jnp.zeros((D_MODEL,), dtype=jnp.float32), 'Wk': jax.random.normal(ks[2], (D_MODEL, D_MODEL), dtype=jnp.float32) * s, 'bk': jnp.zeros((D_MODEL,), dtype=jnp.float32), 'Wv': jax.random.normal(ks[3], (D_MODEL, D_MODEL), dtype=jnp.float32) * s, 'bv': jnp.zeros((D_MODEL,), dtype=jnp.float32), 'Wo': jax.random.normal(ks[4], (D_MODEL, D_MODEL), dtype=jnp.float32) * s, 'bo': jnpp_zeros() if False else jnp.zeros((D_MODEL,), dtype=jnp.float32)}
    _L0_attn_b_in = _L0_attn_b_setup()

    def _L0_ffn_setup():
        import jax, jax.numpy as jnp
        import numpy as np
        import math
        B, S, H = (8, 1024, 256)
        E, I, K = (8, 512, 2)
        CAP_FACTOR = 1.0

        def _router(x, expert_embeddings):
            dot = jnp.einsum('bsh,eh->bse', x, expert_embeddings)
            n = dot.shape[0] * dot.shape[1]
            dot2 = dot.reshape(n, E)
            vals, idx = jax.lax.top_k(dot2, K)
            rows = jnp.arange(n)[:, None]
            masked = jnp.full_like(dot2, -jnp.inf).at[rows, idx].set(vals)
            return jax.nn.softmax(masked, axis=-1)
        key = jax.random.key(seed)
        k1, k2, k3, k4 = jax.random.split(key, 4)

        def kaiming(k, shape):
            bound = math.sqrt(3.0 / shape[-1])
            return jax.random.uniform(k, shape, jnp.float32, -bound, bound)
        x = jax.random.normal(k1, (B, S, H), jnp.float32)
        expert_embeddings = kaiming(k2, (E, H))
        first_linear = kaiming(k3, (E, I, H))
        second_linear = kaiming(k4, (E, H, I))
        return {'x': x, 'expert_embeddings': expert_embeddings, 'first_linear': first_linear, 'second_linear': second_linear}
    _L0_ffn_in = _L0_ffn_setup()
    _d = {'L0_attn_a_x': _L0_attn_a_in['x'], 'L0_attn_a_ln1_g': _L0_attn_a_in['ln1_g'], 'L0_attn_a_ln1_b': _L0_attn_a_in['ln1_b'], 'L0_attn_a_w_qkv': _L0_attn_a_in['w_qkv'], 'L0_attn_a_b_qkv': _L0_attn_a_in['b_qkv'], 'L0_attn_a_w_out': _L0_attn_a_in['w_out'], 'L0_attn_a_b_out': _L0_attn_a_in['b_out'], 'L0_attn_a_ln2_g': _L0_attn_a_in['ln2_g'], 'L0_attn_a_ln2_b': _L0_attn_a_in['ln2_b'], 'L0_attn_a_w1': _L0_attn_a_in['w1'], 'L0_attn_a_b1': _L0_attn_a_in['b1'], 'L0_attn_a_w2': _L0_attn_a_in['w2'], 'L0_attn_a_b2': _L0_attn_a_in['b2'], 'L0_attn_b_Wq': _L0_attn_b_in['Wq'], 'L0_attn_b_bq': _L0_attn_b_in['bq'], 'L0_attn_b_Wk': _L0_attn_b_in['Wk'], 'L0_attn_b_bk': _L0_attn_b_in['bk'], 'L0_attn_b_Wv': _L0_attn_b_in['Wv'], 'L0_attn_b_bv': _L0_attn_b_in['bv'], 'L0_attn_b_Wo': _L0_attn_b_in['Wo'], 'L0_attn_b_bo': _L0_attn_b_in['bo'], 'L0_ffn_expert_embeddings': _L0_ffn_in['expert_embeddings'], 'L0_ffn_first_linear': _L0_ffn_in['first_linear'], 'L0_ffn_second_linear': _L0_ffn_in['second_linear']}
    _x0 = _d['L0_attn_a_x']
    _d['L0_attn_a_x'] = jax.random.normal(jax.random.fold_in(jax.random.key(seed), 1), (32, 512, 256), dtype=_x0.dtype)
    del _x0
    return _d

def reference(L0_attn_a_x, L0_attn_a_ln1_g, L0_attn_a_ln1_b, L0_attn_a_w_qkv, L0_attn_a_b_qkv, L0_attn_a_w_out, L0_attn_a_b_out, L0_attn_a_ln2_g, L0_attn_a_ln2_b, L0_attn_a_w1, L0_attn_a_b1, L0_attn_a_w2, L0_attn_a_b2, L0_attn_b_Wq, L0_attn_b_bq, L0_attn_b_Wk, L0_attn_b_bk, L0_attn_b_Wv, L0_attn_b_bv, L0_attn_b_Wo, L0_attn_b_bo, L0_ffn_expert_embeddings, L0_ffn_first_linear, L0_ffn_second_linear):

    def _L0_attn_a_ref(x, ln1_g, ln1_b, w_qkv, b_qkv, w_out, b_out, ln2_g, ln2_b, w1, b1, w2, b2):
        import jax, jax.numpy as jnp
        import numpy as np
        N_HEAD = 16
        BUCKET = 64
        HIDDEN = 256
        EPS = 1e-05

        def _ln(x, g, b):
            m = x.mean(-1, keepdims=True)
            v = x.var(-1, keepdims=True)
            return (x - m) * jax.lax.rsqrt(v + EPS) * g + b
        B, T, C = x.shape
        nb = T // BUCKET
        hd = C // N_HEAD
        scale = 1.0 / np.sqrt(hd)
        h = _ln(x, ln1_g, ln1_b)
        qkv = h @ w_qkv + b_qkv
        q, k, v = jnp.split(qkv, 3, axis=-1)

        def buck(t):
            return t.reshape(B, nb, BUCKET, N_HEAD, hd)
        qb, kb, vb = (buck(q), buck(k), buck(v))
        kp = jnp.concatenate([jnp.zeros_like(kb[:, :1]), kb[:, :-1]], axis=1)
        vp = jnp.concatenate([jnp.zeros_like(vb[:, :1]), vb[:, :-1]], axis=1)
        kc = jnp.concatenate([kp, kb], axis=2)
        vc = jnp.concatenate([vp, vb], axis=2)
        scores = jnp.einsum('bnihd,bnjhd->bnhij', qb, kc) * scale
        i = jnp.arange(BUCKET)[:, None]
        j = jnp.arange(2 * BUCKET)[None, :]
        mask = (j < BUCKET) | (j - BUCKET <= i)
        scores = jnp.where(mask, scores, -jnp.inf)
        attn = jax.nn.softmax(scores, axis=-1)
        ob = jnp.einsum('bnhij,bnjhd->bnihd', attn, vc).reshape(B, T, C)
        x = x + ob @ w_out + b_out
        h2 = _ln(x, ln2_g, ln2_b)
        m = jax.nn.gelu(h2 @ w1 + b1, approximate=False) @ w2 + b2
        return x + m

    def _L0_attn_b_ref(x, Wq, bq, Wk, bk, Wv, bv, Wo, bo):
        import jax, jax.numpy as jnp
        import numpy as np
        D_MODEL = 256
        N_HEADS = 16
        HEAD_DIM = D_MODEL // N_HEADS
        BATCH = 2
        SEQ = 512

        def _alibi_bias(seq_len, n_heads, dtype):
            slopes = 1.0 / 2.0 ** (jnp.arange(n_heads, dtype=dtype) / n_heads)
            rel = jnp.arange(seq_len, dtype=dtype)[None, :] - jnp.arange(seq_len, dtype=dtype)[:, None]
            return slopes[:, None, None] * rel[None, :, :]
        B, S, D = x.shape
        H, Hd = (N_HEADS, HEAD_DIM)
        scale = Hd ** (-0.5)
        Q = (x @ Wq + bq).reshape(B, S, H, Hd)
        K = (x @ Wk + bk).reshape(B, S, H, Hd)
        V = (x @ Wv + bv).reshape(B, S, H, Hd)
        scores = jnp.einsum('bqhd,bkhd->bhqk', Q, K) * scale
        scores = scores + _alibi_bias(S, H, x.dtype)[None]
        attn = jax.nn.softmax(scores, axis=-1)
        out = jnp.einsum('bhqk,bkhd->bqhd', attn, V).reshape(B, S, D)
        return out @ Wo + bo

    def _L0_ffn_ref(x, expert_embeddings, first_linear, second_linear):
        import jax, jax.numpy as jnp
        import numpy as np
        import math
        B, S, H = (8, 1024, 256)
        E, I, K = (8, 512, 2)
        CAP_FACTOR = 1.0

        def _router(x, expert_embeddings):
            dot = jnp.einsum('bsh,eh->bse', x, expert_embeddings)
            n = dot.shape[0] * dot.shape[1]
            dot2 = dot.reshape(n, E)
            vals, idx = jax.lax.top_k(dot2, K)
            rows = jnp.arange(n)[:, None]
            masked = jnp.full_like(dot2, -jnp.inf).at[rows, idx].set(vals)
            return jax.nn.softmax(masked, axis=-1)
        batch, seq, hidden = x.shape
        n_tokens = batch * seq
        expert_capacity = math.ceil(n_tokens / E * CAP_FACTOR)
        weights = _router(x, expert_embeddings)
        ones = (weights > 0).astype(weights.dtype)
        cap_ones = jnp.where(jnp.cumsum(ones, axis=0) <= expert_capacity, ones, 0.0)
        caw = weights * cap_ones
        vals, idx = jax.lax.top_k(caw.T, expert_capacity)
        index = idx.reshape(-1)
        x_flat = x.reshape(n_tokens, hidden)
        tokens = x_flat[index].reshape(E, expert_capacity, hidden)
        inter = jax.nn.relu(jnp.einsum('ech,eih->eci', tokens, first_linear))
        out = jnp.einsum('eci,ehi->ech', inter, second_linear)
        out = out * vals[:, :, None]
        final = jnp.zeros((n_tokens, hidden), x.dtype).at[index].add(out.reshape(-1, hidden))
        return final.reshape(x.shape)
    x = L0_attn_a_x
    x = x + _L0_attn_a_ref(_layernorm(x, axis=-1), L0_attn_a_ln1_g, L0_attn_a_ln1_b, L0_attn_a_w_qkv, L0_attn_a_b_qkv, L0_attn_a_w_out, L0_attn_a_b_out, L0_attn_a_ln2_g, L0_attn_a_ln2_b, L0_attn_a_w1, L0_attn_a_b1, L0_attn_a_w2, L0_attn_a_b2)
    x = x + _L0_ffn_ref(_layernorm(x, axis=-1), L0_ffn_expert_embeddings, L0_ffn_first_linear, L0_ffn_second_linear)
    x = x + _L0_attn_b_ref(_layernorm(x, axis=-1), L0_attn_b_Wq, L0_attn_b_bq, L0_attn_b_Wk, L0_attn_b_bk, L0_attn_b_Wv, L0_attn_b_bv, L0_attn_b_Wo, L0_attn_b_bo)
    x = x + _L0_ffn_ref(_layernorm(x, axis=-1), L0_ffn_expert_embeddings, L0_ffn_first_linear, L0_ffn_second_linear)
    return x

_drawn_inputs = setup_inputs


def setup_inputs(seed=0):
    import zlib

    import numpy as np

    out = dict(_drawn_inputs(seed))
    spreads = {'L0_attn_a_ln1_g': (1.0, 0.6),
     'L0_attn_a_ln1_b': (0.0, 0.351),
     'L0_attn_a_b_qkv': (0.0, 0.1),
     'L0_attn_a_b_out': (0.0, 0.1),
     'L0_attn_a_ln2_g': (1.0, 0.6),
     'L0_attn_a_ln2_b': (0.0, 0.353),
     'L0_attn_a_b1': (0.0, 0.1),
     'L0_attn_a_b2': (0.0, 0.1),
     'L0_attn_b_bq': (0.0, 0.8),
     'L0_attn_b_bk': (0.0, 0.8),
     'L0_attn_b_bv': (0.0, 0.1),
     'L0_attn_b_bo': (0.0, 0.1)}
    factors = {'L0_attn_b_Wq': 7.35, 'L0_attn_b_Wk': 8.0}
    for name, (base, spread) in spreads.items():
        noise = np.random.default_rng([zlib.crc32(name.encode()), seed]).standard_normal(out[name].shape)
        drawn = base * np.exp(spread * noise) if base else spread * noise
        out[name] = jnp.asarray(drawn.astype(out[name].dtype))
    for name, factor in factors.items():
        out[name] = (out[name] * factor).astype(out[name].dtype)
    return out
```

```python
from contextlib import ExitStack

import concourse.bass as bass
from concourse import mybir

F32 = mybir.dt.float32
F32R = mybir.dt.float32r
BF16 = mybir.dt.bfloat16
U32 = mybir.dt.uint32
ACT = mybir.ActivationFunctionType
ALU = mybir.AluOpType
AX = mybir.AxisListType

P = 128
NB, T, C = 32, 512, 256
TT = T // P
CT = C // P
NH, HD = 16, 16
NPAIR = NH // 2
HG = 4
NG = NH // HG
BUCKET = 64
KPAD = BUCKET + T
NE, TOPK, EI = 8, 2, 512
CAP = NB * T // NE
FF = 4 * C
FT = FF // P
EPS = 1e-5
BIG = 65536.0
STACK = 6 * HD


class Turns:

    def __init__(self, jobs):
        self.per, self.of = {}, {}
        for name, bank in jobs:
            k = self.per.get(bank, 0)
            self.of[name] = (bank, k)
            self.per[bank] = k + 1

    def bank(self, job):
        return self.of[job][0]

    def turn(self, i, job):
        bank, k = self.of[job]
        return i * self.per[bank] + k + 1

    def drained(self, i, job):
        return self.turn(i, job) + 1


class Chain:

    def __init__(self, sem, engine, per, passed):
        self.sem, self.engine, self.per, self.passed, self.n, self.i = sem, engine, per, passed, 0, 0

    def start(self, i):
        self.i, self.n = i, 0

    def link(self, ins):
        self.n += 1
        assert self.n <= self.per, "more links than per"
        ins.then_inc(self.sem, 1)
        self.engine.wait_ge(self.sem, self.i * self.per + self.n)

    def end(self):
        assert self.n == self.per, f"links: {self.n}, per: {self.per}"


def apart(engine, passed):
    engine.sem_inc(passed, 1)


def pairs(engine, sequence):
    with engine.Fori(0, NB // 2) as j:
        for p in range(2):
            sequence(2 * j + p, p)


def all_but_last(engine, sequence):
    with engine.Fori(0, NB // 2 - 1) as j:
        for p in range(2):
            sequence(2 * j + p, p, False)
    sequence(NB - 2, 0, False)
    sequence(NB - 1, 1, True)


def rows(ap, i):
    return ap[bass.ds(i * T, T), :].rearrange("(t p) c -> p t c", p=P)


STACK_DMAS = 6 * NH


def stack(sp, sem, QS, KS, kcol, parts):
    for h in range(NH):
        half, at, row = h // 8, HD * (h % 8), 3 * HD * (h % 2)
        for blk, (q, k) in enumerate((("q_hi", "k_hi"), ("q_hi", "k_lo"), ("q_lo", "k_hi"))):
            to = row + HD * blk
            sp.dma_start(QS[to:to + HD, h, :].bitcast(F32), parts[q][at:at + HD, half, :].bitcast(F32)).then_inc(sem, 16)
            sp.dma_start(KS[to:to + HD, h // 2, kcol:kcol + T].bitcast(F32),
                         parts[k][at:at + HD, half, :].bitcast(F32)).then_inc(sem, 16)


def statistics(nc, chain, src, st, mv, ready):
    for t in range(TT):
        ins = nc.vector.bn_stats(st[:, t, :], src[:, t, :])
    chain.link(ins)
    apart(chain.engine, chain.passed)
    for t in range(TT):
        ins = nc.vector.bn_aggr(mv[:, t, :], st[:, t, :])
    ins.then_inc(ready, 1)


def normalize(nc, src, dst, mv, rs):
    for t in range(TT):
        ins = nc.vector.tensor_scalar(dst[:, t, :], src[:, t, :], mv[:, t, 0:1], rs[:, t:t + 1],
                                      ALU.subtract, ALU.mult)
    return ins


def transposes(nc, dst, src, c, ident):
    for t in range(TT):
        ins = nc.tensor.transpose(dst[:, t * P:(t + 1) * P], src[:, t, c * P:(c + 1) * P], ident[:])
    return ins


def route_tiles(sb):
    b = {n: sb(n, [P, TT, NE]) for n in ("lg", "lg2", "eq", "rank", "slot", "prod")}
    b |= {"o": sb("o", [P, TOPK, TT, NE]), "oh": sb("oh", [P, TT * NE], BF16), "carry": sb("carry", [P, NE])}
    b |= {n: sb(n, [P, TOPK, TT]) for n in ("m", "p", "r", "s", "kept")}
    b |= {n: sb(n, [P, TT]) for n in ("pm", "gap", "e2")}
    b["idx"] = sb("idx", [P, TOPK * TT], U32)
    return b


ROUTER_LINKS = 11 + 5 + 2 + 8 + 3


def router(nc, dve, link, b, w, J, bank, full, free, S, i, tab):
    V = nc.vector
    lg, lg2, eq, o, m, pm, p, rank, slot, r, s, kept, prod = (b[n] for n in (
        "lg", "lg2", "eq", "o", "m", "pm", "p", "rank", "slot", "r", "s", "kept", "prod"))

    def over_experts(ap):
        return ap.unsqueeze(2).broadcast_to([P, TT, NE])

    logit, cum = J.bank("logit"), J.bank("cum")
    dve.wait_ge(full[logit], J.turn(i, "logit"))
    V.tensor_copy(lg[:], bank[logit][:, 0:TT * NE].rearrange("p (t e) -> p t e", e=NE)).then_inc(free[logit], 1)
    dve.wait_ge(free[logit], J.drained(i, "logit"))
    src = lg
    for k in range(TOPK):
        link(V.tensor_reduce(m[:, k, :], src[:], AX.X, ALU.max))
        link(V.tensor_tensor(eq[:], src[:], over_experts(m[:, k, :]), ALU.is_equal))
        link(V.tensor_tensor(eq[:], eq[:], w["rev"][:], ALU.mult))
        link(V.tensor_reduce(pm[:], eq[:], AX.X, ALU.max))
        link(V.tensor_tensor(o[:, k, :, :], eq[:], over_experts(pm[:]), ALU.is_equal))
        if k == 0:
            link(V.scalar_tensor_tensor(lg2[:], o[:, 0, :, :], -3e38, lg[:], ALU.mult, ALU.add))
            src = lg2
    V.tensor_tensor(b["gap"][:], m[:, 1, :], m[:, 0, :], ALU.subtract).then_inc(S["gap_ready"], 1)
    dve.wait_ge(S["gap_exp"], i + 1)
    link(V.tensor_scalar(pm[:], b["e2"][:], 1.0, None, ALU.add))
    link(V.reciprocal(p[:, 0, :], pm[:]))
    link(V.tensor_tensor(p[:, 1, :], p[:, 0, :], b["e2"][:], ALU.mult))
    link(V.tensor_scalar(pm[:], p[:, 1, :], 0.0, None, ALU.is_gt))
    link(V.tensor_tensor(o[:, 1, :, :], o[:, 1, :, :], over_experts(pm[:]), ALU.mult))
    V.tensor_tensor(b["oh"][:].rearrange("p (t e) -> p t e", e=NE), o[:, 0, :, :], o[:, 1, :, :],
                    ALU.add).then_inc(S["picks_ready"], 1)
    dve.wait_ge(full[cum], J.turn(i, "cum"))
    link(V.tensor_tensor(rank[:], bank[cum][:, 0:TT * NE].rearrange("p (t e) -> p t e", e=NE),
                         b["carry"][:].unsqueeze(1).broadcast_to([P, TT, NE]), ALU.add))
    V.tensor_tensor(b["carry"][:], bank[cum][:, TT * NE:TT * NE + NE], b["carry"][:], ALU.add).then_inc(free[cum], 1)
    link(V.tensor_tensor(slot[:], rank[:], w["base"][:], ALU.add))
    for k in range(TOPK):
        for what, dst in ((rank, r), (slot, s)):
            link(V.tensor_tensor(prod[:], o[:, k, :, :], what[:], ALU.mult))
            link(V.tensor_reduce(dst[:, k, :], prod[:], AX.X, ALU.add))
    link(V.tensor_scalar(kept[:], r[:], 1.0, None, ALU.is_ge))
    link(V.scalar_tensor_tensor(kept[:], r[:], float(CAP), kept[:], ALU.is_le, ALU.mult))
    link(V.tensor_scalar(r[:], kept[:], -BIG, BIG, ALU.mult, ALU.add))
    V.tensor_tensor(tab["w"][:, bass.ds(i * TOPK * TT, TOPK * TT)].rearrange("p (k t) -> p k t", t=TT),
                    p[:], kept[:], ALU.mult)
    V.tensor_tensor(b["idx"][:].rearrange("p (k t) -> p k t", t=TT), s[:], r[:], ALU.add).then_inc(S["idx_ready"], 1)


def count_picks(nc, pe, b, w, J, bank, full, free, S, i):
    n = J.bank("cum")
    pe.wait_ge(free[n], J.turn(i, "cum"))
    pe.wait_ge(S["picks_ready"], i + 1)
    for t in range(TT + 1):
        for u in range(min(t + 1, TT)):
            tri = u == t
            ins = nc.tensor.matmul(bank[n][:, t * NE:(t + 1) * NE], (w["tri"] if tri else w["ones"])[:],
                                   b["oh"][:, u * NE:(u + 1) * NE], start=u == 0, stop=u == min(t, TT - 1))
    ins.then_inc(full[n], 1)


def logits(nc, pe, zT, wr, J, bank, full, free, i):
    n = J.bank("logit")
    pe.wait_ge(free[n], J.turn(i, "logit"))
    for c in range(CT):
        pe.wait_ge(free[J.bank(("zT", c))], J.drained(i, ("zT", c)))
    for t in range(TT):
        for c in range(CT):
            ins = nc.tensor.matmul(bank[n][:, t * NE:(t + 1) * NE], zT[:, c, t * P:(t + 1) * P], wr[:, c, :],
                                   start=c == 0, stop=c == CT - 1)
    ins.then_inc(full[n], 1)


def send_rows(nc, pool, z, b, d, S, i, tab):
    pool.wait_ge(S["idx_ready"], i + 1)
    apart(pool, S["pool_passed"])
    nc.gpsimd.tensor_copy(tab["idx"][:, bass.ds(i * TOPK * TT, TOPK * TT)], b["idx"][:])
    for n in range(TOPK * TT):
        pool.indirect_dma_start(d["queue"], bass.IndirectOffsetOnAxis(ap=b["idx"][:, n:n + 1], axis=0),
                                z[:, n % TT, :], None, bounds_check=NE * CAP - 1, oob_is_err=False).then_inc(S["sent"], 16)
    pool.wait_ge(S["sent"], 16 * TOPK * TT * (i + 1))


def root(nc, pool, link, mv, rs, rt, half, stats, turn, done, passed):
    pool.wait_ge(stats, turn)
    apart(pool, passed)
    link(nc.gpsimd.tensor_scalar(rt[:, 0, :], mv[:, :, 1], EPS, None, ALU.add))
    nc.gpsimd.tensor_tensor(rs[:, 0, :], rt[:, 0, :], half[:], ALU.pow).then_inc(done, 1)


def values(nc, pe, VT, wv, t, lo, width, J, bank, full, free, i):
    n = J.bank(("v", t))
    pe.wait_ge(free[n], J.turn(i, ("v", t)))
    for c in range(CT):
        ins = nc.tensor.matmul(bank[n][0:width, 0:C], VT[:, c, lo:lo + width], wv[:, c, :], start=c == 0, stop=c == CT - 1)
    ins.then_inc(full[n], 1)


def project(nc, pe, XT, lo, w, m, J, bank, full, free, i):
    n = J.bank(("qk", m))
    pe.wait_ge(free[n], J.turn(i, ("qk", m)))
    for c in range(CT):
        ins = nc.tensor.matmul(bank[n][:], w[:, c, m * P:(m + 1) * P], XT[:, c, lo:lo + T], start=c == 0, stop=c == CT - 1)
    ins.then_inc(full[n], 1)


PARTS = (("q_hi", "q_lo", 0), ("q_hi", "q_lo", 1), ("k_hi", "k_lo", 0), ("k_hi", "k_lo", 1))


def high_parts(nc, act, parts, bqk, J, bank, full, S, i):
    for m, (hi, _, c) in enumerate(PARTS):
        n = J.bank(("qk", m))
        act.wait_ge(full[n], J.turn(i, ("qk", m)))
        nc.scalar.activation(parts[hi][:, c, :], bank[n][:], ACT.Identity, bias=bqk[:, m:m + 1]).then_inc(S["hi_ready"], 1)


def low_parts(nc, dve, parts, bqk, J, bank, free, S, i):
    for m, (hi, lo, c) in enumerate(PARTS):
        n = J.bank(("qk", m))
        dve.wait_ge(S["hi_ready"], 4 * i + m + 1)
        nc.vector.scalar_tensor_tensor(parts[lo][:, c, :], bank[n][:], bqk[:, m:m + 1], parts[hi][:, c, :].bitcast(F32),
                                       ALU.add, ALU.subtract).then_inc(free[n], 1)


def output_tiles(nc, pe, oN, wo, J, bank, full, free, S, i):
    pe.wait_ge(S["on_ready"], NG * i + NG + 2)
    for t in range(TT):
        n = J.bank(("y", t))
        pe.wait_ge(free[n], J.turn(i, ("y", t)))
        for g in range(NG):
            ins = nc.tensor.matmul(bank[n][:, 0:C], oN[:, g, t * P:(t + 1) * P], wo[:, g, :], start=g == 0, stop=g == NG - 1)
        ins.then_inc(full[n], 1)


def spread_sums(nc, pe, g, slotsum, oT, J, bank, full, free, i):
    n = J.bank(("d", g))
    pe.wait_ge(free[n], J.turn(i, ("d", g)))
    pe.wait_ge(free[J.bank(("o", g))], J.drained(i, ("o", g)))
    nc.tensor.matmul(bank[n][:], slotsum[:], oT[:, g % 2, :], start=True, stop=True).then_inc(full[n], 1)


def copy_output(nc, act, g, oT, J, bank, full, free, S, i):
    n = J.bank(("o", g))
    act.wait_ge(full[n], J.turn(i, ("o", g)))
    act.wait_ge(S["on_ready"], NG * i + g + 1)
    nc.scalar.activation(oT[:, g % 2, :], bank[n][:], ACT.Copy).then_inc(free[n], 1)


def invert_sums(nc, dve, g, rD, J, bank, full, free, S, i):
    n = J.bank(("d", g))
    dve.wait_ge(full[n], J.turn(i, ("d", g)))
    dve.wait_ge(S["on_ready"], NG * i + g + 2)
    nc.vector.reciprocal(rD[:], bank[n][:]).then_inc(free[n], 1)


def normalize_outputs(nc, pool, oT, rD, oN, J, free, S, i):
    for g in range(NG):
        pool.wait_ge(free[J.bank(("d", g))], J.drained(i, ("d", g)))
        nc.gpsimd.tensor_tensor(oN[:, g, :], oT[:, g % 2, :], rD[:], ALU.mult).then_inc(S["on_ready"], 1)


def semaphore(nc, used, name):
    used.append(nc.alloc_semaphore(name))
    return used[-1]


def banks(nc, ctx, used, prefix):
    return ([ctx.enter_context(nc.psum_tensor(f"{prefix}_bank{n}", [P, 512], F32)) for n in range(8)],
            [semaphore(nc, used, f"{prefix}_full{n}") for n in range(8)],
            [semaphore(nc, used, f"{prefix}_free{n}") for n in range(8)])


def sems(nc, used, prefix, names):
    return {n: semaphore(nc, used, f"{prefix}_{n}") for n in names.split()}


def open_banks(pe, free):
    for f in free:
        pe.sem_inc(f, 1)


def load_all(engine, sem, loads):
    for dst, src in loads:
        engine.dma_start(dst, src).then_inc(sem, 16)
    return 16 * len(loads)


def slots_of(w_out):
    return w_out.rearrange("(g s d) n -> s d g n", g=NG, s=HG)


NKT, QW = 5, 3 * BUCKET


def queries_of(kt):
    q0, q1 = max(0, P * kt - BUCKET), min(T, P * kt + 2 * BUCKET)
    return q0, q1, q0 - (P * kt - BUCKET)


def phase_local(nc, ctx, used, a, d, tab):
    jobs = [(("hT", c), c) for c in range(CT)]
    jobs += [(("qk", m), (2, 3, 0, 1)[m]) for m in range(4)]
    jobs += [(("v", t), 2 + t % 2) for t in range(NKT)]
    jobs += [(("s", t, hp), 4 + hp % 2) for t in range(TT) for hp in range(NPAIR)]
    jobs += [("mT", 0)]
    for g in range(NG):
        jobs += [(("st", g, kt, e), e + 2 * (kt % 2)) for kt in range(NKT) for e in range(2)]
        jobs += [(("o", g), 6 + g % 2), (("d", g), 4 + g % 2)]
    jobs += [(("y", t), t) for t in range(TT)]
    jobs += [(("h2T", c), 4 + c) for c in range(CT)]
    jobs += [(("f1", m), m % 4) for m in range(FT)]
    jobs += [(("f2", t), 4 + t % 2) for t in range(TT)]
    jobs += [(("zT", c), 6 + c) for c in range(CT)]
    jobs += [("logit", 0), ("cum", 1)]
    J = Turns(jobs)

    def sb(name, shape, dt=F32):
        return ctx.enter_context(nc.sbuf_tensor("l_" + name, shape, dt))

    bank, full, free = banks(nc, ctx, used, "l")
    ident, identb, slotsum = sb("ident", [P, P]), sb("identb", [P, P], BF16), sb("slotsum", [P, P])
    masks, mask_q, mask_k = sb("masks", [P, 2, QW]), sb("mask_q", [P, QW], BF16), sb("mask_k", [P, QW], BF16)
    trif = sb("trif", [P, P])
    w = {"tri": sb("tri", [P, P], BF16), "ones": sb("ones", [P, P], BF16),
         "rev": sb("rev", [P, TT, NE]), "base": sb("base", [P, TT, NE])}
    g1, b1, g2, b2 = (sb(n, [P, CT]) for n in ("g1", "b1", "g2", "b2"))
    wqkv, bqk = sb("wqkv", [P, CT, 3 * C]), sb("bqk", [P, 4])
    bv, bo, bf2 = sb("bv", [P, C]), sb("bo", [P, C]), sb("bf2", [P, C])
    wo = sb("wo", [P, NG, C])
    w1, bf1, w2 = sb("w1", [P, CT, FF]), sb("bf1", [P, FT]), sb("w2", [P, FT, C])
    wr, half = sb("wr", [P, CT, NE]), sb("half", [P, TT])
    x = [sb(f"x{p}", [P, TT, C]) for p in range(2)]
    t0, y, z, hh = sb("t0", [P, TT, C]), sb("y", [P, TT, C]), sb("z", [P, TT, C]), sb("hh", [P, TT, C])
    st, mv = sb("st", [P, TT, 6]), sb("mv", [P, TT, 2])
    rs, rt = sb("rs", [P, 2, TT]), sb("rt", [P, 3, TT])
    hT, hT2 = sb("hT", [P, CT, KPAD]), sb("hT2", [P, CT, T])
    parts = {n: sb(n, [P, CT, T], F32R) for n in ("q_hi", "q_lo", "k_hi", "k_lo")}
    QS, KS = sb("QS", [P, NH, T], F32R), sb("KS", [P, NPAIR, KPAD], F32R)
    VP = sb("VP", [P, NKT, NH, 2 * HD])
    nm, mT = sb("nm", [P, TT, NH]), sb("mT", [NH, T], F32R)
    pr = sb("pr", [P, 2, HG, QW])
    oT, rD, oN = sb("oT", [P, 2, T]), sb("rD", [P, T]), sb("oN", [P, NG, T])
    G = sb("G", [P, FT, T])
    b = route_tiles(sb)
    zero = sb("zero", [P, C])

    S = sems(nc, used, "l", """weights out_weights zeroed cleared consts casts x_in0 x_in1 stats rstd t0_ready hh_ready hi_ready
        stacked max_ready m_in pv_done on_ready t0b res_ready x1_out z_ready gap_ready gap_exp picks_ready
        idx_ready sent dve_own pool_own dve_passed pool_passed pe_passed sp_passed""")
    x_in = [S["x_in0"], S["x_in1"]]

    loads = [
        (ident[:], a["c_ident"]), (slotsum[:], a["c_slotsum"]), (masks[:], a["c_masks"]), (trif[:], a["c_tri"]),
        (w["rev"][:], a["c_rev"]), (w["base"][:], a["c_base"]),
        (g1[:], a["ln1_g"]), (b1[:], a["ln1_b"]), (g2[:], a["ln2_g"]), (b2[:], a["ln2_b"]),
        (wqkv[:], a["w_qkv"].rearrange("(c p) n -> p c n", p=P)), (bqk[:], a["b_qk"]),
        (bv[:], a["b_v"].partition_broadcast(P)), (bo[:], a["b_out"].partition_broadcast(P)),
        (bf2[:], a["b2"].partition_broadcast(P)), (w1[:], a["w1"].rearrange("(c p) n -> p c n", p=P)),
        (bf1[:], a["b1"]), (w2[:], a["w2"].rearrange("(m p) n -> p m n", p=P)),
        (wr[:], a["router"].rearrange("(c p) e -> p c e", p=P)),
    ]
    LOADED = 16 * len(loads)
    QUEUE_TILES = NE * CAP // P
    block = ctx.enter_context(nc.Block())

    @block.sync
    def _(sp):
        load_all(sp, S["weights"], loads)
        sp.dma_start(x[0][:], rows(a["x"], 0)).then_inc(x_in[0], 16)
        sp.wait_ge(S["zeroed"], 2)
        load_all(sp, S["out_weights"], [(wo[32 * s:32 * s + HD, :, :], slots_of(a["w_out"])[s]) for s in range(HG)])
        queue = d["queue"].rearrange("(t p) c -> t p c", p=P)
        for t in range(QUEUE_TILES):
            sp.dma_start(queue[t], zero[:]).then_inc(S["cleared"], 16)
        sp.sem_inc(S["x1_out"], 16)
        sp.wait_ge(S["casts"], 16)

        def sequence(i, p, last):
            if not last:
                sp.dma_start(x[1 - p][:], rows(a["x"], i + 1)).then_inc(x_in[1 - p], 16)
            for m in range(4):
                sp.wait_ge(free[J.bank(("qk", m))], J.drained(i, ("qk", m)))
                apart(sp, S["sp_passed"])
            sp.wait_ge(S["pv_done"], NG * NKT * i + 2)
            apart(sp, S["sp_passed"])
            stack(sp, S["stacked"], QS, KS, BUCKET, parts)
            sp.wait_ge(free[J.bank("mT")], J.drained(i, "mT"))
            apart(sp, S["sp_passed"])
            sp.dma_start(QS[STACK:STACK + 1, :, :].bitcast(F32), mT[:, :].bitcast(F32)).then_inc(S["m_in"], 16)
            for t in range(TT):
                sp.wait_ge(free[J.bank(("f2", t))], J.drained(i, ("f2", t)))
                apart(sp, S["sp_passed"])
            sp.dma_start(rows(d["x1"], i), y[:]).then_inc(S["x1_out"], 16)

        all_but_last(sp, sequence)
        sp.wait_ge(S["x1_out"], 16 * NB + 16)

    @block.gpsimd
    def _(pool):
        V = nc.gpsimd
        V.memset(half[:], -0.5)
        pool.wait_ge(S["zeroed"], 2)
        pool.dma_start(KS[STACK:STACK + 1, :, :], a["c_one"]).then_inc(S["casts"], 16)
        pool.sem_inc(S["on_ready"], 2)
        chain = Chain(S["pool_own"], pool, 9, S["pool_passed"])
        pool.wait_ge(S["weights"], LOADED)

        def sequence(i, p):
            chain.start(i)
            pool.wait_ge(S["stats"], 3 * i + 1)
            apart(pool, S["pool_passed"])
            chain.link(V.tensor_scalar(rt[:, 0, :], mv[:, :, 1], EPS, None, ALU.add))
            chain.link(V.tensor_tensor(rs[:, 0, :], rt[:, 0, :], half[:], ALU.pow))
            chain.link(V.tensor_tensor(rt[:, 1, :], rs[:, 0, :], rs[:, 0, :], ALU.mult))
            chain.link(V.tensor_tensor(rt[:, 1, :], rt[:, 1, :], mv[:, :, 1], ALU.mult))
            apart(pool, S["pool_passed"])
            chain.link(V.tensor_scalar(rt[:, 1, :], rt[:, 1, :], EPS, None, ALU.add))
            chain.link(V.tensor_tensor(rt[:, 2, :], rt[:, 1, :], half[:], ALU.pow))
            V.tensor_tensor(rs[:, 1, :], rs[:, 0, :], rt[:, 2, :], ALU.mult).then_inc(S["rstd"], 1)
            pool.wait_ge(S["hh_ready"], 2 * i + 1)
            for t in range(TT):
                ins = V.tensor_tensor(t0[:, t, :], t0[:, t, :], bo[:], ALU.add)
            ins.then_inc(S["t0b"], 1)
            for t in range(TT):
                ins = V.tensor_tensor(x[p][:, t, :], x[p][:, t, :], bf2[:], ALU.add)
            chain.link(ins)
            normalize_outputs(nc, pool, oT, rD, oN, J, free, S, i)
            root(nc, pool, chain.link, mv, rs, rt, half, S["stats"], 3 * i + 2, S["rstd"], S["pool_passed"])
            V.tensor_tensor(x[p][:], x[p][:], y[:], ALU.add).then_inc(S["res_ready"], 1)
            root(nc, pool, chain.link, mv, rs, rt, half, S["stats"], 3 * i + 3, S["rstd"], S["pool_passed"])
            chain.end()
            pool.wait_ge(S["cleared"], 16 * QUEUE_TILES)
            send_rows(nc, pool, z, b, d, S, i, tab)

        pairs(pool, sequence)

    @block.scalar
    def _(act):
        A = nc.scalar
        act.wait_ge(S["weights"], LOADED)
        act.wait_ge(S["consts"], 1)

        def sequence(i, p):
            for c in range(CT):
                n = J.bank(("hT", c))
                act.wait_ge(full[n], J.turn(i, ("hT", c)))
                A.activation(hT[:, c, BUCKET:], bank[n][:], ACT.Identity, bias=b1[:, c:c + 1],
                             scale=g1[:, c:c + 1]).then_inc(free[n], 1)
            high_parts(nc, act, parts, bqk, J, bank, full, S, i)
            n = J.bank("mT")
            act.wait_ge(full[n], J.turn(i, "mT"))
            A.activation(mT[:, :], bank[n][0:NH, :], ACT.Copy).then_inc(free[n], 1)
            for g in range(NG):
                for kt in range(NKT):
                    q0, q1, _ = queries_of(kt)
                    nk, nq = min(P, KPAD - kt * P), q1 - q0
                    act.wait_ge(S["pv_done"], NKT * (NG * i + g) + kt + 1)
                    for e in range(2):
                        n = J.bank(("st", g, kt, e))
                        act.wait_ge(full[n], J.turn(i, ("st", g, kt, e)))
                        A.activation(pr[0:nk, kt % 2, 2 * e:2 * e + 2, 0:nq],
                                     bank[n][0:nk, 0:2 * nq].rearrange("p (h q) -> p h q", h=2),
                                     ACT.Exp).then_inc(free[n], 1)
                copy_output(nc, act, g, oT, J, bank, full, free, S, i)
            for c in range(CT):
                n = J.bank(("h2T", c))
                act.wait_ge(full[n], J.turn(i, ("h2T", c)))
                A.activation(hT2[:, c, :], bank[n][:], ACT.Identity, bias=b2[:, c:c + 1],
                             scale=g2[:, c:c + 1]).then_inc(free[n], 1)
            for m in range(FT):
                n = J.bank(("f1", m))
                act.wait_ge(full[n], J.turn(i, ("f1", m)))
                A.activation(G[:, m, :], bank[n][:], ACT.Gelu, bias=bf1[:, m:m + 1]).then_inc(free[n], 1)
            for c in range(CT):
                n = J.bank(("zT", c))
                act.wait_ge(full[n], J.turn(i, ("zT", c)))
                A.activation(hT2[:, c, :], bank[n][:], ACT.Copy).then_inc(free[n], 1)
            act.wait_ge(S["gap_ready"], i + 1)
            A.activation(b["e2"][:], b["gap"][:], ACT.Exp).then_inc(S["gap_exp"], 1)

        pairs(act, sequence)

    @block.vector
    def _(dve):
        V = nc.vector
        chain = Chain(S["dve_own"], dve, 3 + ROUTER_LINKS, S["dve_passed"])
        V.memset(zero[:], 0.0).then_inc(S["zeroed"], 1)
        V.memset(QS[:].bitcast(F32), 0.0)
        V.memset(KS[:].bitcast(F32), 0.0)
        V.memset(hT[:, :, 0:BUCKET], 0.0)
        V.memset(b["carry"][:], 0.0)
        V.memset(w["ones"][:], 1.0)
        V.memset(VP[:], 0.0)
        V.memset(wo[:], 0.0).then_inc(S["zeroed"], 1)
        dve.wait_ge(S["zeroed"], 2)
        V.memset(VP[:, :, :, HD:HD + 1], 1.0)
        dve.wait_ge(S["weights"], LOADED)
        V.tensor_copy(identb[:], ident[:])
        V.tensor_copy(mask_q[:], masks[:, 0, :])
        V.tensor_copy(mask_k[:], masks[:, 1, :])
        V.tensor_copy(w["tri"][:], trif[:])
        V.tensor_scalar(wqkv[:, :, 0:C], wqkv[:, :, 0:C], HD ** -0.5, None, ALU.mult)
        V.tensor_scalar(bqk[:, 0:CT], bqk[:, 0:CT], HD ** -0.5, None, ALU.mult).then_inc(S["consts"], 1)
        dve.wait_ge(S["consts"], 1)

        def sequence(i, j, p):
            chain.start(i)
            dve.wait_ge(x_in[p], 16 * j + 16)
            statistics(nc, chain, x[p], st, mv, S["stats"])
            dve.wait_ge(S["rstd"], 3 * i + 1)
            normalize(nc, x[p], t0, mv, rs[:, 0, :])
            normalize(nc, x[p], hh, mv, rs[:, 1, :]).then_inc(S["hh_ready"], 1)
            low_parts(nc, dve, parts, bqk, J, bank, free, S, i)
            for t in range(NKT):
                n, lo, hi = J.bank(("v", t)), (BUCKET if t == 0 else 0), min(P, KPAD - t * P)
                dve.wait_ge(full[n], J.turn(i, ("v", t)))
                V.tensor_tensor(VP[lo:hi, t, :, 0:HD], bank[n][lo:hi, 0:C].rearrange("p (h d) -> p h d", d=HD),
                                bv[lo:hi, :].rearrange("p (h d) -> p h d", d=HD), ALU.add).then_inc(free[n], 1)
            for t in range(TT):
                for hp in range(NPAIR):
                    n = J.bank(("s", t, hp))
                    dve.wait_ge(full[n], J.turn(i, ("s", t, hp)))
                    V.tensor_reduce(nm[:, t, 2 * hp:2 * hp + 2],
                                    bank[n][:, 0:2 * QW].rearrange("p (h k) -> p h k", h=2), AX.X, ALU.max,
                                    negate=True).then_inc(free[n], 1)
            for g in range(NG):
                invert_sums(nc, dve, g, rD, J, bank, full, free, S, i)
            dve.wait_ge(S["t0b"], i + 1)
            dve.wait_ge(S["x1_out"], 16 * i + 16)
            for t in range(TT):
                n = J.bank(("y", t))
                dve.wait_ge(full[n], J.turn(i, ("y", t)))
                V.tensor_tensor(y[:, t, :], bank[n][:, 0:C], t0[:, t, :], ALU.add).then_inc(free[n], 1)
            for t in range(TT):
                dve.wait_ge(free[J.bank(("y", t))], J.drained(i, ("y", t)))
            statistics(nc, chain, y, st, mv, S["stats"])
            dve.wait_ge(S["rstd"], 3 * i + 2)
            normalize(nc, y, hh, mv, rs[:, 0, :]).then_inc(S["hh_ready"], 1)
            dve.wait_ge(S["res_ready"], i + 1)
            for t in range(TT):
                n = J.bank(("f2", t))
                dve.wait_ge(full[n], J.turn(i, ("f2", t)))
                V.tensor_tensor(y[:, t, :], bank[n][:, 0:C], x[p][:, t, :], ALU.add).then_inc(free[n], 1)
            for t in range(TT):
                dve.wait_ge(free[J.bank(("f2", t))], J.drained(i, ("f2", t)))
            statistics(nc, chain, y, st, mv, S["stats"])
            dve.wait_ge(S["rstd"], 3 * i + 3)
            normalize(nc, y, z, mv, rs[:, 0, :]).then_inc(S["z_ready"], 1)
            router(nc, dve, chain.link, b, w, J, bank, full, free, S, i, tab)
            chain.end()

        with dve.Fori(0, NB // 2) as j:
            for p in range(2):
                sequence(2 * j + p, j, p)

    @block.tensor
    def _(pe):
        M = nc.tensor
        open_banks(pe, free)
        pe.sem_inc(S["pv_done"], 2)
        pe.wait_ge(S["weights"], LOADED)
        pe.wait_ge(S["out_weights"], 16 * HG)
        pe.wait_ge(S["consts"], 1)

        def sequence(i, p):
            pe.wait_ge(S["hh_ready"], 2 * i + 1)
            for c in range(CT):
                n = J.bank(("hT", c))
                pe.wait_ge(free[n], J.turn(i, ("hT", c)))
                transposes(nc, bank[n], hh, c, ident).then_inc(full[n], 1)
            for c in range(CT):
                pe.wait_ge(free[J.bank(("hT", c))], J.drained(i, ("hT", c)))
            for m in range(4):
                project(nc, pe, hT, BUCKET, wqkv, m, J, bank, full, free, i)
            for t in range(NKT):
                values(nc, pe, hT, wqkv[:, :, 2 * C:], t, P * t, min(P, KPAD - t * P), J, bank, full, free, i)
            pe.wait_ge(S["stacked"], 16 * STACK_DMAS * (i + 1))
            for t in range(TT):
                for hp in range(NPAIR):
                    n = J.bank(("s", t, hp))
                    pe.wait_ge(free[n], J.turn(i, ("s", t, hp)))
                    M.matmul(bank[n][:, 0:2 * QW].rearrange("p (h k) -> p h k", h=2), identb[:],
                             mask_q[:].unsqueeze(1).broadcast_to([P, 2, QW]), start=True, stop=False)
                    for e in range(2):
                        ins = M.matmul(bank[n][:, e * QW:(e + 1) * QW], QS[0:STACK, 2 * hp + e, t * P:(t + 1) * P],
                                       KS[0:STACK, hp, t * P:t * P + QW], start=False, stop=e == 1)
                    ins.then_inc(full[n], 1)
            for hp in (NPAIR - 2, NPAIR - 1):
                pe.wait_ge(free[J.bank(("s", TT - 1, hp))], J.drained(i, ("s", TT - 1, hp)))
            n = J.bank("mT")
            pe.wait_ge(free[n], J.turn(i, "mT"))
            for t in range(TT):
                ins = M.transpose(bank[n][0:NH, t * P:(t + 1) * P], nm[:, t, :], ident[:])
            ins.then_inc(full[n], 1)
            pe.wait_ge(S["m_in"], 16 * (i + 1))
            for g in range(NG):
                no = J.bank(("o", g))
                for kt in range(NKT):
                    q0, q1, m0 = queries_of(kt)
                    nk, nq = min(P, KPAD - kt * P), q1 - q0
                    for e in range(2):
                        n, hp = J.bank(("st", g, kt, e)), 2 * g + e
                        pe.wait_ge(free[n], J.turn(i, ("st", g, kt, e)))
                        apart(pe, S["pe_passed"])
                        to = bank[n][0:nk, 0:2 * nq].rearrange("p (h q) -> p h q", h=2)
                        M.matmul(to, identb[0:nk, 0:nk], mask_k[0:nk, m0:m0 + nq].unsqueeze(1).broadcast_to([nk, 2, nq]),
                                 start=True, stop=False)
                        M.matmul(to, KS[0:STACK + 1, hp, kt * P:kt * P + nk], QS[0:STACK + 1, 2 * hp:2 * hp + 2, q0:q1],
                                 start=False, stop=True).then_inc(full[n], 1)
                    if kt == 0:
                        pe.wait_ge(free[no], J.turn(i, ("o", g)))
                    for e in range(2):
                        n = J.bank(("st", g, kt, e))
                        pe.wait_ge(free[n], J.drained(i, ("st", g, kt, e)))
                    apart(pe, S["pe_passed"])
                    for s in range(HG):
                        ins = M.matmul(bank[no][32 * s:32 * s + 32, q0:q1], VP[0:nk, kt, HG * g + s, :],
                                       pr[0:nk, kt % 2, s, 0:nq], start=kt == 0, stop=kt == NKT - 1,
                                       skip_group_check=True)
                    ins.then_inc(S["pv_done"], 1)
                pe.wait_ge(S["pv_done"], NKT * (NG * i + g + 1) + 2)
                pe.sem_inc(full[no], 1)
                spread_sums(nc, pe, g, slotsum, oT, J, bank, full, free, i)
            output_tiles(nc, pe, oN, wo, J, bank, full, free, S, i)
            pe.wait_ge(S["hh_ready"], 2 * i + 2)
            for c in range(CT):
                n = J.bank(("h2T", c))
                pe.wait_ge(free[n], J.turn(i, ("h2T", c)))
                transposes(nc, bank[n], hh, c, ident).then_inc(full[n], 1)
            for c in range(CT):
                pe.wait_ge(free[J.bank(("h2T", c))], J.drained(i, ("h2T", c)))
            for m in range(FT):
                n = J.bank(("f1", m))
                pe.wait_ge(free[n], J.turn(i, ("f1", m)))
                for c in range(CT):
                    ins = M.matmul(bank[n][:], w1[:, c, m * P:(m + 1) * P], hT2[:, c, :], start=c == 0, stop=c == CT - 1)
                ins.then_inc(full[n], 1)
            for m in range(FT - 4, FT):
                pe.wait_ge(free[J.bank(("f1", m))], J.drained(i, ("f1", m)))
            for t in range(TT):
                n = J.bank(("f2", t))
                pe.wait_ge(free[n], J.turn(i, ("f2", t)))
                for m in range(FT):
                    ins = M.matmul(bank[n][:, 0:C], G[:, m, t * P:(t + 1) * P], w2[:, m, :], start=m == 0, stop=m == FT - 1)
                ins.then_inc(full[n], 1)
            pe.wait_ge(S["z_ready"], i + 1)
            for c in range(CT):
                n = J.bank(("zT", c))
                pe.wait_ge(free[n], J.turn(i, ("zT", c)))
                transposes(nc, bank[n], z, c, ident).then_inc(full[n], 1)
            logits(nc, pe, hT2, wr, J, bank, full, free, i)
            count_picks(nc, pe, b, w, J, bank, full, free, S, i)

        pairs(pe, sequence)


def phase_experts(nc, ctx, used, a, d, prefix):
    per_seq = CAP // T
    jobs = [(("xT", c), c) for c in range(CT)]
    jobs += [(("h", m), 2 + m) for m in range(EI // P)]
    jobs += [(("o", t), 6 + t % 2) for t in range(TT)]
    J = Turns(jobs)
    def sb(name, shape, dt=F32):
        return ctx.enter_context(nc.sbuf_tensor(prefix + name, shape, dt))

    bank, full, free = banks(nc, ctx, used, prefix)
    ident = sb("ident", [P, P])
    x = [sb(f"x{p}", [P, TT, C]) for p in range(2)]
    w1 = [sb(f"w1{p}", [P, CT, EI]) for p in range(2)]
    w2 = [sb(f"w2{p}", [P, EI // P, C]) for p in range(2)]
    xT, h = sb("xT", [P, CT, T]), sb("h", [P, EI // P, T])
    y = [sb(f"y{p}", [P, TT, C]) for p in range(2)]
    S = sems(nc, used, prefix, "ident x_in0 x_in1 w_in0 w_in1 y_out0 y_out1 sp_passed")
    x_in, w_in, y_out = ([S[n + str(p)] for p in range(2)] for n in ("x_in", "w_in", "y_out"))
    block = ctx.enter_context(nc.Block())

    def chunks(engine, chunk):
        with engine.Fori(0, NE // 2) as j:
            for q in range(2 * per_seq):
                chunk(2 * per_seq * j + q, j, q)

    def weights_of(engine, e, at):
        engine.dma_start(w1[at][:], a["first"][bass.ds(e * C, C), :].rearrange("(c p) i -> p c i", p=P)).then_inc(w_in[at], 16)
        engine.dma_start(w2[at][:], a["second"][bass.ds(e * EI, EI), :].rearrange("(m p) n -> p m n", p=P)).then_inc(w_in[at], 16)

    @block.sync
    def _(sp):
        sp.dma_start(ident[:], a["c_ident"]).then_inc(S["ident"], 16)

        def chunk(n, j, q):
            if q % per_seq == 0:
                if q == 0:
                    sp.wait_ge(free[J.bank(("xT", 0))], J.turn(n, ("xT", 0)))
                    apart(sp, S["sp_passed"])
                weights_of(sp, 2 * j + q // per_seq, q // per_seq)
            sp.dma_start(x[q % 2][:], rows(d["queue"], n)).then_inc(x_in[q % 2], 16)
            sp.wait_ge(free[J.bank(("xT", 1))], J.turn(n, ("xT", 1)))
            apart(sp, S["sp_passed"])

        chunks(sp, chunk)

    @block.scalar
    def _(act):
        for p in range(2):
            act.sem_inc(y_out[p], 16)

        def chunk(n, j, q):
            for c in range(CT):
                k = J.bank(("xT", c))
                act.wait_ge(full[k], J.turn(n, ("xT", c)))
                nc.scalar.activation(xT[:, c, :], bank[k][:], ACT.Copy).then_inc(free[k], 1)
            for m in (0, 2):
                k = J.bank(("h", m))
                act.wait_ge(full[k], J.turn(n, ("h", m)))
                nc.scalar.activation(h[:, m, :], bank[k][:], ACT.Relu).then_inc(free[k], 1)
            for t in range(TT):
                act.wait_ge(free[J.bank(("o", t))], J.drained(n, ("o", t)))
            act.dma_start(rows(d["done"], n), y[q % 2][:]).then_inc(y_out[q % 2], 16)

        chunks(act, chunk)
        for p in range(2):
            act.wait_ge(y_out[p], 16 * (NE * per_seq // 2) + 16)

    @block.vector
    def _(dve):
        def chunk(n, j, q):
            for m in (1, 3):
                k = J.bank(("h", m))
                dve.wait_ge(full[k], J.turn(n, ("h", m)))
                nc.vector.tensor_scalar(h[:, m, :], bank[k][:], 0.0, None, ALU.max).then_inc(free[k], 1)
            dve.wait_ge(y_out[q % 2], 16 * (per_seq * j + q // 2) + 16)
            for t in range(TT):
                k = J.bank(("o", t))
                dve.wait_ge(full[k], J.turn(n, ("o", t)))
                nc.vector.tensor_copy(y[q % 2][:, t, :], bank[k][:, 0:C]).then_inc(free[k], 1)

        chunks(dve, chunk)

    @block.tensor
    def _(pe):
        open_banks(pe, free)
        pe.wait_ge(S["ident"], 16)

        def chunk(n, j, q):
            pe.wait_ge(x_in[q % 2], 16 * (per_seq * j + q // 2) + 16)
            for c in range(CT):
                k = J.bank(("xT", c))
                pe.wait_ge(free[k], J.turn(n, ("xT", c)))
                transposes(nc, bank[k], x[q % 2], c, ident).then_inc(full[k], 1)
            at = q // per_seq
            if q % per_seq == 0:
                pe.wait_ge(w_in[at], 32 * j + 32)
            for c in range(CT):
                pe.wait_ge(free[J.bank(("xT", c))], J.drained(n, ("xT", c)))
            for m in range(EI // P):
                k = J.bank(("h", m))
                pe.wait_ge(free[k], J.turn(n, ("h", m)))
                for c in range(CT):
                    ins = nc.tensor.matmul(bank[k][:], w1[at][:, c, m * P:(m + 1) * P], xT[:, c, :], start=c == 0, stop=c == CT - 1)
                ins.then_inc(full[k], 1)
            for m in range(EI // P):
                pe.wait_ge(free[J.bank(("h", m))], J.drained(n, ("h", m)))
            for t in range(TT):
                k = J.bank(("o", t))
                pe.wait_ge(free[k], J.turn(n, ("o", t)))
                for m in range(EI // P):
                    ins = nc.tensor.matmul(bank[k][:, 0:C], h[:, m, t * P:(t + 1) * P], w2[at][:, m, :], start=m == 0, stop=m == EI // P - 1)
                ins.then_inc(full[k], 1)

        chunks(pe, chunk)


def fetch_rows(nc, pool, got, idx, d, S, tab, i, p, link):
    link(nc.gpsimd.tensor_copy(idx[p][:], tab["idx"][:, bass.ds(i * TOPK * TT, TOPK * TT)]))
    apart(pool, S["pool_passed"])
    for n in range(TOPK * TT):
        pool.indirect_dma_start(got[p][:, n, :], None, d["done"], bass.IndirectOffsetOnAxis(ap=idx[p][:, n:n + 1], axis=0),
                                bounds_check=NE * CAP - 1, oob_is_err=False).then_inc(S[f"got{p}"], 16)


def combine(nc, link, x, got, wt, tab, i):
    link(nc.vector.tensor_copy(wt[:], tab["w"][:, bass.ds(i * TOPK * TT, TOPK * TT)]))
    for k in range(TOPK):
        for t in range(TT):
            n = k * TT + t
            ins = nc.vector.scalar_tensor_tensor(x[:, t, :], got[:, n, :], wt[:, n:n + 1], x[:, t, :], ALU.mult, ALU.add)
        if k == 0:
            link(ins)
    return ins


def phase_alibi(nc, ctx, used, a, d, tab):
    ROWS = STACK + 6
    jobs = [(("tT", c), c) for c in range(CT)]
    jobs += [(("qk", m), (2, 3, 0, 1)[m]) for m in range(4)]
    jobs += [(("v", t), 2 + t % 2) for t in range(TT)]
    jobs += [(("s", h, t), 4 + t) for h in range(NH) for t in range(TT)]
    jobs += [("mT", 0)]
    for g in range(NG):
        jobs += [(("st", g, kt, s), s) for kt in range(TT) for s in range(HG)]
        jobs += [(("o", g), 6 + g % 2), (("d", g), 4 + g % 2)]
    jobs += [(("y", t), t) for t in range(TT)]
    jobs += [(("zT", c), 6 + c) for c in range(CT)]
    jobs += [("logit", 0), ("cum", 1)]
    J = Turns(jobs)

    def sb(name, shape, dt=F32):
        return ctx.enter_context(nc.sbuf_tensor("b_" + name, shape, dt))

    bank, full, free = banks(nc, ctx, used, "b")
    ident, slotsum, trif = sb("ident", [P, P]), sb("slotsum", [P, P]), sb("trif", [P, P])
    w = {"tri": sb("tri", [P, P], BF16), "ones": sb("ones", [P, P], BF16),
         "rev": sb("rev", [P, TT, NE]), "base": sb("base", [P, TT, NE])}
    wqk, bqk, wv = sb("wqk", [P, CT, 2 * C]), sb("bqk", [P, 4]), sb("wv", [P, CT, C])
    bv, bo, wo = sb("bv", [P, C]), sb("bo", [P, C]), sb("wo", [P, NG, C])
    wr, half = sb("wr", [P, CT, NE]), sb("half", [P, TT])
    x = [sb(f"x{p}", [P, TT, C]) for p in range(2)]
    got = [sb(f"got{p}", [P, TOPK * TT, C]) for p in range(2)]
    idx = [sb(f"idx{p}", [P, TOPK * TT], U32) for p in range(2)]
    wt = sb("wt", [P, TOPK * TT])
    t0, z = sb("t0", [P, TT, C]), sb("z", [P, TT, C])
    st, mv = sb("st", [P, TT, 6]), sb("mv", [P, TT, 2])
    rs, rt = sb("rs", [P, 2, TT]), sb("rt", [P, 3, TT])
    tT = sb("tT", [P, CT, T])
    parts = {n: sb(n, [P, CT, T], F32R) for n in ("q_hi", "q_lo", "k_hi", "k_lo")}
    QS, KS = sb("QS", [P, NH, T], F32R), sb("KS", [P, NPAIR, T], F32R)
    VP = sb("VP", [P, TT, NH, 2 * HD])
    nm, mT = sb("nm", [P, TT, NH]), sb("mT", [NH, T], F32R)
    pr = sb("pr", [P, 2, HG, T])
    oT, rD, oN = sb("oT", [P, 2, T]), sb("rD", [P, T]), sb("oN", [P, NG, T])
    b = route_tiles(sb)
    S = sems(nc, used, "b", """weights out_weights zeroed consts casts x_in0 x_in1 first got0 got1 stats rstd t0_ready hi_ready
        stacked m_in pv_done on_ready xb_ready x3_out0 x3_out1 z_ready gap_ready gap_exp picks_ready
        idx_ready sent dve_own pool_own dve_passed pool_passed pe_passed sp_passed""")
    x_in, out = [S["x_in0"], S["x_in1"]], [S["x3_out0"], S["x3_out1"]]

    def mat(m):
        return m.rearrange("(c p) n -> p c n", p=P)

    loads = [
        (ident[:], a["c_ident"]), (slotsum[:], a["c_slotsum"]), (trif[:], a["c_tri"]),
        (w["rev"][:], a["c_rev"]), (w["base"][:], a["c_base"]),
        (wqk[:, :, 0:C], mat(a["wq"])), (wqk[:, :, C:2 * C], mat(a["wk"])), (wv[:], mat(a["wv"])),
        (bqk[:, 0:CT], a["bq"]), (bqk[:, CT:2 * CT], a["bk"]),
        (bv[:], a["bv"].partition_broadcast(P)), (bo[:], a["bo"].partition_broadcast(P)),
        (wr[:], a["router"].rearrange("(c p) e -> p c e", p=P)),
    ]
    LOADED = 16 * len(loads)
    block = ctx.enter_context(nc.Block())

    @block.sync
    def _(sp):
        load_all(sp, S["weights"], loads)
        sp.dma_start(x[0][:], rows(d["x1"], 0)).then_inc(x_in[0], 16)
        sp.dma_start(x[1][:], rows(d["x1"], 1)).then_inc(x_in[1], 16)
        sp.wait_ge(S["zeroed"], 1)
        load_all(sp, S["out_weights"], [(wo[32 * s:32 * s + HD, :, :], slots_of(a["wo"])[s]) for s in range(HG)])
        sp.wait_ge(S["casts"], 32)

        def sequence(i, j, p, last):
            for m in range(4):
                sp.wait_ge(free[J.bank(("qk", m))], J.drained(i, ("qk", m)))
                apart(sp, S["sp_passed"])
            sp.wait_ge(S["pv_done"], NG * TT * i + 2)
            apart(sp, S["sp_passed"])
            stack(sp, S["stacked"], QS, KS, 0, parts)
            sp.wait_ge(free[J.bank("mT")], J.drained(i, "mT"))
            apart(sp, S["sp_passed"])
            sp.dma_start(QS[ROWS:ROWS + 1, :, :].bitcast(F32), mT[:, :].bitcast(F32)).then_inc(S["m_in"], 16)
            for t in range(TT):
                sp.wait_ge(free[J.bank(("y", t))], J.drained(i, ("y", t)))
                apart(sp, S["sp_passed"])
            sp.dma_start(rows(d["x3"], i), x[p][:]).then_inc(out[p], 16)
            if not last:
                sp.wait_ge(S["z_ready"], i + 1)
                apart(sp, S["sp_passed"])
                sp.wait_ge(out[p], 16 * j + 16)
                apart(sp, S["sp_passed"])
                sp.dma_start(x[p][:], rows(d["x1"], i + 2)).then_inc(x_in[p], 16)

        with sp.Fori(0, NB // 2 - 1) as j:
            for p in range(2):
                sequence(2 * j + p, j, p, False)
        for p in range(2):
            sequence(NB - 2 + p, NB // 2 - 1, p, True)
        for p in range(2):
            sp.wait_ge(out[p], 16 * (NB // 2))

    @block.gpsimd
    def _(pool):
        V = nc.gpsimd
        V.memset(half[:], -0.5)
        pool.wait_ge(S["zeroed"], 1)
        pool.dma_start(KS[STACK:ROWS + 1, :, :], a["c_alibi_k"]).then_inc(S["casts"], 16)
        pool.dma_start(QS[STACK:ROWS, :, :], a["c_alibi_q"]).then_inc(S["casts"], 16)
        pool.sem_inc(S["on_ready"], 2)
        chain = Chain(S["pool_own"], pool, 3, S["pool_passed"])
        first = S["first"]
        fetch_rows(nc, pool, got, idx, d, S, tab, 0, 0, lambda ins: (ins.then_inc(first, 1), pool.wait_ge(first, 1)))
        pool.wait_ge(S["weights"], LOADED)

        def sequence(i, p, last):
            chain.start(i)
            if not last:
                fetch_rows(nc, pool, got, idx, d, S, tab, i + 1, 1 - p, chain.link)
            root(nc, pool, chain.link, mv, rs, rt, half, S["stats"], 2 * i + 1, S["rstd"], S["pool_passed"])
            for t in range(TT):
                if t == 0:
                    pool.wait_ge(S["t0_ready"], i + 1)
                ins = V.tensor_tensor(x[p][:, t, :], x[p][:, t, :], bo[:], ALU.add)
            ins.then_inc(S["xb_ready"], 1)
            normalize_outputs(nc, pool, oT, rD, oN, J, free, S, i)
            root(nc, pool, chain.link, mv, rs, rt, half, S["stats"], 2 * i + 2, S["rstd"], S["pool_passed"])
            send_rows(nc, pool, z, b, d, S, i, tab)

        all_but_last(pool, sequence)

    @block.scalar
    def _(act):
        A = nc.scalar
        act.wait_ge(S["weights"], LOADED)
        act.wait_ge(S["consts"], 1)

        def sequence(i, p):
            for c in range(CT):
                n = J.bank(("tT", c))
                act.wait_ge(full[n], J.turn(i, ("tT", c)))
                A.activation(tT[:, c, :], bank[n][:], ACT.Copy).then_inc(free[n], 1)
            high_parts(nc, act, parts, bqk, J, bank, full, S, i)
            n = J.bank("mT")
            act.wait_ge(full[n], J.turn(i, "mT"))
            A.activation(mT[:, :], bank[n][0:NH, :], ACT.Copy).then_inc(free[n], 1)
            for g in range(NG):
                for kt in range(TT):
                    act.wait_ge(S["pv_done"], TT * (NG * i + g) + kt + 1)
                    for s in range(HG):
                        n = J.bank(("st", g, kt, s))
                        act.wait_ge(full[n], J.turn(i, ("st", g, kt, s)))
                        A.activation(pr[:, kt % 2, s, :], bank[n][:], ACT.Exp).then_inc(free[n], 1)
                copy_output(nc, act, g, oT, J, bank, full, free, S, i)
            for c in range(CT):
                n = J.bank(("zT", c))
                act.wait_ge(full[n], J.turn(i, ("zT", c)))
                A.activation(tT[:, c, :], bank[n][:], ACT.Copy).then_inc(free[n], 1)
            act.wait_ge(S["gap_ready"], i + 1)
            A.activation(b["e2"][:], b["gap"][:], ACT.Exp).then_inc(S["gap_exp"], 1)

        pairs(act, sequence)

    @block.vector
    def _(dve):
        V = nc.vector
        chain = Chain(S["dve_own"], dve, 5 + ROUTER_LINKS, S["dve_passed"])
        V.memset(QS[:].bitcast(F32), 0.0)
        V.memset(KS[:].bitcast(F32), 0.0)
        for p in range(2):
            V.memset(got[p][:], 0.0)
        V.memset(b["carry"][:], 0.0)
        V.memset(w["ones"][:], 1.0)
        V.memset(VP[:], 0.0)
        V.memset(wo[:], 0.0).then_inc(S["zeroed"], 1)
        dve.wait_ge(S["zeroed"], 1)
        V.memset(VP[:, :, :, HD:HD + 1], 1.0)
        dve.wait_ge(S["weights"], LOADED)
        V.tensor_copy(w["tri"][:], trif[:])
        V.tensor_scalar(wqk[:, :, 0:C], wqk[:, :, 0:C], HD ** -0.5, None, ALU.mult)
        V.tensor_scalar(bqk[:, 0:CT], bqk[:, 0:CT], HD ** -0.5, None, ALU.mult).then_inc(S["consts"], 1)
        dve.wait_ge(S["consts"], 1)

        def sequence(i, j, p):
            chain.start(i)
            dve.wait_ge(x_in[p], 16 * j + 16)
            dve.wait_ge(S[f"got{p}"], 16 * TOPK * TT * (j + 1))
            chain.link(combine(nc, chain.link, x[p], got[p], wt, tab, i))
            statistics(nc, chain, x[p], st, mv, S["stats"])
            dve.wait_ge(S["rstd"], 2 * i + 1)
            normalize(nc, x[p], t0, mv, rs[:, 0, :]).then_inc(S["t0_ready"], 1)
            low_parts(nc, dve, parts, bqk, J, bank, free, S, i)
            for t in range(TT):
                n = J.bank(("v", t))
                dve.wait_ge(full[n], J.turn(i, ("v", t)))
                V.tensor_tensor(VP[:, t, :, 0:HD], bank[n][:, 0:C].rearrange("p (h d) -> p h d", d=HD),
                                bv[:].rearrange("p (h d) -> p h d", d=HD), ALU.add).then_inc(free[n], 1)
            for h in range(NH):
                for t in range(TT):
                    n = J.bank(("s", h, t))
                    dve.wait_ge(full[n], J.turn(i, ("s", h, t)))
                    V.tensor_reduce(nm[:, t, h:h + 1], bank[n][:], AX.X, ALU.max, negate=True).then_inc(free[n], 1)
            for g in range(NG):
                invert_sums(nc, dve, g, rD, J, bank, full, free, S, i)
            dve.wait_ge(S["xb_ready"], i + 1)
            for t in range(TT):
                n = J.bank(("y", t))
                dve.wait_ge(full[n], J.turn(i, ("y", t)))
                V.tensor_tensor(x[p][:, t, :], bank[n][:, 0:C], x[p][:, t, :], ALU.add).then_inc(free[n], 1)
            for t in range(TT):
                dve.wait_ge(free[J.bank(("y", t))], J.drained(i, ("y", t)))
            statistics(nc, chain, x[p], st, mv, S["stats"])
            dve.wait_ge(S["rstd"], 2 * i + 2)
            normalize(nc, x[p], z, mv, rs[:, 0, :]).then_inc(S["z_ready"], 1)
            router(nc, dve, chain.link, b, w, J, bank, full, free, S, i, tab)
            chain.end()

        with dve.Fori(0, NB // 2) as j:
            for p in range(2):
                sequence(2 * j + p, j, p)

    @block.tensor
    def _(pe):
        M = nc.tensor
        open_banks(pe, free)
        pe.sem_inc(S["pv_done"], 2)
        pe.wait_ge(S["weights"], LOADED)
        pe.wait_ge(S["out_weights"], 16 * HG)
        pe.wait_ge(S["consts"], 1)

        def sequence(i, p):
            pe.wait_ge(S["t0_ready"], i + 1)
            for c in range(CT):
                n = J.bank(("tT", c))
                pe.wait_ge(free[n], J.turn(i, ("tT", c)))
                transposes(nc, bank[n], t0, c, ident).then_inc(full[n], 1)
            for c in range(CT):
                pe.wait_ge(free[J.bank(("tT", c))], J.drained(i, ("tT", c)))
            for m in range(4):
                project(nc, pe, tT, 0, wqk, m, J, bank, full, free, i)
            for t in range(TT):
                values(nc, pe, tT, wv, t, P * t, P, J, bank, full, free, i)
            pe.wait_ge(S["stacked"], 16 * STACK_DMAS * (i + 1))
            for h in range(NH):
                for t in range(TT):
                    n = J.bank(("s", h, t))
                    pe.wait_ge(free[n], J.turn(i, ("s", h, t)))
                    M.matmul(bank[n][:], QS[0:ROWS, h, t * P:(t + 1) * P], KS[0:ROWS, h // 2, :],
                             start=True, stop=True).then_inc(full[n], 1)
            for t in range(TT):
                pe.wait_ge(free[J.bank(("s", NH - 1, t))], J.drained(i, ("s", NH - 1, t)))
            n = J.bank("mT")
            pe.wait_ge(free[n], J.turn(i, "mT"))
            for t in range(TT):
                ins = M.transpose(bank[n][0:NH, t * P:(t + 1) * P], nm[:, t, :], ident[:])
            ins.then_inc(full[n], 1)
            pe.wait_ge(S["m_in"], 16 * (i + 1))

            def scores(g, kt):
                for s in range(HG):
                    n, h = J.bank(("st", g, kt, s)), HG * g + s
                    pe.wait_ge(free[n], J.turn(i, ("st", g, kt, s)))
                    M.matmul(bank[n][:], KS[0:ROWS + 1, h // 2, kt * P:(kt + 1) * P], QS[0:ROWS + 1, h, :],
                             start=True, stop=True).then_inc(full[n], 1)

            for g in range(NG):
                no = J.bank(("o", g))
                for kt in range(TT):
                    scores(g, kt)
                    if kt == 0:
                        pe.wait_ge(free[no], J.turn(i, ("o", g)))
                    for s in range(HG):
                        pe.wait_ge(free[J.bank(("st", g, kt, s))], J.drained(i, ("st", g, kt, s)))
                    for s in range(HG):
                        ins = M.matmul(bank[no][32 * s:32 * s + 32, :], VP[:, kt, HG * g + s, :], pr[:, kt % 2, s, :],
                                       start=kt == 0, stop=kt == TT - 1)
                    ins.then_inc(S["pv_done"], 1)
                pe.wait_ge(S["pv_done"], TT * (NG * i + g + 1) + 2)
                pe.sem_inc(full[no], 1)
                spread_sums(nc, pe, g, slotsum, oT, J, bank, full, free, i)
            output_tiles(nc, pe, oN, wo, J, bank, full, free, S, i)
            pe.wait_ge(S["z_ready"], i + 1)
            for c in range(CT):
                n = J.bank(("zT", c))
                pe.wait_ge(free[n], J.turn(i, ("zT", c)))
                transposes(nc, bank[n], z, c, ident).then_inc(full[n], 1)
            logits(nc, pe, tT, wr, J, bank, full, free, i)
            count_picks(nc, pe, b, w, J, bank, full, free, S, i)

        pairs(pe, sequence)


def phase_combine(nc, ctx, used, a, d, tab, out):
    def sb(name, shape, dt=F32):
        return ctx.enter_context(nc.sbuf_tensor("c_" + name, shape, dt))

    x = [sb(f"x{p}", [P, TT, C]) for p in range(2)]
    got = [sb(f"got{p}", [P, TOPK * TT, C]) for p in range(2)]
    idx = [sb(f"idx{p}", [P, TOPK * TT], U32) for p in range(2)]
    wt = sb("wt", [P, TOPK * TT])
    S = sems(nc, used, "c", "zeroed x_in0 x_in1 first got0 got1 sum_ready out0 out1 dve_own pool_own dve_passed pool_passed pe_passed sp_passed")
    x_in, left = [S["x_in0"], S["x_in1"]], [S["out0"], S["out1"]]
    block = ctx.enter_context(nc.Block())

    @block.sync
    def _(sp):
        for p in range(2):
            sp.dma_start(x[p][:], rows(d["x3"], p)).then_inc(x_in[p], 16)

        def sequence(i, j, p, last):
            sp.wait_ge(S["sum_ready"], i + 1)
            apart(sp, S["sp_passed"])
            sp.dma_start(rows(out, i), x[p][:]).then_inc(left[p], 16)
            if not last:
                sp.wait_ge(left[p], 16 * j + 16)
                apart(sp, S["sp_passed"])
                sp.dma_start(x[p][:], rows(d["x3"], i + 2)).then_inc(x_in[p], 16)

        with sp.Fori(0, NB // 2 - 1) as j:
            for p in range(2):
                sequence(2 * j + p, j, p, False)
        for p in range(2):
            sequence(NB - 2 + p, NB // 2 - 1, p, True)
        for p in range(2):
            sp.wait_ge(left[p], 16 * (NB // 2))

    @block.gpsimd
    def _(pool):
        pool.wait_ge(S["zeroed"], 1)
        chain = Chain(S["pool_own"], pool, 1, S["pool_passed"])
        first = S["first"]
        fetch_rows(nc, pool, got, idx, d, S, tab, 0, 0, lambda ins: (ins.then_inc(first, 1), pool.wait_ge(first, 1)))

        def sequence(i, p, last):
            chain.start(i)
            if not last:
                if last is not None:
                    pool.wait_ge(S["sum_ready"], i)
                fetch_rows(nc, pool, got, idx, d, S, tab, i + 1, 1 - p, chain.link)

        sequence(0, 0, None)
        sequence(1, 1, False)
        with pool.Fori(1, NB // 2 - 1) as j:
            for p in range(2):
                sequence(2 * j + p, p, False)
        sequence(NB - 2, 0, False)

    @block.vector
    def _(dve):
        for p in range(2):
            ins = nc.vector.memset(got[p][:], 0.0)
        ins.then_inc(S["zeroed"], 1)
        chain = Chain(S["dve_own"], dve, 2, S["dve_passed"])
        dve.wait_ge(S["zeroed"], 1)

        def sequence(i, j, p):
            chain.start(i)
            dve.wait_ge(x_in[p], 16 * j + 16)
            dve.wait_ge(S[f"got{p}"], 16 * TOPK * TT * (j + 1))
            combine(nc, chain.link, x[p], got[p], wt, tab, i).then_inc(S["sum_ready"], 1)
            dve.wait_ge(S["sum_ready"], i + 1)
            chain.end()

        with dve.Fori(0, NB // 2) as j:
            for p in range(2):
                sequence(2 * j + p, j, p)


def program(nc, a, out):
    d = {n: nc.dram_tensor(f"d_{n}", (NB * T, C), F32).ap() for n in ("x1", "x3", "queue", "done")}
    with ExitStack() as ctx:
        tab = {"idx": ctx.enter_context(nc.sbuf_tensor("tab_idx", [P, NB * TOPK * TT], U32)),
               "w": ctx.enter_context(nc.sbuf_tensor("tab_w", [P, NB * TOPK * TT], F32))}
        for phase, *more in ((phase_local, tab), (phase_experts, "e1_"), (phase_alibi, tab), (phase_experts, "e2_"),
                             (phase_combine, tab, out)):
            with ExitStack() as own:
                used = []
                phase(nc, own, used, a, d, *more)
            nc.clear_and_free_semaphores(used)
            nc.all_engine_barrier()


def shape_constants():
    import numpy as np
    f = np.float32
    none = f(-1e30)
    q, k = np.arange(P), np.arange(QW)
    a, i = q[:, None] // BUCKET, q[:, None] % BUCKET
    b, j = k[None, :] // BUCKET, k[None, :] % BUCKET
    mask_q = np.where((b == a) | ((b == a + 1) & (j <= i)), f(0), none)
    kb, kj = a, i
    qb, qi = b, j
    mask_k = np.where((qb == kb + 1) | ((qb == kb) & (kj <= qi)), f(0), none)
    c = {"c_ident": np.eye(P, dtype=f), "c_masks": np.stack([mask_q, mask_k], 1).astype(f)}
    slot = np.zeros((P, P), f)
    for s in range(HG):
        slot[32 * s + HD, 32 * s:32 * s + 32] = 1
    c["c_slotsum"] = slot
    c["c_tri"] = (q[:, None] <= q[None, :]).astype(f)
    e = np.arange(NE)
    c["c_rev"] = np.broadcast_to((NE - e).astype(f), (P, TT, NE)).copy()
    c["c_base"] = np.broadcast_to((CAP * e - 1).astype(f), (P, TT, NE)).copy()
    c["c_one"] = np.ones((1, NPAIR, KPAD), f)

    def cut(v):
        v = v.astype(f)
        hi = ((v.view(np.uint32) + np.uint32(0x800)) & np.uint32(0xFFFFF000)).view(f)
        return hi, v - hi

    slope = (f(1) / np.power(f(2), np.arange(NH, dtype=f) / f(NH))).astype(f)
    pos = np.arange(T, dtype=f)
    KA, QA = np.zeros((7, NPAIR, T), f), np.zeros((6, NH, T), f)
    for h in range(NH):
        hi, lo = cut(slope[h] * pos)
        KA[2 * (h % 2), h // 2], KA[2 * (h % 2) + 1, h // 2] = hi, lo
        QA[2 * (h % 2), h], QA[2 * (h % 2) + 1, h] = 1, 1
        hi, lo = cut(-slope[h] * pos)
        QA[4, h], QA[5, h] = hi, lo
    KA[4:7] = 1
    return c | {"c_alibi_k": KA, "c_alibi_q": QA}


def kernel(L0_attn_a_x, L0_attn_a_ln1_g, L0_attn_a_ln1_b, L0_attn_a_w_qkv, L0_attn_a_b_qkv, L0_attn_a_w_out,
           L0_attn_a_b_out, L0_attn_a_ln2_g, L0_attn_a_ln2_b, L0_attn_a_w1, L0_attn_a_b1, L0_attn_a_w2, L0_attn_a_b2,
           L0_attn_b_Wq, L0_attn_b_bq, L0_attn_b_Wk, L0_attn_b_bk, L0_attn_b_Wv, L0_attn_b_bv, L0_attn_b_Wo,
           L0_attn_b_bo, L0_ffn_expert_embeddings, L0_ffn_first_linear, L0_ffn_second_linear):
    import numpy as np
    import concourse.bacc as bacc
    from concourse.bass_utils import run_bass_kernel_spmd

    def lay(v):
        return np.ascontiguousarray(v)

    def columns(v):
        return lay(np.transpose(np.reshape(v, (-1, P))))

    arrays = {
        "x": lay(np.reshape(L0_attn_a_x, (NB * T, C))), "ln1_g": columns(L0_attn_a_ln1_g), "ln1_b": columns(L0_attn_a_ln1_b),
        "w_qkv": lay(L0_attn_a_w_qkv), "b_qk": columns(L0_attn_a_b_qkv[0:2 * C]), "b_v": lay(L0_attn_a_b_qkv[2 * C:3 * C]), "w_out": lay(L0_attn_a_w_out),
        "b_out": lay(L0_attn_a_b_out), "ln2_g": columns(L0_attn_a_ln2_g), "ln2_b": columns(L0_attn_a_ln2_b),
        "w1": lay(L0_attn_a_w1), "b1": columns(L0_attn_a_b1), "w2": lay(L0_attn_a_w2), "b2": lay(L0_attn_a_b2),
        "wq": lay(L0_attn_b_Wq), "bq": columns(L0_attn_b_bq), "wk": lay(L0_attn_b_Wk), "bk": columns(L0_attn_b_bk),
        "wv": lay(L0_attn_b_Wv), "bv": lay(L0_attn_b_bv), "wo": lay(L0_attn_b_Wo), "bo": lay(L0_attn_b_bo),
        "router": lay(np.transpose(L0_ffn_expert_embeddings)),
        "first": lay(np.reshape(np.transpose(L0_ffn_first_linear, (0, 2, 1)), (NE * C, EI))),
        "second": lay(np.reshape(np.transpose(L0_ffn_second_linear, (0, 2, 1)), (NE * EI, C))),
    }
    arrays |= shape_constants()
    nc = bacc.Bacc("TRN2", target_bir_lowering=False, num_devices=1)
    a = {n: nc.dram_tensor(f"in_{n}", v.shape, mybir.dt.from_np(v.dtype), kind="ExternalInput").ap()
         for n, v in arrays.items()}
    out = nc.dram_tensor("out", (NB * T, C), F32, kind="ExternalOutput").ap()
    program(nc, a, out)
    r = run_bass_kernel_spmd(nc, [{f"in_{n}": v for n, v in arrays.items()}], core_ids=[0])
    return np.reshape(r.results[0]["out"], (NB, T, C))
```

```python
from contextlib import ExitStack

import concourse.bass as bass
from concourse import mybir

F32 = mybir.dt.float32
F32R = mybir.dt.float32r
BF16 = mybir.dt.bfloat16
U32 = mybir.dt.uint32
ACT = mybir.ActivationFunctionType
ALU = mybir.AluOpType
AX = mybir.AxisListType

P = 128
NB, T, C = 32, 512, 256
TT = T // P
CT = C // P
NH, HD = 16, 16
NPAIR = NH // 2
HG = 4
NG = NH // HG
BUCKET = 64
KPAD = BUCKET + T
NE, TOPK, EI = 8, 2, 512
CAP = NB * T // NE
FF = 4 * C
FT = FF // P
EPS = 1e-5
BIG = 65536.0
STACK = 6 * HD


class Turns:

    def __init__(self, jobs):
        self.per, self.of = {}, {}
        for name, bank in jobs:
            k = self.per.get(bank, 0)
            self.of[name] = (bank, k)
            self.per[bank] = k + 1

    def bank(self, job):
        return self.of[job][0]

    def turn(self, i, job):
        bank, k = self.of[job]
        return i * self.per[bank] + k + 1

    def drained(self, i, job):
        return self.turn(i, job) + 1


class Chain:

    def __init__(self, sem, engine, per, passed):
        self.sem, self.engine, self.per, self.passed, self.n, self.i = sem, engine, per, passed, 0, 0

    def start(self, i):
        self.i, self.n = i, 0

    def link(self, ins):
        self.n += 1
        assert self.n <= self.per, "more links than per"
        ins.then_inc(self.sem, 1)
        self.engine.wait_ge(self.sem, self.i * self.per + self.n)

    def end(self):
        assert self.n == self.per, f"links: {self.n}, per: {self.per}"


def apart(engine, passed):
    engine.sem_inc(passed, 1)


def pairs(engine, sequence):
    with engine.Fori(0, NB // 2) as j:
        for p in range(2):
            sequence(2 * j + p, p)


def all_but_last(engine, sequence):
    with engine.Fori(0, NB // 2 - 1) as j:
        for p in range(2):
            sequence(2 * j + p, p, False)
    sequence(NB - 2, 0, False)
    sequence(NB - 1, 1, True)


def rows(ap, i):
    return ap[bass.ds(i * T, T), :].rearrange("(t p) c -> p t c", p=P)


STACK_DMAS = 3 * 2 * 2


def stack(sp, QS, KS, kcol, parts, bounce, S, i):
    sp.wait_ge(S["stacked"], 16 * STACK_DMAS * i + 16)
    apart(sp, S["sp_passed"])
    for n, part in parts.items():
        sp.dma_start(bounce[n[0]][n.endswith("lo") * 1].rearrange("(c p) n -> p c n", p=P), part[:].bitcast(F32)).then_inc(S["bounced"], 16)
    sp.wait_ge(S["bounced"], 16 * len(parts) * (i + 1))
    apart(sp, S["sp_passed"])
    for blk, (q, k) in enumerate((("q_hi", "k_hi"), ("q_hi", "k_lo"), ("q_lo", "k_hi"))):
        for e in range(2):
            to = 3 * HD * e + HD * blk
            by_head = {n: bounce[n[0]][n.endswith("lo") * 1].rearrange("(a e d) n -> e d a n", e=2, d=HD)[e] for n in (q, k)}
            sp.dma_start(QS[to:to + HD, e::2, :].bitcast(F32), by_head[q]).then_inc(S["stacked"], 16)
            sp.dma_start(KS[to:to + HD, :, kcol:kcol + T].bitcast(F32), by_head[k]).then_inc(S["stacked"], 16)


def statistics(nc, chain, src, st, mv, ready):
    for t in range(TT):
        ins = nc.vector.bn_stats(st[:, t, :], src[:, t, :])
    chain.link(ins)
    apart(chain.engine, chain.passed)
    for t in range(TT):
        ins = nc.vector.bn_aggr(mv[:, t, :], st[:, t, :])
    ins.then_inc(ready, 1)


def normalize(nc, src, dst, mv, rs):
    for t in range(TT):
        ins = nc.vector.tensor_scalar(dst[:, t, :], src[:, t, :], mv[:, t, 0:1], rs[:, t:t + 1],
                                      ALU.subtract, ALU.mult)
    return ins


def transposes(nc, dst, src, c, ident):
    for t in range(TT):
        ins = nc.tensor.transpose(dst[:, t * P:(t + 1) * P], src[:, t, c * P:(c + 1) * P], ident[:])
    return ins


def route_tiles(sb):
    b = {n: sb(n, [P, TT, NE]) for n in ("lg", "lg2", "eq", "rank", "slot", "prod")}
    b |= {"o": sb("o", [P, TOPK, TT, NE]), "oh": sb("oh", [P, TT * NE], BF16), "carry": sb("carry", [P, NE])}
    b |= {n: sb(n, [P, TOPK, TT]) for n in ("m", "p", "r", "s", "kept")}
    b |= {n: sb(n, [P, TT]) for n in ("pm", "gap", "e2")}
    b["idx"] = sb("idx", [P, TOPK * TT], U32)
    return b


TOP_LINKS, WEIGHT_LINKS, RANK_LINKS = 11, 5, 2 + 8 + 3
ROUTER_LINKS = TOP_LINKS + WEIGHT_LINKS + RANK_LINKS


def over_experts(ap):
    return ap.unsqueeze(2).broadcast_to([P, TT, NE])


def take_logits(nc, dve, b, J, bank, full, free, n):
    k = J.bank("logit")
    dve.wait_ge(full[k], J.turn(n, "logit"))
    nc.vector.tensor_copy(b["lg"][:], bank[k][:, 0:TT * NE].rearrange("p (t e) -> p t e", e=NE)).then_inc(free[k], 1)
    dve.wait_ge(free[k], J.drained(n, "logit"))


def route_top(nc, link, b, w, k):
    V = nc.vector
    src, eq, o, m, pm = (b["lg2"] if k else b["lg"]), b["eq"], b["o"], b["m"], b["pm"]
    link(V.tensor_reduce(m[:, k, :], src[:], AX.X, ALU.max))
    link(V.tensor_tensor(eq[:], src[:], over_experts(m[:, k, :]), ALU.is_equal))
    link(V.tensor_tensor(eq[:], eq[:], w["rev"][:], ALU.mult))
    link(V.tensor_reduce(pm[:], eq[:], AX.X, ALU.max))
    link(V.tensor_tensor(o[:, k, :, :], eq[:], over_experts(pm[:]), ALU.is_equal))
    if k == 0:
        link(V.scalar_tensor_tensor(b["lg2"][:], o[:, 0, :, :], -3e38, b["lg"][:], ALU.mult, ALU.add))


def route_gap(nc, b, S):
    nc.vector.tensor_tensor(b["gap"][:], b["m"][:, 1, :], b["m"][:, 0, :], ALU.subtract).then_inc(S["gap_ready"], 1)


def route_weights(nc, dve, link, b, S, i):
    V = nc.vector
    p, o, pm = b["p"], b["o"], b["pm"]
    dve.wait_ge(S["gap_exp"], i + 1)
    link(V.tensor_scalar(pm[:], b["e2"][:], 1.0, None, ALU.add))
    link(V.reciprocal(p[:, 0, :], pm[:]))
    link(V.tensor_tensor(p[:, 1, :], p[:, 0, :], b["e2"][:], ALU.mult))
    link(V.tensor_scalar(pm[:], p[:, 1, :], 0.0, None, ALU.is_gt))
    link(V.tensor_tensor(o[:, 1, :, :], o[:, 1, :, :], over_experts(pm[:]), ALU.mult))
    V.tensor_tensor(b["oh"][:].rearrange("p (t e) -> p t e", e=NE), o[:, 0, :, :], o[:, 1, :, :],
                    ALU.add).then_inc(S["picks_ready"], 1)


def route_ranks(nc, dve, link, b, w, J, bank, full, free, n, S, i, tab, part=None):
    V = nc.vector
    o, p, rank, slot, r, s, kept, prod = (b[k] for k in ("o", "p", "rank", "slot", "r", "s", "kept", "prod"))
    cum = J.bank("cum")
    if part in (None, 0):
        dve.wait_ge(full[cum], J.turn(n, "cum"))
        link(V.tensor_tensor(rank[:], bank[cum][:, 0:TT * NE].rearrange("p (t e) -> p t e", e=NE),
                             b["carry"][:].unsqueeze(1).broadcast_to([P, TT, NE]), ALU.add))
        V.tensor_tensor(b["carry"][:], bank[cum][:, TT * NE:TT * NE + NE], b["carry"][:], ALU.add).then_inc(free[cum], 1)
        link(V.tensor_tensor(slot[:], rank[:], w["base"][:], ALU.add))
    for k in range(TOPK):
        if part in (None, k + 1):
            for what, dst in ((rank, r), (slot, s)):
                link(V.tensor_tensor(prod[:], o[:, k, :, :], what[:], ALU.mult))
                link(V.tensor_reduce(dst[:, k, :], prod[:], AX.X, ALU.add))
    if part in (None, 2):
        link(V.tensor_scalar(kept[:], r[:], 1.0, None, ALU.is_ge))
        link(V.scalar_tensor_tensor(kept[:], r[:], float(CAP), kept[:], ALU.is_le, ALU.mult))
        link(V.tensor_scalar(r[:], kept[:], -BIG, BIG, ALU.mult, ALU.add))
        V.tensor_tensor(tab["w"][:, bass.ds(i * TOPK * TT, TOPK * TT)].rearrange("p (k t) -> p k t", t=TT),
                        p[:], kept[:], ALU.mult)
        V.tensor_tensor(b["idx"][:].rearrange("p (k t) -> p k t", t=TT), s[:], r[:], ALU.add).then_inc(S["idx_ready"], 1)


def router(nc, dve, link, b, w, J, bank, full, free, S, i, tab):
    take_logits(nc, dve, b, J, bank, full, free, i)
    for k in range(TOPK):
        route_top(nc, link, b, w, k)
    route_gap(nc, b, S)
    route_weights(nc, dve, link, b, S, i)
    route_ranks(nc, dve, link, b, w, J, bank, full, free, i, S, i, tab)


def count_picks(nc, pe, b, w, J, bank, full, free, S, i, turn=None):
    n = J.bank("cum")
    pe.wait_ge(free[n], J.turn(i if turn is None else turn, "cum"))
    pe.wait_ge(S["picks_ready"], i + 1)
    for t in range(TT + 1):
        for u in range(min(t + 1, TT)):
            tri = u == t
            ins = nc.tensor.matmul(bank[n][:, t * NE:(t + 1) * NE], (w["tri"] if tri else w["ones"])[:],
                                   b["oh"][:, u * NE:(u + 1) * NE], start=u == 0, stop=u == min(t, TT - 1))
    ins.then_inc(full[n], 1)


def logits(nc, pe, zT, wr, J, bank, full, free, i):
    n = J.bank("logit")
    pe.wait_ge(free[n], J.turn(i, "logit"))
    for c in range(CT):
        if J.bank(("zT", c)) != n:
            pe.wait_ge(free[J.bank(("zT", c))], J.drained(i, ("zT", c)))
    for t in range(TT):
        for c in range(CT):
            ins = nc.tensor.matmul(bank[n][:, t * NE:(t + 1) * NE], zT[:, c, t * P:(t + 1) * P], wr[:, c, :],
                                   start=c == 0, stop=c == CT - 1)
    ins.then_inc(full[n], 1)


def send_rows(nc, pool, z, b, d, S, i, tab):
    issue_rows(nc, pool, z, b, d, S, i, tab)
    pool.wait_ge(S["sent"], 16 * TOPK * TT * (i + 1))


def issue_rows(nc, pool, z, b, d, S, i, tab):
    pool.wait_ge(S["idx_ready"], i + 1)
    apart(pool, S["pool_passed"])
    nc.gpsimd.tensor_copy(tab["idx"][:, bass.ds(i * TOPK * TT, TOPK * TT)], b["idx"][:])
    for n in range(TOPK * TT):
        pool.indirect_dma_start(d["queue"], bass.IndirectOffsetOnAxis(ap=b["idx"][:, n:n + 1], axis=0),
                                z[:, n % TT, :], None, bounds_check=NE * CAP - 1, oob_is_err=False).then_inc(S["sent"], 16)


def root(nc, pool, link, mv, rs, rt, half, stats, turn, done, passed):
    pool.wait_ge(stats, turn)
    apart(pool, passed)
    link(nc.gpsimd.tensor_scalar(rt[:, 0, :], mv[:, :, 1], EPS, None, ALU.add))
    nc.gpsimd.tensor_tensor(rs[:, 0, :], rt[:, 0, :], half[:], ALU.pow).then_inc(done, 1)


def values(nc, pe, VT, wv, t, lo, width, J, bank, full, free, i):
    n = J.bank(("v", t))
    pe.wait_ge(free[n], J.turn(i, ("v", t)))
    for c in range(CT):
        ins = nc.tensor.matmul(bank[n][0:width, 0:C], VT[:, c, lo:lo + width], wv[:, c, :], start=c == 0, stop=c == CT - 1)
    ins.then_inc(full[n], 1)


def project(nc, pe, XT, lo, w, m, J, bank, full, free, i):
    n = J.bank(("qk", m))
    pe.wait_ge(free[n], J.turn(i, ("qk", m)))
    for c in range(CT):
        ins = nc.tensor.matmul(bank[n][:], w[:, c, m * P:(m + 1) * P], XT[:, c, lo:lo + T], start=c == 0, stop=c == CT - 1)
    ins.then_inc(full[n], 1)


PARTS = (("q_hi", "q_lo", 0), ("q_hi", "q_lo", 1), ("k_hi", "k_lo", 0), ("k_hi", "k_lo", 1))


def high_parts(nc, act, parts, bqk, J, bank, full, S, i):
    for m, (hi, _, c) in enumerate(PARTS):
        n = J.bank(("qk", m))
        act.wait_ge(full[n], J.turn(i, ("qk", m)))
        nc.scalar.activation(parts[hi][:, c, :], bank[n][:], ACT.Identity, bias=bqk[:, m:m + 1]).then_inc(S["hi_ready"], 1)


def low_parts(nc, dve, parts, bqk, J, bank, free, S, i):
    for m, (hi, lo, c) in enumerate(PARTS):
        n = J.bank(("qk", m))
        dve.wait_ge(S["hi_ready"], 4 * i + m + 1)
        nc.vector.scalar_tensor_tensor(parts[lo][:, c, :], bank[n][:], bqk[:, m:m + 1], parts[hi][:, c, :].bitcast(F32),
                                       ALU.add, ALU.subtract).then_inc(free[n], 1)


def output_tiles(nc, pe, oN, wo, J, bank, full, free, S, i):
    pe.wait_ge(S["on_ready"], NG * i + NG + 2)
    for t in range(TT):
        n = J.bank(("y", t))
        pe.wait_ge(free[n], J.turn(i, ("y", t)))
        for g in range(NG):
            ins = nc.tensor.matmul(bank[n][:, 0:C], oN[:, g, t * P:(t + 1) * P], wo[:, g, :], start=g == 0, stop=g == NG - 1)
        ins.then_inc(full[n], 1)


def spread_sums(nc, pe, g, slotsum, oT, J, bank, full, free, i):
    n = J.bank(("d", g))
    pe.wait_ge(free[n], J.turn(i, ("d", g)))
    pe.wait_ge(free[J.bank(("o", g))], J.drained(i, ("o", g)))
    nc.tensor.matmul(bank[n][:], slotsum[:], oT[:, g % 2, :], start=True, stop=True).then_inc(full[n], 1)


def copy_output(nc, act, g, oT, J, bank, full, free, S, i):
    n = J.bank(("o", g))
    act.wait_ge(full[n], J.turn(i, ("o", g)))
    act.wait_ge(S["on_ready"], NG * i + g + 1)
    nc.scalar.activation(oT[:, g % 2, :], bank[n][:], ACT.Copy).then_inc(free[n], 1)


def invert_sums(nc, dve, g, rD, J, bank, full, free, S, i):
    n = J.bank(("d", g))
    dve.wait_ge(full[n], J.turn(i, ("d", g)))
    dve.wait_ge(S["on_ready"], NG * i + g + 2)
    nc.vector.reciprocal(rD[:], bank[n][:]).then_inc(free[n], 1)


def normalize_outputs(nc, pool, oT, rD, oN, J, free, S, i):
    for g in range(NG):
        pool.wait_ge(free[J.bank(("d", g))], J.drained(i, ("d", g)))
        nc.gpsimd.tensor_tensor(oN[:, g, :], oT[:, g % 2, :], rD[:], ALU.mult).then_inc(S["on_ready"], 1)


def semaphore(nc, used, name):
    used.append(nc.alloc_semaphore(name))
    return used[-1]


def banks(nc, ctx, used, prefix):
    return ([ctx.enter_context(nc.psum_tensor(f"{prefix}_bank{n}", [P, 512], F32)) for n in range(8)],
            [semaphore(nc, used, f"{prefix}_full{n}") for n in range(8)],
            [semaphore(nc, used, f"{prefix}_free{n}") for n in range(8)])


def sems(nc, used, prefix, names):
    return {n: semaphore(nc, used, f"{prefix}_{n}") for n in names.split()}


def open_banks(pe, free):
    for f in free:
        pe.sem_inc(f, 1)


def load_all(engine, sem, loads):
    for dst, src in loads:
        engine.dma_start(dst, src).then_inc(sem, 16)
    return 16 * len(loads)


def slots_of(w_out):
    return w_out.rearrange("(g s d) n -> s d g n", g=NG, s=HG)


NKT, QW = 5, 3 * BUCKET


def queries_of(kt):
    q0, q1 = max(0, P * kt - BUCKET), min(T, P * kt + 2 * BUCKET)
    return q0, q1, q0 - (P * kt - BUCKET)


def phase_local(nc, ctx, used, a, d, tab):
    jobs = [(("hT", c), c) for c in range(CT)]
    jobs += [(("qk", m), (2, 3, 0, 1)[m]) for m in range(4)]
    jobs += [(("v", t), 2 + t % 2) for t in range(NKT)]
    jobs += [(("s", t, hp), 4 + hp % 2) for t in range(TT) for hp in range(NPAIR)]
    jobs += [("mT", 0)]
    for g in range(NG):
        jobs += [(("st", g, kt, e), e + 2 * (kt % 2)) for kt in range(NKT) for e in range(2)]
        jobs += [(("o", g), 6 + g % 2), (("d", g), 4 + g % 2)]
    jobs += [(("y", t), t) for t in range(TT)]
    jobs += [(("h2T", c), 4 + c) for c in range(CT)]
    jobs += [(("f1", m), m % 4) for m in range(FT)]
    jobs += [(("f2", t), 4 + t % 2) for t in range(TT)]
    jobs += [(("zT", c), 6 + c) for c in range(CT)]
    jobs += [("logit", 0), ("cum", 1)]
    J = Turns(jobs)

    def sb(name, shape, dt=F32):
        return ctx.enter_context(nc.sbuf_tensor("l_" + name, shape, dt))

    bank, full, free = banks(nc, ctx, used, "l")
    ident, identb, slotsum = sb("ident", [P, P]), sb("identb", [P, P], BF16), sb("slotsum", [P, P])
    masks, mask_q, mask_k = sb("masks", [P, 2, QW]), sb("mask_q", [P, QW], BF16), sb("mask_k", [P, QW], BF16)
    trif = sb("trif", [P, P])
    w = {"tri": sb("tri", [P, P], BF16), "ones": sb("ones", [P, P], BF16),
         "rev": sb("rev", [P, TT, NE]), "base": sb("base", [P, TT, NE])}
    g1, b1, g2, b2 = (sb(n, [P, CT]) for n in ("g1", "b1", "g2", "b2"))
    wqkv, bqk = sb("wqkv", [P, CT, 3 * C]), sb("bqk", [P, 4])
    bv, bo, bf2 = sb("bv", [P, C]), sb("bo", [P, C]), sb("bf2", [P, C])
    wo = sb("wo", [P, NG, C])
    w1, bf1, w2 = sb("w1", [P, CT, FF]), sb("bf1", [P, FT]), sb("w2", [P, FT, C])
    wr, half = sb("wr", [P, CT, NE]), sb("half", [P, TT])
    x = [sb(f"x{p}", [P, TT, C]) for p in range(2)]
    t0, y, z, hh = sb("t0", [P, TT, C]), sb("y", [P, TT, C]), sb("z", [P, TT, C]), sb("hh", [P, TT, C])
    st, mv = sb("st", [P, TT, 6]), sb("mv", [P, TT, 2])
    rs, rt = sb("rs", [P, 2, TT]), sb("rt", [P, 3, TT])
    hT, hT2 = sb("hT", [P, CT, KPAD]), sb("hT2", [P, CT, T])
    parts = {n: sb(n, [P, CT, T], F32R) for n in ("q_hi", "q_lo", "k_hi", "k_lo")}
    QS, KS = sb("QS", [P, NH, T], F32R), sb("KS", [P, NPAIR, KPAD], F32R)
    VP = sb("VP", [P, NKT, NH, 2 * HD])
    nm, mT = sb("nm", [P, TT, NH]), sb("mT", [NH, T], F32R)
    pr = sb("pr", [P, 2, HG, QW])
    oT, rD, oN = sb("oT", [P, 2, T]), sb("rD", [P, T]), sb("oN", [P, NG, T])
    G = sb("G", [P, FT, T])
    b = route_tiles(sb)
    zero = sb("zero", [P, C])

    S = sems(nc, used, "l", """weights out_weights zeroed cleared consts casts x_in0 x_in1 stats rstd t0_ready hh_ready hi_ready
        bounced stacked max_ready m_in pv_done on_ready t0b res_ready x1_out z_ready gap_ready gap_exp picks_ready
        idx_ready sent dve_own pool_own dve_passed pool_passed pe_passed sp_passed""")
    x_in = [S["x_in0"], S["x_in1"]]

    loads = [
        (ident[:], a["c_ident"]), (slotsum[:], a["c_slotsum"]), (masks[:], a["c_masks"]), (trif[:], a["c_tri"]),
        (w["rev"][:], a["c_rev"]), (w["base"][:], a["c_base"]),
        (g1[:], a["ln1_g"]), (b1[:], a["ln1_b"]), (g2[:], a["ln2_g"]), (b2[:], a["ln2_b"]),
        (wqkv[:], a["w_qkv"].rearrange("(c p) n -> p c n", p=P)), (bqk[:], a["b_qk"]),
        (bv[:], a["b_v"].partition_broadcast(P)), (bo[:], a["b_out"].partition_broadcast(P)),
        (bf2[:], a["b2"].partition_broadcast(P)), (w1[:], a["w1"].rearrange("(c p) n -> p c n", p=P)),
        (bf1[:], a["b1"]), (w2[:], a["w2"].rearrange("(m p) n -> p m n", p=P)),
        (wr[:], a["router"].rearrange("(c p) e -> p c e", p=P)),
    ]
    LOADED = 16 * len(loads)
    QUEUE_TILES = NE * CAP // P
    block = ctx.enter_context(nc.Block())

    @block.sync
    def _(sp):
        load_all(sp, S["weights"], loads)
        sp.dma_start(x[0][:], rows(a["x"], 0)).then_inc(x_in[0], 16)
        sp.wait_ge(S["zeroed"], 2)
        load_all(sp, S["out_weights"], [(wo[32 * s:32 * s + HD, :, :], slots_of(a["w_out"])[s]) for s in range(HG)])
        queue = d["queue"].rearrange("(t p) c -> t p c", p=P)
        for t in range(QUEUE_TILES):
            sp.dma_start(queue[t], zero[:]).then_inc(S["cleared"], 16)
        sp.sem_inc(S["x1_out"], 16)
        sp.sem_inc(S["stacked"], 16)
        sp.wait_ge(S["casts"], 16)

        def sequence(i, p, last):
            if not last:
                sp.dma_start(x[1 - p][:], rows(a["x"], i + 1)).then_inc(x_in[1 - p], 16)
            for m in range(4):
                sp.wait_ge(free[J.bank(("qk", m))], J.drained(i, ("qk", m)))
                apart(sp, S["sp_passed"])
            sp.wait_ge(S["pv_done"], NG * NKT * i + 2)
            apart(sp, S["sp_passed"])
            stack(sp, QS, KS, BUCKET, parts, d["bounce"], S, i)
            sp.wait_ge(free[J.bank("mT")], J.drained(i, "mT"))
            apart(sp, S["sp_passed"])
            sp.dma_start(QS[STACK:STACK + 1, :, :].bitcast(F32), mT[:, :].bitcast(F32)).then_inc(S["m_in"], 16)
            for t in range(TT):
                sp.wait_ge(free[J.bank(("f2", t))], J.drained(i, ("f2", t)))
                apart(sp, S["sp_passed"])
            sp.dma_start(rows(d["x1"], i), y[:]).then_inc(S["x1_out"], 16)

        all_but_last(sp, sequence)
        sp.wait_ge(S["x1_out"], 16 * NB + 16)

    @block.gpsimd
    def _(pool):
        V = nc.gpsimd
        V.memset(half[:], -0.5)
        pool.wait_ge(S["zeroed"], 2)
        pool.dma_start(KS[STACK:STACK + 1, :, :], a["c_one"]).then_inc(S["casts"], 16)
        pool.sem_inc(S["on_ready"], 2)
        chain = Chain(S["pool_own"], pool, 9, S["pool_passed"])
        pool.wait_ge(S["weights"], LOADED)

        def sequence(i, p):
            chain.start(i)
            pool.wait_ge(S["stats"], 3 * i + 1)
            apart(pool, S["pool_passed"])
            chain.link(V.tensor_scalar(rt[:, 0, :], mv[:, :, 1], EPS, None, ALU.add))
            chain.link(V.tensor_tensor(rs[:, 0, :], rt[:, 0, :], half[:], ALU.pow))
            chain.link(V.tensor_tensor(rt[:, 1, :], rs[:, 0, :], rs[:, 0, :], ALU.mult))
            chain.link(V.tensor_tensor(rt[:, 1, :], rt[:, 1, :], mv[:, :, 1], ALU.mult))
            apart(pool, S["pool_passed"])
            chain.link(V.tensor_scalar(rt[:, 1, :], rt[:, 1, :], EPS, None, ALU.add))
            chain.link(V.tensor_tensor(rt[:, 2, :], rt[:, 1, :], half[:], ALU.pow))
            V.tensor_tensor(rs[:, 1, :], rs[:, 0, :], rt[:, 2, :], ALU.mult).then_inc(S["rstd"], 1)
            pool.wait_ge(S["hh_ready"], 2 * i + 1)
            for t in range(TT):
                ins = V.tensor_tensor(t0[:, t, :], t0[:, t, :], bo[:], ALU.add)
            ins.then_inc(S["t0b"], 1)
            for t in range(TT):
                ins = V.tensor_tensor(x[p][:, t, :], x[p][:, t, :], bf2[:], ALU.add)
            chain.link(ins)
            normalize_outputs(nc, pool, oT, rD, oN, J, free, S, i)
            root(nc, pool, chain.link, mv, rs, rt, half, S["stats"], 3 * i + 2, S["rstd"], S["pool_passed"])
            V.tensor_tensor(x[p][:], x[p][:], y[:], ALU.add).then_inc(S["res_ready"], 1)
            root(nc, pool, chain.link, mv, rs, rt, half, S["stats"], 3 * i + 3, S["rstd"], S["pool_passed"])
            chain.end()
            pool.wait_ge(S["cleared"], 16 * QUEUE_TILES)
            send_rows(nc, pool, z, b, d, S, i, tab)

        pairs(pool, sequence)

    @block.scalar
    def _(act):
        A = nc.scalar
        act.wait_ge(S["weights"], LOADED)
        act.wait_ge(S["consts"], 1)

        def sequence(i, p):
            for c in range(CT):
                n = J.bank(("hT", c))
                act.wait_ge(full[n], J.turn(i, ("hT", c)))
                A.activation(hT[:, c, BUCKET:], bank[n][:], ACT.Identity, bias=b1[:, c:c + 1],
                             scale=g1[:, c:c + 1]).then_inc(free[n], 1)
            high_parts(nc, act, parts, bqk, J, bank, full, S, i)
            n = J.bank("mT")
            act.wait_ge(full[n], J.turn(i, "mT"))
            A.activation(mT[:, :], bank[n][0:NH, :], ACT.Copy).then_inc(free[n], 1)
            for g in range(NG):
                for kt in range(NKT):
                    q0, q1, _ = queries_of(kt)
                    nk, nq = min(P, KPAD - kt * P), q1 - q0
                    act.wait_ge(S["pv_done"], NKT * (NG * i + g) + kt + 1)
                    for e in range(2):
                        n = J.bank(("st", g, kt, e))
                        act.wait_ge(full[n], J.turn(i, ("st", g, kt, e)))
                        A.activation(pr[0:nk, kt % 2, 2 * e:2 * e + 2, 0:nq],
                                     bank[n][0:nk, 0:2 * nq].rearrange("p (h q) -> p h q", h=2),
                                     ACT.Exp).then_inc(free[n], 1)
                copy_output(nc, act, g, oT, J, bank, full, free, S, i)
            for c in range(CT):
                n = J.bank(("h2T", c))
                act.wait_ge(full[n], J.turn(i, ("h2T", c)))
                A.activation(hT2[:, c, :], bank[n][:], ACT.Identity, bias=b2[:, c:c + 1],
                             scale=g2[:, c:c + 1]).then_inc(free[n], 1)
            for m in range(FT):
                n = J.bank(("f1", m))
                act.wait_ge(full[n], J.turn(i, ("f1", m)))
                A.activation(G[:, m, :], bank[n][:], ACT.Gelu, bias=bf1[:, m:m + 1]).then_inc(free[n], 1)
            for c in range(CT):
                n = J.bank(("zT", c))
                act.wait_ge(full[n], J.turn(i, ("zT", c)))
                A.activation(hT2[:, c, :], bank[n][:], ACT.Copy).then_inc(free[n], 1)
            act.wait_ge(S["gap_ready"], i + 1)
            A.activation(b["e2"][:], b["gap"][:], ACT.Exp).then_inc(S["gap_exp"], 1)

        pairs(act, sequence)

    @block.vector
    def _(dve):
        V = nc.vector
        chain = Chain(S["dve_own"], dve, 3 + ROUTER_LINKS, S["dve_passed"])
        V.memset(zero[:], 0.0).then_inc(S["zeroed"], 1)
        V.memset(QS[:].bitcast(F32), 0.0)
        V.memset(KS[:].bitcast(F32), 0.0)
        V.memset(hT[:, :, 0:BUCKET], 0.0)
        V.memset(b["carry"][:], 0.0)
        V.memset(w["ones"][:], 1.0)
        V.memset(VP[:], 0.0)
        V.memset(wo[:], 0.0).then_inc(S["zeroed"], 1)
        dve.wait_ge(S["zeroed"], 2)
        V.memset(VP[:, :, :, HD:HD + 1], 1.0)
        dve.wait_ge(S["weights"], LOADED)
        V.tensor_copy(identb[:], ident[:])
        V.tensor_copy(mask_q[:], masks[:, 0, :])
        V.tensor_copy(mask_k[:], masks[:, 1, :])
        V.tensor_copy(w["tri"][:], trif[:])
        V.tensor_scalar(wqkv[:, :, 0:C], wqkv[:, :, 0:C], HD ** -0.5, None, ALU.mult)
        V.tensor_scalar(bqk[:, 0:CT], bqk[:, 0:CT], HD ** -0.5, None, ALU.mult).then_inc(S["consts"], 1)
        dve.wait_ge(S["consts"], 1)

        def sequence(i, j, p):
            chain.start(i)
            dve.wait_ge(x_in[p], 16 * j + 16)
            statistics(nc, chain, x[p], st, mv, S["stats"])
            dve.wait_ge(S["rstd"], 3 * i + 1)
            normalize(nc, x[p], t0, mv, rs[:, 0, :])
            normalize(nc, x[p], hh, mv, rs[:, 1, :]).then_inc(S["hh_ready"], 1)
            low_parts(nc, dve, parts, bqk, J, bank, free, S, i)
            for t in range(NKT):
                n, lo, hi = J.bank(("v", t)), (BUCKET if t == 0 else 0), min(P, KPAD - t * P)
                dve.wait_ge(full[n], J.turn(i, ("v", t)))
                V.tensor_tensor(VP[lo:hi, t, :, 0:HD], bank[n][lo:hi, 0:C].rearrange("p (h d) -> p h d", d=HD),
                                bv[lo:hi, :].rearrange("p (h d) -> p h d", d=HD), ALU.add).then_inc(free[n], 1)
            for t in range(TT):
                for hp in range(NPAIR):
                    n = J.bank(("s", t, hp))
                    dve.wait_ge(full[n], J.turn(i, ("s", t, hp)))
                    V.tensor_reduce(nm[:, t, 2 * hp:2 * hp + 2],
                                    bank[n][:, 0:2 * QW].rearrange("p (h k) -> p h k", h=2), AX.X, ALU.max,
                                    negate=True).then_inc(free[n], 1)
            for g in range(NG):
                invert_sums(nc, dve, g, rD, J, bank, full, free, S, i)
            dve.wait_ge(S["t0b"], i + 1)
            dve.wait_ge(S["x1_out"], 16 * i + 16)
            for t in range(TT):
                n = J.bank(("y", t))
                dve.wait_ge(full[n], J.turn(i, ("y", t)))
                V.tensor_tensor(y[:, t, :], bank[n][:, 0:C], t0[:, t, :], ALU.add).then_inc(free[n], 1)
            for t in range(TT):
                dve.wait_ge(free[J.bank(("y", t))], J.drained(i, ("y", t)))
            statistics(nc, chain, y, st, mv, S["stats"])
            dve.wait_ge(S["rstd"], 3 * i + 2)
            normalize(nc, y, hh, mv, rs[:, 0, :]).then_inc(S["hh_ready"], 1)
            dve.wait_ge(S["res_ready"], i + 1)
            for t in range(TT):
                n = J.bank(("f2", t))
                dve.wait_ge(full[n], J.turn(i, ("f2", t)))
                V.tensor_tensor(y[:, t, :], bank[n][:, 0:C], x[p][:, t, :], ALU.add).then_inc(free[n], 1)
            for t in range(TT):
                dve.wait_ge(free[J.bank(("f2", t))], J.drained(i, ("f2", t)))
            statistics(nc, chain, y, st, mv, S["stats"])
            dve.wait_ge(S["rstd"], 3 * i + 3)
            normalize(nc, y, z, mv, rs[:, 0, :]).then_inc(S["z_ready"], 1)
            router(nc, dve, chain.link, b, w, J, bank, full, free, S, i, tab)
            chain.end()

        with dve.Fori(0, NB // 2) as j:
            for p in range(2):
                sequence(2 * j + p, j, p)

    @block.tensor
    def _(pe):
        M = nc.tensor
        open_banks(pe, free)
        pe.sem_inc(S["pv_done"], 2)
        pe.wait_ge(S["weights"], LOADED)
        pe.wait_ge(S["out_weights"], 16 * HG)
        pe.wait_ge(S["consts"], 1)

        def sequence(i, p):
            pe.wait_ge(S["hh_ready"], 2 * i + 1)
            for c in range(CT):
                n = J.bank(("hT", c))
                pe.wait_ge(free[n], J.turn(i, ("hT", c)))
                transposes(nc, bank[n], hh, c, ident).then_inc(full[n], 1)
            for c in range(CT):
                pe.wait_ge(free[J.bank(("hT", c))], J.drained(i, ("hT", c)))
            for m in range(4):
                project(nc, pe, hT, BUCKET, wqkv, m, J, bank, full, free, i)
            for t in range(NKT):
                values(nc, pe, hT, wqkv[:, :, 2 * C:], t, P * t, min(P, KPAD - t * P), J, bank, full, free, i)
            pe.wait_ge(S["stacked"], 16 * STACK_DMAS * (i + 1) + 16)
            for t in range(TT):
                for hp in range(NPAIR):
                    n = J.bank(("s", t, hp))
                    pe.wait_ge(free[n], J.turn(i, ("s", t, hp)))
                    M.matmul(bank[n][:, 0:2 * QW].rearrange("p (h k) -> p h k", h=2), identb[:],
                             mask_q[:].unsqueeze(1).broadcast_to([P, 2, QW]), start=True, stop=False)
                    for e in range(2):
                        ins = M.matmul(bank[n][:, e * QW:(e + 1) * QW], QS[0:STACK, 2 * hp + e, t * P:(t + 1) * P],
                                       KS[0:STACK, hp, t * P:t * P + QW], start=False, stop=e == 1)
                    ins.then_inc(full[n], 1)
            for hp in (NPAIR - 2, NPAIR - 1):
                pe.wait_ge(free[J.bank(("s", TT - 1, hp))], J.drained(i, ("s", TT - 1, hp)))
            n = J.bank("mT")
            pe.wait_ge(free[n], J.turn(i, "mT"))
            for t in range(TT):
                ins = M.transpose(bank[n][0:NH, t * P:(t + 1) * P], nm[:, t, :], ident[:])
            ins.then_inc(full[n], 1)
            pe.wait_ge(S["m_in"], 16 * (i + 1))
            for g in range(NG):
                no = J.bank(("o", g))
                for kt in range(NKT):
                    q0, q1, m0 = queries_of(kt)
                    nk, nq = min(P, KPAD - kt * P), q1 - q0
                    for e in range(2):
                        n, hp = J.bank(("st", g, kt, e)), 2 * g + e
                        pe.wait_ge(free[n], J.turn(i, ("st", g, kt, e)))
                        apart(pe, S["pe_passed"])
                        to = bank[n][0:nk, 0:2 * nq].rearrange("p (h q) -> p h q", h=2)
                        M.matmul(to, identb[0:nk, 0:nk], mask_k[0:nk, m0:m0 + nq].unsqueeze(1).broadcast_to([nk, 2, nq]),
                                 start=True, stop=False)
                        M.matmul(to, KS[0:STACK + 1, hp, kt * P:kt * P + nk], QS[0:STACK + 1, 2 * hp:2 * hp + 2, q0:q1],
                                 start=False, stop=True).then_inc(full[n], 1)
                    if kt == 0:
                        pe.wait_ge(free[no], J.turn(i, ("o", g)))
                    for e in range(2):
                        n = J.bank(("st", g, kt, e))
                        pe.wait_ge(free[n], J.drained(i, ("st", g, kt, e)))
                    apart(pe, S["pe_passed"])
                    for s in range(HG):
                        ins = M.matmul(bank[no][32 * s:32 * s + 32, q0:q1], VP[0:nk, kt, HG * g + s, :],
                                       pr[0:nk, kt % 2, s, 0:nq], start=kt == 0, stop=kt == NKT - 1,
                                       skip_group_check=True)
                    ins.then_inc(S["pv_done"], 1)
                pe.wait_ge(S["pv_done"], NKT * (NG * i + g + 1) + 2)
                pe.sem_inc(full[no], 1)
                spread_sums(nc, pe, g, slotsum, oT, J, bank, full, free, i)
            output_tiles(nc, pe, oN, wo, J, bank, full, free, S, i)
            pe.wait_ge(S["hh_ready"], 2 * i + 2)
            for c in range(CT):
                n = J.bank(("h2T", c))
                pe.wait_ge(free[n], J.turn(i, ("h2T", c)))
                transposes(nc, bank[n], hh, c, ident).then_inc(full[n], 1)
            for c in range(CT):
                pe.wait_ge(free[J.bank(("h2T", c))], J.drained(i, ("h2T", c)))
            for m in range(FT):
                n = J.bank(("f1", m))
                pe.wait_ge(free[n], J.turn(i, ("f1", m)))
                for c in range(CT):
                    ins = M.matmul(bank[n][:], w1[:, c, m * P:(m + 1) * P], hT2[:, c, :], start=c == 0, stop=c == CT - 1)
                ins.then_inc(full[n], 1)
            for m in range(FT - 4, FT):
                pe.wait_ge(free[J.bank(("f1", m))], J.drained(i, ("f1", m)))
            for t in range(TT):
                n = J.bank(("f2", t))
                pe.wait_ge(free[n], J.turn(i, ("f2", t)))
                for m in range(FT):
                    ins = M.matmul(bank[n][:, 0:C], G[:, m, t * P:(t + 1) * P], w2[:, m, :], start=m == 0, stop=m == FT - 1)
                ins.then_inc(full[n], 1)
            pe.wait_ge(S["z_ready"], i + 1)
            for c in range(CT):
                n = J.bank(("zT", c))
                pe.wait_ge(free[n], J.turn(i, ("zT", c)))
                transposes(nc, bank[n], z, c, ident).then_inc(full[n], 1)
            logits(nc, pe, hT2, wr, J, bank, full, free, i)
            count_picks(nc, pe, b, w, J, bank, full, free, S, i)

        pairs(pe, sequence)


def phase_experts(nc, ctx, used, a, d, prefix):
    per_seq = CAP // T
    jobs = [(("xT", c), c) for c in range(CT)]
    jobs += [(("h", m), 2 + m) for m in range(EI // P)]
    jobs += [(("o", t), 6 + t % 2) for t in range(TT)]
    J = Turns(jobs)
    def sb(name, shape, dt=F32):
        return ctx.enter_context(nc.sbuf_tensor(prefix + name, shape, dt))

    bank, full, free = banks(nc, ctx, used, prefix)
    ident = sb("ident", [P, P])
    x = [sb(f"x{p}", [P, TT, C]) for p in range(2)]
    w1 = [sb(f"w1{p}", [P, CT, EI]) for p in range(2)]
    w2 = [sb(f"w2{p}", [P, EI // P, C]) for p in range(2)]
    xT, h = sb("xT", [P, CT, T]), sb("h", [P, EI // P, T])
    y = [sb(f"y{p}", [P, TT, C]) for p in range(2)]
    S = sems(nc, used, prefix, "ident x_in0 x_in1 w_in0 w_in1 y_out0 y_out1 sp_passed")
    x_in, w_in, y_out = ([S[n + str(p)] for p in range(2)] for n in ("x_in", "w_in", "y_out"))
    block = ctx.enter_context(nc.Block())

    def chunks(engine, chunk):
        with engine.Fori(0, NE // 2) as j:
            for q in range(2 * per_seq):
                chunk(2 * per_seq * j + q, j, q)

    def weights_of(engine, e, at):
        engine.dma_start(w1[at][:], a["first"][bass.ds(e * C, C), :].rearrange("(c p) i -> p c i", p=P)).then_inc(w_in[at], 16)
        engine.dma_start(w2[at][:], a["second"][bass.ds(e * EI, EI), :].rearrange("(m p) n -> p m n", p=P)).then_inc(w_in[at], 16)

    @block.sync
    def _(sp):
        sp.dma_start(ident[:], a["c_ident"]).then_inc(S["ident"], 16)

        def chunk(n, j, q):
            if q % per_seq == 0:
                if q == 0:
                    sp.wait_ge(free[J.bank(("xT", 0))], J.turn(n, ("xT", 0)))
                    apart(sp, S["sp_passed"])
                weights_of(sp, 2 * j + q // per_seq, q // per_seq)
            sp.dma_start(x[q % 2][:], rows(d["queue"], n)).then_inc(x_in[q % 2], 16)
            sp.wait_ge(free[J.bank(("xT", 1))], J.turn(n, ("xT", 1)))
            apart(sp, S["sp_passed"])

        chunks(sp, chunk)

    @block.scalar
    def _(act):
        for p in range(2):
            act.sem_inc(y_out[p], 16)

        def chunk(n, j, q):
            for c in range(CT):
                k = J.bank(("xT", c))
                act.wait_ge(full[k], J.turn(n, ("xT", c)))
                nc.scalar.activation(xT[:, c, :], bank[k][:], ACT.Copy).then_inc(free[k], 1)
            for m in (0, 2):
                k = J.bank(("h", m))
                act.wait_ge(full[k], J.turn(n, ("h", m)))
                nc.scalar.activation(h[:, m, :], bank[k][:], ACT.Relu).then_inc(free[k], 1)
            for t in range(TT):
                act.wait_ge(free[J.bank(("o", t))], J.drained(n, ("o", t)))
            act.dma_start(rows(d["done"], n), y[q % 2][:]).then_inc(y_out[q % 2], 16)

        chunks(act, chunk)
        for p in range(2):
            act.wait_ge(y_out[p], 16 * (NE * per_seq // 2) + 16)

    @block.vector
    def _(dve):
        def chunk(n, j, q):
            for m in (1, 3):
                k = J.bank(("h", m))
                dve.wait_ge(full[k], J.turn(n, ("h", m)))
                nc.vector.tensor_scalar(h[:, m, :], bank[k][:], 0.0, None, ALU.max).then_inc(free[k], 1)
            dve.wait_ge(y_out[q % 2], 16 * (per_seq * j + q // 2) + 16)
            for t in range(TT):
                k = J.bank(("o", t))
                dve.wait_ge(full[k], J.turn(n, ("o", t)))
                nc.vector.tensor_copy(y[q % 2][:, t, :], bank[k][:, 0:C]).then_inc(free[k], 1)

        chunks(dve, chunk)

    @block.tensor
    def _(pe):
        open_banks(pe, free)
        pe.wait_ge(S["ident"], 16)

        def chunk(n, j, q):
            pe.wait_ge(x_in[q % 2], 16 * (per_seq * j + q // 2) + 16)
            for c in range(CT):
                k = J.bank(("xT", c))
                pe.wait_ge(free[k], J.turn(n, ("xT", c)))
                transposes(nc, bank[k], x[q % 2], c, ident).then_inc(full[k], 1)
            at = q // per_seq
            if q % per_seq == 0:
                pe.wait_ge(w_in[at], 32 * j + 32)
            for c in range(CT):
                pe.wait_ge(free[J.bank(("xT", c))], J.drained(n, ("xT", c)))
            for m in range(EI // P):
                k = J.bank(("h", m))
                pe.wait_ge(free[k], J.turn(n, ("h", m)))
                for c in range(CT):
                    ins = nc.tensor.matmul(bank[k][:], w1[at][:, c, m * P:(m + 1) * P], xT[:, c, :], start=c == 0, stop=c == CT - 1)
                ins.then_inc(full[k], 1)
            for m in range(EI // P):
                pe.wait_ge(free[J.bank(("h", m))], J.drained(n, ("h", m)))
            for t in range(TT):
                k = J.bank(("o", t))
                pe.wait_ge(free[k], J.turn(n, ("o", t)))
                for m in range(EI // P):
                    ins = nc.tensor.matmul(bank[k][:, 0:C], h[:, m, t * P:(t + 1) * P], w2[at][:, m, :], start=m == 0, stop=m == EI // P - 1)
                ins.then_inc(full[k], 1)

        chunks(pe, chunk)


def fetch_rows(nc, pool, got, idx, d, S, tab, i, p, link):
    link(nc.gpsimd.tensor_copy(idx[p][:], tab["idx"][:, bass.ds(i * TOPK * TT, TOPK * TT)]))
    apart(pool, S["pool_passed"])
    for n in range(TOPK * TT):
        pool.indirect_dma_start(got[p][:, n, :], None, d["done"], bass.IndirectOffsetOnAxis(ap=idx[p][:, n:n + 1], axis=0),
                                bounds_check=NE * CAP - 1, oob_is_err=False).then_inc(S[f"got{p}"], 16)


def combine(nc, link, x, got, wt, tab, i):
    link(nc.vector.tensor_copy(wt[:], tab["w"][:, bass.ds(i * TOPK * TT, TOPK * TT)]))
    for k in range(TOPK):
        for t in range(TT):
            n = k * TT + t
            ins = nc.vector.scalar_tensor_tensor(x[:, t, :], got[:, n, :], wt[:, n:n + 1], x[:, t, :], ALU.mult, ALU.add)
        if k == 0:
            link(ins)
    return ins


UNITS = 2 * TT * NG
ALL_STAGES = "FSAOC"
STAGE_LEAD = {"F": 2, "S": 1, "A": 0, "O": -1, "C": -2}


def stages(i):
    return "".join(k for k in ALL_STAGES if 0 <= i + STAGE_LEAD[k] < NB)


def periods(engine, period):
    for i in range(-2, 2):
        period(i, i % 2, stages(i))
    with engine.Fori(1, NB // 2 - 2) as j:
        for p in range(2):
            period(2 * j + p, p, ALL_STAGES)
    for i in range(NB - 4, NB + 2):
        period(i, i % 2, stages(i))


def after(engine, sem, value):
    if not isinstance(value, int) or value > 0:
        engine.wait_ge(sem, value)


def stack_half(sp, QS, KS, half, bounce, sem):
    by_head = {k: v.rearrange("s (f a e d) n -> s f e d a n", f=2, e=2, d=HD) for k, v in bounce.items()}
    for blk, (q, k) in enumerate(((0, 0), (0, 1), (1, 0))):
        for e in range(2):
            to = 3 * HD * e + HD * blk
            sp.dma_start(QS[to:to + HD, 8 * half + e:8 * half + 8:2, :].bitcast(F32), by_head["q"][q, half, e]).then_inc(sem, 16)
            sp.dma_start(KS[to:to + HD, 4 * half:4 * half + 4, :].bitcast(F32), by_head["k"][k, half, e]).then_inc(sem, 16)


HALF_DMAS = 12


def phase_alibi(nc, ctx, used, a, d, tab):
    ROWS = STACK + 6
    MISC = [(0, "cum", "C"), (1, ("mT", 1), "A"), (2, ("v", 0), "S"), (3, ("v", 1), "S"),
            (4, ("n", 0), "O"), (5, ("n", 1), "O"), (6, ("tT", 0), "F"), (7, ("n", 2), "O"), (8, ("n", 3), "O"),
            (9, ("tT", 1), "F"), (10, ("qk", 0), "F"), (11, ("nT", 0), "O"), (12, ("qk", 1), "F"),
            (13, ("nT", 1), "O"), (14, ("qk", 2), "F"), (15, ("y", 0), "O"), (16, ("qk", 3), "F"),
            (17, ("y", 1), "O"), (18, ("mT", 0), "S"), (23, ("zT", 0), "O"), (24, ("zT", 1), "O"), (26, "logit", "O")]
    AT = {job: u for u, job, _ in MISC}
    MISC_BANK = 7
    JM = Turns([(job, MISC_BANK) for _, job, _ in MISC])
    JS = Turns([(("s", n), 4 + n % 2) for n in range(2 * UNITS)])
    JA = Turns([(("st", u), u % 2) for u in range(UNITS)])
    JO = Turns([(("o", g), 6) for g in range(NG)])

    def sb(name, shape, dt=F32):
        return ctx.enter_context(nc.sbuf_tensor("b_" + name, shape, dt))

    scores_at = [ctx.enter_context(nc.psum_tensor(f"b_scores{n}", [P, 2, T], F32)) for n in range(2)]
    bank = {n: ctx.enter_context(nc.psum_tensor(f"b_bank{n}", [P, 512], F32)) for n in (4, 5, 6, 7)}
    full = {n: semaphore(nc, used, f"b_full{n}") for n in (0, 1, 4, 5, 7)}
    free = {n: semaphore(nc, used, f"b_free{n}") for n in (0, 1, 4, 5, 6, 7)}
    misc, misc_full, misc_free = bank[MISC_BANK], full[MISC_BANK], free[MISC_BANK]

    ident = sb("ident", [P, P])
    w = {"tri": sb("tri", [P, P], BF16), "ones": sb("ones", [P, P], BF16),
         "rev": sb("rev", [P, TT, NE]), "base": sb("base", [P, TT, NE])}
    wqk, bqk, wv = sb("wqk", [P, CT, 2 * C]), sb("bqk", [P, 4]), sb("wv", [P, CT, C])
    bv, bo, wo = sb("bv", [P, C]), sb("bo", [P, C]), sb("wo", [P, CT, C])
    wr, half = sb("wr", [P, CT, NE]), sb("half", [P, TT])
    x = sb("x", [P, TT, C])
    got = [sb(f"got{p}", [P, TOPK * TT, C]) for p in range(2)]
    idx = [sb(f"idx{p}", [P, TOPK * TT], U32) for p in range(2)]
    wt, t0, tT = sb("wt", [P, TOPK * TT]), sb("t0", [P, TT, C]), sb("tT", [P, CT, T])
    st = {k: sb("st" + k, [P, TT, 6]) for k in "FO"}
    mv = {k: sb("mv" + k, [P, TT, 2]) for k in "FO"}
    rs = {k: sb("rs" + k, [P, 1, TT]) for k in "FO"}
    rt = sb("rt", [P, 1, TT])
    parts = [sb(f"parts{n}", [P, 2, T], F32R) for n in range(2)]
    QS, KS = ([sb(f"{n}{p}", [P, heads, T], F32R) for p in range(2)] for n, heads in (("QS", NH), ("KS", NPAIR)))
    VP = [sb(f"VP{p}", [P, TT, NH, 2 * HD]) for p in range(2)]
    nm, mT = sb("nm", [P, TT, NH]), [sb(f"mT{f}", [NH // 2, T], F32R) for f in range(2)]
    pr, oT = sb("pr", [P, 2, HG, T]), sb("oT", [P, NG, T])
    sums, on, nT = sb("sums", [P, NH]), sb("on", [P, TT, C]), sb("nT", [P, CT, T])
    res, z = sb("res", [P, TT, C]), sb("z", [P, TT, C])
    b = route_tiles(sb)
    trif = z[:, 0, 0:P]
    S = sems(nc, used, "b", """weights zeroed casts consts x_in got0 got1 combined statsF statsO rstdF rstdO t0_ready hi_ready
        bounced0 bounced1 stacked0 stacked1 m_in0 m_in1 pv_done sums_own on_ready x2_out res_in res_ready x3_out z_ready
        gap_ready gap_exp picks_ready idx_ready sent fetch_own f_own o_own c_own poolF_own poolO_own
        dve_passed pool_passed pe_passed sp_passed act_passed""")
    bounce, bounced = d["bounce"], [S["bounced0"], S["bounced1"]]
    stacked, m_in, got_in = [S["stacked0"], S["stacked1"]], [S["m_in0"], S["m_in1"]], [S["got0"], S["got1"]]

    def mat(m):
        return m.rearrange("(c p) n -> p c n", p=P)

    loads = [
        (ident[:], a["c_ident"]), (trif, a["c_tri"]),
        (w["rev"][:], a["c_rev"]), (w["base"][:], a["c_base"]),
        (wqk[:, :, 0:C], mat(a["wq"])), (wqk[:, :, C:2 * C], mat(a["wk"])), (wv[:], mat(a["wv"])), (wo[:], mat(a["wo"])),
        (bqk[:, 0:CT], a["bq"]), (bqk[:, CT:2 * CT], a["bk"]),
        (bv[:], a["bv"].partition_broadcast(P)), (bo[:], a["bo"].partition_broadcast(P)),
        (wr[:], a["router"].rearrange("(c p) e -> p c e", p=P)),
    ]
    LOADED = 16 * len(loads)
    block = ctx.enter_context(nc.Block())

    def m_row(sp, f, buf, s):
        sp.dma_start(QS[buf][ROWS:ROWS + 1, 8 * f:8 * f + 8, :].bitcast(F32), mT[f][:, :].bitcast(F32)).then_inc(m_in[f], 16)

    @block.sync
    def _(sp):
        load_all(sp, S["weights"], loads)
        sp.dma_start(x[:], rows(d["x1"], 0)).then_inc(S["x_in"], 16)
        sp.wait_ge(S["casts"], 64)

        def period(i, p, on_now):
            n = i + 2
            if "O" in on_now:
                after(sp, S["z_ready"], i - 1)
                apart(sp, S["sp_passed"])
                after(sp, S["x3_out"], 16 * (i - 1))
                apart(sp, S["sp_passed"])
                sp.dma_start(res[:], rows(d["x2"], i - 1)).then_inc(S["res_in"], 16)
            if "S" in on_now:
                after(sp, S["pv_done"], NG * TT * i)
                apart(sp, S["sp_passed"])
                stack_half(sp, QS[1 - p], KS[1 - p], 1, bounce, stacked[1])
            if "A" in on_now:
                sp.wait_ge(misc_free, JM.drained(n, ("mT", 1)))
                apart(sp, S["sp_passed"])
                m_row(sp, 1, p, i)
            if "F" in on_now:
                sp.wait_ge(S["combined"], i + 3)
                apart(sp, S["sp_passed"])
                sp.dma_start(rows(d["x2"], i + 2), x[:]).then_inc(S["x2_out"], 16)
                if not isinstance(i, int) or i + 3 < NB:
                    sp.wait_ge(S["t0_ready"], i + 3)
                    apart(sp, S["sp_passed"])
                    sp.wait_ge(S["x2_out"], 16 * (i + 3))
                    apart(sp, S["sp_passed"])
                    sp.dma_start(x[:], rows(d["x1"], i + 3)).then_inc(S["x_in"], 16)
                after(sp, stacked[1], 16 * HALF_DMAS * (i + 2))
                apart(sp, S["sp_passed"])
                for m in range(4):
                    sp.wait_ge(misc_free, JM.drained(n, ("qk", m)))
                    apart(sp, S["sp_passed"])
                    sp.dma_start(bounce["qk"[m // 2]][:, (m % 2) * P:(m % 2 + 1) * P, :].rearrange("s p n -> p s n"),
                                 parts[m % 2][:].bitcast(F32)).then_inc(bounced[m % 2], 16)
                for k in range(2):
                    sp.wait_ge(bounced[k], 32 * (i + 3))
                    apart(sp, S["sp_passed"])
                after(sp, S["pv_done"], NG * TT * i + 8)
                apart(sp, S["sp_passed"])
                stack_half(sp, QS[p], KS[p], 0, bounce, stacked[0])
            if "S" in on_now:
                sp.wait_ge(misc_free, JM.drained(n, ("mT", 0)))
                apart(sp, S["sp_passed"])
                m_row(sp, 0, 1 - p, i + 1)
            if "O" in on_now:
                sp.wait_ge(misc_free, JM.drained(n, ("y", 1)))
                apart(sp, S["sp_passed"])
                sp.dma_start(rows(d["x3"], i - 1), res[:]).then_inc(S["x3_out"], 16)

        periods(sp, period)
        sp.wait_ge(S["x3_out"], 16 * NB)
        sp.wait_ge(S["x2_out"], 16 * NB)
        for k in range(2):
            sp.wait_ge(bounced[k], 32 * NB)

    @block.gpsimd
    def _(pool):
        V = nc.gpsimd
        V.memset(half[:], -0.5)
        pool.wait_ge(S["zeroed"], 1)
        for p in range(2):
            pool.dma_start(KS[p][STACK:ROWS + 1, :, :], a["c_alibi_k"]).then_inc(S["casts"], 16)
            pool.dma_start(QS[p][STACK:ROWS, :, :], a["c_alibi_q"]).then_inc(S["casts"], 16)
        fetch = Chain(S["fetch_own"], pool, 1, S["pool_passed"])
        chain_f = Chain(S["poolF_own"], pool, 1, S["pool_passed"])
        chain_o = Chain(S["poolO_own"], pool, 1, S["pool_passed"])
        fetch.start(0)
        fetch_rows(nc, pool, got, idx, d, S, tab, 0, 0, fetch.link)
        pool.wait_ge(S["weights"], LOADED)

        def period(i, p, on_now):
            if "F" in on_now:
                chain_f.start(i + 2)
                if not isinstance(i, int) or i + 3 < NB:
                    fetch.start(i + 3)
                    fetch_rows(nc, pool, got, idx, d, S, tab, i + 3, 1 - p, fetch.link)
                root(nc, pool, chain_f.link, mv["F"], rs["F"], rt, half, S["statsF"], i + 3, S["rstdF"], S["pool_passed"])
            if "C" in on_now:
                issue_rows(nc, pool, z, b, d, S, i - 2, tab)
            if "O" in on_now:
                pool.wait_ge(S["res_in"], 16 * i)
                apart(pool, S["pool_passed"])
                V.tensor_tensor(res[:], res[:], bo[:].unsqueeze(1).broadcast_to([P, TT, C]), ALU.add).then_inc(S["res_ready"], 1)
            if "C" in on_now:
                pool.wait_ge(S["sent"], 16 * TOPK * TT * (i - 1))
            if "O" in on_now:
                chain_o.start(i - 1)
                root(nc, pool, chain_o.link, mv["O"], rs["O"], rt, half, S["statsO"], i, S["rstdO"], S["pool_passed"])

        periods(pool, period)

    @block.scalar
    def _(act):
        A = nc.scalar
        act.wait_ge(S["weights"], LOADED)
        act.wait_ge(S["consts"], 1)

        def copy(n, job, dst, src):
            act.wait_ge(misc_full, JM.turn(n, job))
            A.activation(dst, src, ACT.Copy).then_inc(misc_free, 1)

        def copy_group(s, g):
            act.wait_ge(S["pv_done"], TT * (NG * s + g + 1))
            A.activation(oT[:, g, :], bank[6][:], ACT.Copy).then_inc(free[6], 1)

        def period(i, p, on_now):
            n = i + 2
            for u in range(UNITS):
                slot = u // 2
                if "A" in on_now:
                    if u % 2 == 0:
                        after(act, S["pv_done"], NG * TT * i + slot - 1)
                    act.wait_ge(full[u % 2], JA.turn(i, ("st", u)))
                    A.activation(pr[:, slot % 2, 2 * (u % 2):2 * (u % 2) + 2, :], scores_at[u % 2][:],
                                 ACT.Exp).then_inc(free[u % 2], 1)
                if u == AT["mT", 1] and "A" in on_now:
                    after(act, m_in[1], 16 * i)
                    copy(n, ("mT", 1), mT[1][:, :], misc[0:NH // 2, :])
                if u == 1 and "O" in on_now:
                    copy_group(i - 1, NG - 1)
                for c in range(CT):
                    if u == AT["tT", c] and "F" in on_now:
                        copy(n, ("tT", c), tT[:, c, :], misc[:])
                    if u == AT["nT", c] and "O" in on_now:
                        copy(n, ("nT", c), nT[:, c, :], misc[:])
                    if u == AT["zT", c] and "O" in on_now:
                        copy(n, ("zT", c), nT[:, c, :], misc[:])
                if u in (9, 17, 25) and "A" in on_now:
                    if u == 9:
                        after(act, misc_full, JM.turn(n, ("n", 3)))
                    copy_group(i, u // 8 - 1)
                for m in range(4):
                    if u == AT["qk", m] and "F" in on_now:
                        after(act, bounced[m % 2], 16 * (2 * (i + 2) + m // 2))
                        act.wait_ge(misc_full, JM.turn(n, ("qk", m)))
                        A.activation(parts[m % 2][:, 0, :], misc[:], ACT.Identity, bias=bqk[:, m:m + 1]).then_inc(S["hi_ready"], 1)
                if u == AT["mT", 0] and "S" in on_now:
                    after(act, m_in[0], 16 * (i + 1))
                    copy(n, ("mT", 0), mT[0][:, :], misc[0:NH // 2, :])
                if u == 29 and "O" in on_now:
                    act.wait_ge(S["gap_ready"], i)
                    A.activation(b["e2"][:], b["gap"][:], ACT.Exp).then_inc(S["gap_exp"], 1)

        periods(act, period)

    @block.vector
    def _(dve):
        V = nc.vector
        chain_f = Chain(S["f_own"], dve, 3, S["dve_passed"])
        chain_o = Chain(S["o_own"], dve, 1 + TOP_LINKS + WEIGHT_LINKS, S["dve_passed"])
        chain_c = Chain(S["c_own"], dve, RANK_LINKS, S["dve_passed"])
        for p in range(2):
            V.memset(QS[p][:].bitcast(F32), 0.0)
            V.memset(KS[p][:].bitcast(F32), 0.0)
            V.memset(got[p][:], 0.0)
            V.memset(VP[p][:], 0.0)
        V.memset(b["carry"][:], 0.0)
        V.memset(w["ones"][:], 1.0).then_inc(S["zeroed"], 1)
        dve.wait_ge(S["zeroed"], 1)
        for p in range(2):
            V.memset(VP[p][:, :, :, HD:HD + 1], 1.0)
        dve.wait_ge(S["weights"], LOADED)
        V.tensor_copy(w["tri"][:], trif)
        V.tensor_scalar(wqk[:, :, 0:C], wqk[:, :, 0:C], HD ** -0.5, None, ALU.mult)
        V.tensor_scalar(bqk[:, 0:CT], bqk[:, 0:CT], HD ** -0.5, None, ALU.mult).then_inc(S["consts"], 1)
        dve.wait_ge(S["consts"], 1)

        def add_pick(f, k, buf):
            for t in range(TT):
                ins = V.scalar_tensor_tensor(x[:, t, :], got[buf][:, k * TT + t, :], wt[:, k * TT + t:k * TT + t + 1], x[:, t, :],
                                             ALU.mult, ALU.add)
            return ins

        def period(i, p, on_now):
            n = i + 2
            for u in range(UNITS):
                if "S" in on_now:
                    h = u // 2
                    if u == 0 and "A" in on_now:
                        dve.wait_ge(misc_full, JM.turn(n - 1, ("mT", 0)))
                    if u == UNITS // 2 and "A" in on_now:
                        dve.wait_ge(misc_full, JM.turn(n, ("mT", 1)))
                    for t in (2 * (u % 2), 2 * (u % 2) + 1):
                        k = JS.bank(("s", 4 * h + t))
                        dve.wait_ge(full[k], JS.turn(i + 1, ("s", 4 * h + t)))
                        V.tensor_reduce(nm[:, t, h:h + 1], bank[k][:], AX.X, ALU.max, negate=True).then_inc(free[k], 1)
                if "F" in on_now:
                    if u == 0:
                        chain_f.start(i + 2)
                        dve.wait_ge(S["x_in"], 16 * (i + 3))
                        dve.wait_ge(got_in[p], 8 * TOPK * TT * (i - p + 4))
                        chain_f.link(V.tensor_copy(wt[:], tab["w"][:, bass.ds((i + 2) * TOPK * TT, TOPK * TT)]))
                        chain_f.link(add_pick(i + 2, 0, p))
                    if u == 1:
                        add_pick(i + 2, 1, p).then_inc(S["combined"], 1)
                        dve.wait_ge(S["combined"], i + 3)
                    if u == 2:
                        statistics(nc, chain_f, x, st["F"], mv["F"], S["statsF"])
                    if u == 5:
                        dve.wait_ge(S["rstdF"], i + 3)
                        normalize(nc, x, t0, mv["F"], rs["F"][:, 0, :]).then_inc(S["t0_ready"], 1)
                    for m in range(4):
                        if u == AT["qk", m]:
                            dve.wait_ge(S["hi_ready"], 4 * (i + 2) + m + 1)
                            V.scalar_tensor_tensor(parts[m % 2][:, 1, :], misc[:], bqk[:, m:m + 1], parts[m % 2][:, 0, :].bitcast(F32),
                                                   ALU.add, ALU.subtract).then_inc(misc_free, 1)
                for q in range(2):
                    if u == AT["v", q] and "S" in on_now:
                        after(dve, S["pv_done"], NG * TT * i)
                        dve.wait_ge(misc_full, JM.turn(n, ("v", q)))
                        V.tensor_tensor(VP[1 - p][:, 2 * q:2 * q + 2, :, 0:HD], misc[:].rearrange("p (t h d) -> p t h d", t=2, d=HD),
                                        bv[:].rearrange("p (h d) -> p h d", d=HD).unsqueeze(1).broadcast_to([P, 2, NH, HD]),
                                        ALU.add).then_inc(misc_free, 1)
                if "C" in on_now and u in (1, 3, 4):
                    if u == 1:
                        chain_c.start(i - 2)
                    route_ranks(nc, dve, chain_c.link, b, w, JM, bank, full, free, n, S, i - 2, tab, {1: 0, 3: 1, 4: 2}[u])
                if "O" in on_now:
                    if u == 0:
                        chain_o.start(i - 1)
                    for t in range(TT):
                        if u == AT["n", t]:
                            dve.wait_ge(misc_full, JM.turn(n, ("n", t)))
                            by_head = misc[:].rearrange("p (h r) -> p h r", r=2 * HD)
                            V.reciprocal(sums[:], by_head[:, :, HD]).then_inc(S["sums_own"], 1)
                            dve.wait_ge(S["sums_own"], TT * (i - 1) + t + 1)
                            V.tensor_tensor(on[:, t, :].rearrange("p (h d) -> p h d", d=HD), by_head[:, :, 0:HD],
                                            sums[:].unsqueeze(2).broadcast_to([P, NH, HD]), ALU.mult).then_inc(misc_free, 1)
                    for q in range(2):
                        if u == AT["y", q]:
                            dve.wait_ge(S["res_ready"], i)
                            dve.wait_ge(misc_full, JM.turn(n, ("y", q)))
                            V.tensor_tensor(res[:, 2 * q:2 * q + 2, :], misc[:].rearrange("p (t n) -> p t n", t=2),
                                            res[:, 2 * q:2 * q + 2, :], ALU.add).then_inc(misc_free, 1)
                            dve.wait_ge(misc_free, JM.drained(n, ("y", q)))
                    if u == 18:
                        statistics(nc, chain_o, res, st["O"], mv["O"], S["statsO"])
                    if u == 21:
                        dve.wait_ge(S["rstdO"], i)
                        normalize(nc, res, z, mv["O"], rs["O"][:, 0, :]).then_inc(S["z_ready"], 1)
                    if u == AT["logit"]:
                        take_logits(nc, dve, b, JM, bank, full, free, n)
                        route_top(nc, chain_o.link, b, w, 0)
                    if u == AT["logit"] + 1:
                        route_top(nc, chain_o.link, b, w, 1)
                    if u == AT["logit"] + 2:
                        route_gap(nc, b, S)
                    if u == AT["logit"] + 4:
                        route_weights(nc, dve, chain_o.link, b, S, i - 1)

        periods(dve, period)

    @block.tensor
    def _(pe):
        M = nc.tensor
        for f in free.values():
            pe.sem_inc(f, 1)
        pe.wait_ge(S["weights"], LOADED)
        pe.wait_ge(S["consts"], 1)

        def products(i, p, slot):
            g, kt = slot // TT, slot % TT
            for e in range(2):
                pe.wait_ge(free[e], JA.drained(i, ("st", 2 * slot + e)))
            if kt == 0:
                pe.wait_ge(free[6], JO.turn(i, ("o", g)))
            for s in range(HG):
                ins = M.matmul(bank[6][32 * s:32 * s + 32, :], VP[p][:, kt, HG * g + s, :], pr[:, slot % 2, s, :],
                               start=kt == 0, stop=kt == TT - 1)
            ins.then_inc(S["pv_done"], 1)

        def extra(i, p, job):
            n = i + 2
            kind, k = (job, 0) if isinstance(job, str) else job
            if kind == "cum":
                count_picks(nc, pe, b, w, JM, bank, full, free, S, i - 2, n)
            elif kind == "mT":
                s, last = (i + 1, 31) if k == 0 else (i, 63)
                for q in (last - 1, last):
                    pe.wait_ge(free[JS.bank(("s", q))], JS.drained(s, ("s", q)))
                for t in range(TT):
                    ins = M.transpose(misc[0:NH // 2, t * P:(t + 1) * P], nm[:, t, 8 * k:8 * k + 8], ident[:])
            elif kind == "v":
                for t in (2 * k, 2 * k + 1):
                    for c in range(CT):
                        ins = M.matmul(misc[:, (t % 2) * C:(t % 2 + 1) * C], tT[:, c, t * P:(t + 1) * P], wv[:, c, :],
                                       start=c == 0, stop=c == CT - 1)
            elif kind == "tT":
                pe.wait_ge(S["t0_ready"], i + 3)
                ins = transposes(nc, misc, t0, k, ident)
            elif kind == "qk":
                for c in range(CT):
                    ins = M.matmul(misc[:], wqk[:, c, k * P:(k + 1) * P], tT[:, c, :], start=c == 0, stop=c == CT - 1)
            elif kind == "n":
                pe.wait_ge(free[6], JO.drained(i - 1, ("o", NG - 1)))
                for g in range(NG):
                    ins = M.transpose(misc[:, g * P:(g + 1) * P], oT[:, g, k * P:(k + 1) * P], ident[:])
            elif kind == "nT":
                ins = transposes(nc, misc, on, k, ident)
            elif kind == "y":
                for t in (2 * k, 2 * k + 1):
                    for c in range(CT):
                        ins = M.matmul(misc[:, (t % 2) * C:(t % 2 + 1) * C], nT[:, c, t * P:(t + 1) * P], wo[:, c, :],
                                       start=c == 0, stop=c == CT - 1)
            elif kind == "zT":
                pe.wait_ge(S["z_ready"], i)
                ins = transposes(nc, misc, z, k, ident)
            else:
                logits(nc, pe, nT, wr, JM, bank, full, free, n)
            if kind not in ("cum", "logit"):
                ins.then_inc(misc_full, 1)

        def period(i, p, on_now):
            n = i + 2
            todo = {u: (job, stage) for u, job, stage in MISC}
            for u in range(UNITS):
                g, kt, e = u // 8, u % 8 // 2, u % 2
                if "A" in on_now:
                    if u % 16 == 0:
                        pe.wait_ge(m_in[u // 16], 16 * (i + 1))
                        if u == 16:
                            pe.wait_ge(stacked[1], 16 * HALF_DMAS * (i + 1))
                    pe.wait_ge(free[e], JA.turn(i, ("st", u)))
                    for s in range(2):
                        ins = M.matmul(scores_at[e][:, s, :], KS[p][0:ROWS + 1, 2 * g + e, kt * P:(kt + 1) * P],
                                       QS[p][0:ROWS + 1, HG * g + 2 * e + s, :], start=True, stop=True)
                    ins.then_inc(full[e], 1)
                if u % 2 == 1:
                    if u > 1 and "A" in on_now:
                        products(i, p, u // 2 - 1)
                    if u == 1 and "O" in on_now:
                        products(i - 1, 1 - p, NG * TT - 1)
                if "S" in on_now:
                    h = u // 2
                    if u % 16 == 0:
                        pe.wait_ge(stacked[u // 16], 16 * HALF_DMAS * (i + 2))
                    for t in (2 * e, 2 * e + 1):
                        k = JS.bank(("s", 4 * h + t))
                        pe.wait_ge(free[k], JS.turn(i + 1, ("s", 4 * h + t)))
                        M.matmul(bank[k][:], QS[1 - p][0:ROWS, h, t * P:(t + 1) * P], KS[1 - p][0:ROWS, h // 2, :],
                                 start=True, stop=True).then_inc(full[k], 1)
                if u in todo:
                    job, stage = todo[u]
                    pe.wait_ge(misc_free, JM.turn(n, job))
                    if stage in on_now:
                        extra(i, p, job)
                    else:
                        pe.sem_inc(misc_full, 1)
                        pe.sem_inc(misc_free, 1)

        periods(pe, period)


def phase_combine(nc, ctx, used, a, d, tab, out):
    def sb(name, shape, dt=F32):
        return ctx.enter_context(nc.sbuf_tensor("c_" + name, shape, dt))

    x = [sb(f"x{p}", [P, TT, C]) for p in range(2)]
    got = [sb(f"got{p}", [P, TOPK * TT, C]) for p in range(2)]
    idx = [sb(f"idx{p}", [P, TOPK * TT], U32) for p in range(2)]
    wt = sb("wt", [P, TOPK * TT])
    S = sems(nc, used, "c", "zeroed x_in0 x_in1 first got0 got1 sum_ready out0 out1 dve_own pool_own dve_passed pool_passed pe_passed sp_passed")
    x_in, left = [S["x_in0"], S["x_in1"]], [S["out0"], S["out1"]]
    block = ctx.enter_context(nc.Block())

    @block.sync
    def _(sp):
        for p in range(2):
            sp.dma_start(x[p][:], rows(d["x3"], p)).then_inc(x_in[p], 16)

        def sequence(i, j, p, last):
            sp.wait_ge(S["sum_ready"], i + 1)
            apart(sp, S["sp_passed"])
            sp.dma_start(rows(out, i), x[p][:]).then_inc(left[p], 16)
            if not last:
                sp.wait_ge(left[p], 16 * j + 16)
                apart(sp, S["sp_passed"])
                sp.dma_start(x[p][:], rows(d["x3"], i + 2)).then_inc(x_in[p], 16)

        with sp.Fori(0, NB // 2 - 1) as j:
            for p in range(2):
                sequence(2 * j + p, j, p, False)
        for p in range(2):
            sequence(NB - 2 + p, NB // 2 - 1, p, True)
        for p in range(2):
            sp.wait_ge(left[p], 16 * (NB // 2))

    @block.gpsimd
    def _(pool):
        pool.wait_ge(S["zeroed"], 1)
        chain = Chain(S["pool_own"], pool, 1, S["pool_passed"])
        first = S["first"]
        fetch_rows(nc, pool, got, idx, d, S, tab, 0, 0, lambda ins: (ins.then_inc(first, 1), pool.wait_ge(first, 1)))

        def sequence(i, p, last):
            chain.start(i)
            if not last:
                if last is not None:
                    pool.wait_ge(S["sum_ready"], i)
                fetch_rows(nc, pool, got, idx, d, S, tab, i + 1, 1 - p, chain.link)

        sequence(0, 0, None)
        sequence(1, 1, False)
        with pool.Fori(1, NB // 2 - 1) as j:
            for p in range(2):
                sequence(2 * j + p, p, False)
        sequence(NB - 2, 0, False)

    @block.vector
    def _(dve):
        for p in range(2):
            ins = nc.vector.memset(got[p][:], 0.0)
        ins.then_inc(S["zeroed"], 1)
        chain = Chain(S["dve_own"], dve, 2, S["dve_passed"])
        dve.wait_ge(S["zeroed"], 1)

        def sequence(i, j, p):
            chain.start(i)
            dve.wait_ge(x_in[p], 16 * j + 16)
            dve.wait_ge(S[f"got{p}"], 16 * TOPK * TT * (j + 1))
            combine(nc, chain.link, x[p], got[p], wt, tab, i).then_inc(S["sum_ready"], 1)
            dve.wait_ge(S["sum_ready"], i + 1)
            chain.end()

        with dve.Fori(0, NB // 2) as j:
            for p in range(2):
                sequence(2 * j + p, j, p)


def program(nc, a, out):
    d = {n: nc.dram_tensor(f"d_{n}", (NB * T, C), F32).ap() for n in ("x1", "x2", "x3", "queue", "done")}
    d["bounce"] = {n: nc.dram_tensor(f"d_{n}_parts", (2, C, T), F32).ap() for n in "qk"}
    with ExitStack() as ctx:
        tab = {"idx": ctx.enter_context(nc.sbuf_tensor("tab_idx", [P, NB * TOPK * TT], U32)),
               "w": ctx.enter_context(nc.sbuf_tensor("tab_w", [P, NB * TOPK * TT], F32))}
        for phase, *more in ((phase_local, tab), (phase_experts, "e1_"), (phase_alibi, tab), (phase_experts, "e2_"),
                             (phase_combine, tab, out)):
            with ExitStack() as own:
                used = []
                phase(nc, own, used, a, d, *more)
            nc.clear_and_free_semaphores(used)
            nc.all_engine_barrier()


def shape_constants():
    import numpy as np
    f = np.float32
    none = f(-1e30)
    q, k = np.arange(P), np.arange(QW)
    a, i = q[:, None] // BUCKET, q[:, None] % BUCKET
    b, j = k[None, :] // BUCKET, k[None, :] % BUCKET
    mask_q = np.where((b == a) | ((b == a + 1) & (j <= i)), f(0), none)
    kb, kj = a, i
    qb, qi = b, j
    mask_k = np.where((qb == kb + 1) | ((qb == kb) & (kj <= qi)), f(0), none)
    c = {"c_ident": np.eye(P, dtype=f), "c_masks": np.stack([mask_q, mask_k], 1).astype(f)}
    slot = np.zeros((P, P), f)
    for s in range(HG):
        slot[32 * s + HD, 32 * s:32 * s + 32] = 1
    c["c_slotsum"] = slot
    c["c_tri"] = (q[:, None] <= q[None, :]).astype(f)
    e = np.arange(NE)
    c["c_rev"] = np.broadcast_to((NE - e).astype(f), (P, TT, NE)).copy()
    c["c_base"] = np.broadcast_to((CAP * e - 1).astype(f), (P, TT, NE)).copy()
    c["c_one"] = np.ones((1, NPAIR, KPAD), f)

    def cut(v):
        v = v.astype(f)
        hi = ((v.view(np.uint32) + np.uint32(0x800)) & np.uint32(0xFFFFF000)).view(f)
        return hi, v - hi

    slope = (f(1) / np.power(f(2), np.arange(NH, dtype=f) / f(NH))).astype(f)
    pos = np.arange(T, dtype=f)
    KA, QA = np.zeros((7, NPAIR, T), f), np.zeros((6, NH, T), f)
    for h in range(NH):
        hi, lo = cut(slope[h] * pos)
        KA[2 * (h % 2), h // 2], KA[2 * (h % 2) + 1, h // 2] = hi, lo
        QA[2 * (h % 2), h], QA[2 * (h % 2) + 1, h] = 1, 1
        hi, lo = cut(-slope[h] * pos)
        QA[4, h], QA[5, h] = hi, lo
    KA[4:7] = 1
    return c | {"c_alibi_k": KA, "c_alibi_q": QA}


def kernel(L0_attn_a_x, L0_attn_a_ln1_g, L0_attn_a_ln1_b, L0_attn_a_w_qkv, L0_attn_a_b_qkv, L0_attn_a_w_out,
           L0_attn_a_b_out, L0_attn_a_ln2_g, L0_attn_a_ln2_b, L0_attn_a_w1, L0_attn_a_b1, L0_attn_a_w2, L0_attn_a_b2,
           L0_attn_b_Wq, L0_attn_b_bq, L0_attn_b_Wk, L0_attn_b_bk, L0_attn_b_Wv, L0_attn_b_bv, L0_attn_b_Wo,
           L0_attn_b_bo, L0_ffn_expert_embeddings, L0_ffn_first_linear, L0_ffn_second_linear):
    import numpy as np
    import concourse.bacc as bacc
    from concourse.bass_utils import run_bass_kernel_spmd

    def lay(v):
        return np.ascontiguousarray(v)

    def columns(v):
        return lay(np.transpose(np.reshape(v, (-1, P))))

    arrays = {
        "x": lay(np.reshape(L0_attn_a_x, (NB * T, C))), "ln1_g": columns(L0_attn_a_ln1_g), "ln1_b": columns(L0_attn_a_ln1_b),
        "w_qkv": lay(L0_attn_a_w_qkv), "b_qk": columns(L0_attn_a_b_qkv[0:2 * C]), "b_v": lay(L0_attn_a_b_qkv[2 * C:3 * C]), "w_out": lay(L0_attn_a_w_out),
        "b_out": lay(L0_attn_a_b_out), "ln2_g": columns(L0_attn_a_ln2_g), "ln2_b": columns(L0_attn_a_ln2_b),
        "w1": lay(L0_attn_a_w1), "b1": columns(L0_attn_a_b1), "w2": lay(L0_attn_a_w2), "b2": lay(L0_attn_a_b2),
        "wq": lay(L0_attn_b_Wq), "bq": columns(L0_attn_b_bq), "wk": lay(L0_attn_b_Wk), "bk": columns(L0_attn_b_bk),
        "wv": lay(L0_attn_b_Wv), "bv": lay(L0_attn_b_bv), "wo": lay(L0_attn_b_Wo), "bo": lay(L0_attn_b_bo),
        "router": lay(np.transpose(L0_ffn_expert_embeddings)),
        "first": lay(np.reshape(np.transpose(L0_ffn_first_linear, (0, 2, 1)), (NE * C, EI))),
        "second": lay(np.reshape(np.transpose(L0_ffn_second_linear, (0, 2, 1)), (NE * EI, C))),
    }
    arrays |= shape_constants()
    nc = bacc.Bacc("TRN2", target_bir_lowering=False, num_devices=1)
    a = {n: nc.dram_tensor(f"in_{n}", v.shape, mybir.dt.from_np(v.dtype), kind="ExternalInput").ap()
         for n, v in arrays.items()}
    out = nc.dram_tensor("out", (NB * T, C), F32, kind="ExternalOutput").ap()
    program(nc, a, out)
    r = run_bass_kernel_spmd(nc, [{f"in_{n}": v for n, v in arrays.items()}], core_ids=[0])
    return np.reshape(r.results[0]["out"], (NB, T, C))
```

```python
from contextlib import ExitStack

import concourse.bass as bass
from concourse import mybir

F32 = mybir.dt.float32
F32R = mybir.dt.float32r
BF16 = mybir.dt.bfloat16
U32 = mybir.dt.uint32
ACT = mybir.ActivationFunctionType
ALU = mybir.AluOpType
AX = mybir.AxisListType

P = 128
NB, T, C = 32, 512, 256
TT = T // P
CT = C // P
NH, HD = 16, 16
NPAIR = NH // 2
HG = 4
NG = NH // HG
BUCKET = 64
KPAD = BUCKET + T
NE, TOPK, EI = 8, 2, 512
CAP = NB * T // NE
FF = 4 * C
FT = FF // P
EPS = 1e-5
BIG = 65536.0
STACK = 6 * HD


class Turns:

    def __init__(self, jobs):
        self.per, self.of = {}, {}
        for name, bank in jobs:
            k = self.per.get(bank, 0)
            self.of[name] = (bank, k)
            self.per[bank] = k + 1

    def bank(self, job):
        return self.of[job][0]

    def turn(self, i, job):
        bank, k = self.of[job]
        return i * self.per[bank] + k + 1

    def drained(self, i, job):
        return self.turn(i, job) + 1


class Chain:

    def __init__(self, sem, engine, per, passed):
        self.sem, self.engine, self.per, self.passed, self.n, self.i = sem, engine, per, passed, 0, 0

    def start(self, i):
        self.i, self.n = i, 0

    def link(self, ins):
        self.n += 1
        assert self.n <= self.per, "more links than per"
        ins.then_inc(self.sem, 1)
        self.engine.wait_ge(self.sem, self.i * self.per + self.n)

    def end(self):
        assert self.n == self.per, f"links: {self.n}, per: {self.per}"


def apart(engine, passed):
    engine.sem_inc(passed, 1)


def rows(ap, i):
    return ap[bass.ds(i * T, T), :].rearrange("(t p) c -> p t c", p=P)


def statistics(nc, chain, src, st, mv, ready):
    for t in range(TT):
        ins = nc.vector.bn_stats(st[:, t, :], src[:, t, :])
    chain.link(ins)
    apart(chain.engine, chain.passed)
    for t in range(TT):
        ins = nc.vector.bn_aggr(mv[:, t, :], st[:, t, :])
    ins.then_inc(ready, 1)


def normalize(nc, src, dst, mv, rs):
    return normalize_on(nc.vector, src, dst, mv, rs)


def normalize_on(engine, src, dst, mv, rs):
    for t in range(TT):
        ins = engine.tensor_scalar(dst[:, t, :], src[:, t, :], mv[:, t, 0:1], rs[:, t:t + 1],
                                   ALU.subtract, ALU.mult)
    return ins


def transposes(nc, dst, src, c, ident):
    for t in range(TT):
        ins = nc.tensor.transpose(dst[:, t * P:(t + 1) * P], src[:, t, c * P:(c + 1) * P], ident[:])
    return ins


def route_tiles(sb):
    b = {n: sb(n, [P, TT, NE]) for n in ("lg", "lg2", "eq", "rank", "slot", "prod")}
    b |= {"o": sb("o", [P, TOPK, TT, NE]), "oh": sb("oh", [P, TT * NE], BF16), "carry": sb("carry", [P, NE])}
    b |= {n: sb(n, [P, TOPK, TT]) for n in ("m", "p", "r", "s", "kept")}
    b |= {n: sb(n, [P, TT]) for n in ("pm", "gap", "e2")}
    b["idx"] = sb("idx", [P, TOPK * TT], U32)
    return b


TOP_LINKS, WEIGHT_LINKS, RANK_LINKS = 11, 5, 2 + 8 + 3
ROUTER_LINKS = TOP_LINKS + WEIGHT_LINKS + RANK_LINKS


def over_experts(ap):
    return ap.unsqueeze(2).broadcast_to([P, TT, NE])


def take_logits(nc, dve, b, J, bank, full, free, n):
    k = J.bank("logit")
    dve.wait_ge(full[k], J.turn(n, "logit"))
    nc.vector.tensor_copy(b["lg"][:], bank[k][:, 0:TT * NE].rearrange("p (t e) -> p t e", e=NE)).then_inc(free[k], 1)
    dve.wait_ge(free[k], J.drained(n, "logit"))


def route_top(nc, link, b, w, k):
    V = nc.vector
    src, eq, o, m, pm = (b["lg2"] if k else b["lg"]), b["eq"], b["o"], b["m"], b["pm"]
    link(V.tensor_reduce(m[:, k, :], src[:], AX.X, ALU.max))
    link(V.tensor_tensor(eq[:], src[:], over_experts(m[:, k, :]), ALU.is_equal))
    link(V.tensor_tensor(eq[:], eq[:], w["rev"][:], ALU.mult))
    link(V.tensor_reduce(pm[:], eq[:], AX.X, ALU.max))
    link(V.tensor_tensor(o[:, k, :, :], eq[:], over_experts(pm[:]), ALU.is_equal))
    if k == 0:
        link(V.scalar_tensor_tensor(b["lg2"][:], o[:, 0, :, :], -3e38, b["lg"][:], ALU.mult, ALU.add))


def route_gap(nc, b, S):
    nc.vector.tensor_tensor(b["gap"][:], b["m"][:, 1, :], b["m"][:, 0, :], ALU.subtract).then_inc(S["gap_ready"], 1)


def route_weights(nc, dve, link, b, S, i):
    V = nc.vector
    p, o, pm = b["p"], b["o"], b["pm"]
    dve.wait_ge(S["gap_exp"], i + 1)
    link(V.tensor_scalar(pm[:], b["e2"][:], 1.0, None, ALU.add))
    link(V.reciprocal(p[:, 0, :], pm[:]))
    link(V.tensor_tensor(p[:, 1, :], p[:, 0, :], b["e2"][:], ALU.mult))
    link(V.tensor_scalar(pm[:], p[:, 1, :], 0.0, None, ALU.is_gt))
    link(V.tensor_tensor(o[:, 1, :, :], o[:, 1, :, :], over_experts(pm[:]), ALU.mult))
    V.tensor_tensor(b["oh"][:].rearrange("p (t e) -> p t e", e=NE), o[:, 0, :, :], o[:, 1, :, :],
                    ALU.add).then_inc(S["picks_ready"], 1)


def route_ranks(nc, dve, link, b, w, J, bank, full, free, n, S, i, tab, part=None):
    V = nc.vector
    o, p, rank, slot, r, s, kept, prod = (b[k] for k in ("o", "p", "rank", "slot", "r", "s", "kept", "prod"))
    cum = J.bank("cum")
    if part in (None, 0):
        dve.wait_ge(full[cum], J.turn(n, "cum"))
        link(V.tensor_tensor(rank[:], bank[cum][:, 0:TT * NE].rearrange("p (t e) -> p t e", e=NE),
                             b["carry"][:].unsqueeze(1).broadcast_to([P, TT, NE]), ALU.add))
        V.tensor_tensor(b["carry"][:], bank[cum][:, TT * NE:TT * NE + NE], b["carry"][:], ALU.add).then_inc(free[cum], 1)
        link(V.tensor_tensor(slot[:], rank[:], w["base"][:], ALU.add))
    for k in range(TOPK):
        if part in (None, k + 1):
            for what, dst in ((rank, r), (slot, s)):
                link(V.tensor_tensor(prod[:], o[:, k, :, :], what[:], ALU.mult))
                link(V.tensor_reduce(dst[:, k, :], prod[:], AX.X, ALU.add))
    if part in (None, 2):
        link(V.tensor_scalar(kept[:], r[:], 1.0, None, ALU.is_ge))
        link(V.scalar_tensor_tensor(kept[:], r[:], float(CAP), kept[:], ALU.is_le, ALU.mult))
        link(V.tensor_scalar(r[:], kept[:], -BIG, BIG, ALU.mult, ALU.add))
        V.tensor_tensor(tab["w"][:, bass.ds(i * TOPK * TT, TOPK * TT)].rearrange("p (k t) -> p k t", t=TT),
                        p[:], kept[:], ALU.mult)
        V.tensor_tensor(b["idx"][:].rearrange("p (k t) -> p k t", t=TT), s[:], r[:], ALU.add).then_inc(S["idx_ready"], 1)


def count_picks(nc, pe, b, w, J, bank, full, free, S, i, turn=None):
    n = J.bank("cum")
    pe.wait_ge(free[n], J.turn(i if turn is None else turn, "cum"))
    pe.wait_ge(S["picks_ready"], i + 1)
    for t in range(TT + 1):
        for u in range(min(t + 1, TT)):
            tri = u == t
            ins = nc.tensor.matmul(bank[n][:, t * NE:(t + 1) * NE], (w["tri"] if tri else w["ones"])[:],
                                   b["oh"][:, u * NE:(u + 1) * NE], start=u == 0, stop=u == min(t, TT - 1))
    ins.then_inc(full[n], 1)


def logits(nc, pe, zT, wr, J, bank, full, free, i, passed=None):
    n = J.bank("logit")
    pe.wait_ge(free[n], J.turn(i, "logit"))
    for t in range(TT):
        for c in range(CT):
            ins = nc.tensor.matmul(bank[n][:, t * NE:(t + 1) * NE], zT[:, c, t * P:(t + 1) * P], wr[:, c, :],
                                   start=c == 0, stop=c == CT - 1)
    ins.then_inc(full[n], 1)


def send_rows(nc, pool, z, b, d, S, i, tab):
    issue_rows(nc, pool, z, b, d, S, i, tab)
    pool.wait_ge(S["sent"], 16 * TOPK * TT * (i + 1))


def issue_rows(nc, pool, z, b, d, S, i, tab):
    pool.wait_ge(S["idx_ready"], i + 1)
    apart(pool, S["pool_passed"])
    nc.gpsimd.tensor_copy(tab["idx"][:, bass.ds(i * TOPK * TT, TOPK * TT)], b["idx"][:])
    for n in range(TOPK * TT):
        pool.indirect_dma_start(d["queue"], bass.IndirectOffsetOnAxis(ap=b["idx"][:, n:n + 1], axis=0),
                                z[:, n % TT, :], None, bounds_check=NE * CAP - 1, oob_is_err=False).then_inc(S["sent"], 16)


def root(nc, pool, link, mv, rs, rt, half, stats, turn, done, passed):
    pool.wait_ge(stats, turn)
    apart(pool, passed)
    link(nc.gpsimd.tensor_scalar(rt[:, 0, :], mv[:, :, 1], EPS, None, ALU.add))
    nc.gpsimd.tensor_tensor(rs[:, 0, :], rt[:, 0, :], half[:], ALU.pow).then_inc(done, 1)


def semaphore(nc, used, name):
    used.append(nc.alloc_semaphore(name))
    return used[-1]


def banks(nc, ctx, used, prefix):
    return ([ctx.enter_context(nc.psum_tensor(f"{prefix}_bank{n}", [P, 512], F32)) for n in range(8)],
            [semaphore(nc, used, f"{prefix}_full{n}") for n in range(8)],
            [semaphore(nc, used, f"{prefix}_free{n}") for n in range(8)])


def sems(nc, used, prefix, names):
    return {n: semaphore(nc, used, f"{prefix}_{n}") for n in names.split()}


def open_banks(pe, free):
    for f in free:
        pe.sem_inc(f, 1)


def load_all(engine, sem, loads):
    for dst, src in loads:
        engine.dma_start(dst, src).then_inc(sem, 16)
    return 16 * len(loads)


UNITS = 2 * TT * NG
ALL_STAGES = "FSAOC"
STAGE_LEAD = {"F": 2, "S": 1, "A": 0, "O": -1, "C": -2}


def stages(i):
    return "".join(k for k in ALL_STAGES if 0 <= i + STAGE_LEAD[k] < NB)


def periods(engine, period):
    for i in range(-2, 2):
        period(i, i % 2, stages(i))
    with engine.Fori(1, NB // 2 - 2) as j:
        for p in range(2):
            period(2 * j + p, p, ALL_STAGES)
    for i in range(NB - 4, NB + 2):
        period(i, i % 2, stages(i))


def after(engine, sem, value):
    if not isinstance(value, int) or value > 0:
        engine.wait_ge(sem, value)


def stack_half(sp, QS, KS, half, bounce, sem, kcol=0):
    by_head = {k: v.rearrange("s (f a e d) n -> s f e d a n", f=2, e=2, d=HD) for k, v in bounce.items()}
    for blk, (q, k) in enumerate(((0, 0), (0, 1), (1, 0))):
        for e in range(2):
            to = 3 * HD * e + HD * blk
            sp.dma_start(QS[to:to + HD, 8 * half + e:8 * half + 8:2, :].bitcast(F32), by_head["q"][q, half, e]).then_inc(sem, 16)
            sp.dma_start(KS[to:to + HD, 4 * half:4 * half + 4, kcol:kcol + T].bitcast(F32), by_head["k"][k, half, e]).then_inc(sem, 16)


HALF_DMAS = 12


NKT, QW = 5, 3 * BUCKET


def queries_of(kt):
    q0, q1 = max(0, P * kt - BUCKET), min(T, P * kt + 2 * BUCKET)
    return q0, q1, q0 - (P * kt - BUCKET)


def phase_local(nc, ctx, used, a, d, tab):
    STEPS = 2 * NG * NKT
    MISC = [(0, ("v", 0), "S"), (1, ("mT", 1), "A"), (2, ("v", 1), "S"), (3, ("v", 2), "S"), (4, ("n", 0), "O"),
            (5, ("n", 1), "O"), (6, ("n", 2), "O"), (7, ("n", 3), "O"), (9, ("nT", 0), "O"), (10, ("nT", 1), "O"),
            (12, ("y", 0), "O"), (13, ("hT", 0), "F"), (14, ("y", 1), "O"), (15, ("hT", 1), "F"), (16, ("zT", 0), "C"),
            (17, ("zT", 1), "C"), (18, ("qk", 0), "F"), (19, "logit", "C"), (20, ("qk", 1), "F"), (22, ("qk", 2), "F"),
            (25, ("qk", 3), "F"), (27, "cum", "C"), (30, ("h2T", 0), "O"), (32, ("h2T", 1), "O"), (39, ("mT", 0), "S")]
    on_banks = [(job, (7, 5, 6)[n % 3]) for n, (_, job, _) in enumerate(MISC)]
    MISC += [(STEPS + m, ("f1", m), "O") for m in range(FT)]
    MISC += [(STEPS + 1, ("f2", q), "O") for q in range(2)]
    on_banks += [(("f1", m), 7) for m in range(FT)] + [(("f2", q), 5 + q) for q in range(2)]
    JM = Turns(on_banks)
    AT = {job: u for u, job, _ in MISC}
    JS = Turns([(("s", k), 2 + k % 2) for k in range(TT * NPAIR)])
    JA = Turns([(("st", u), u % 2) for u in range(STEPS)])
    JO = Turns([(("o", g), 4) for g in range(NG)])

    def max_jobs(u):
        if u < STEPS:
            return [2 * (u // 5) + u % 5 // 2] if u % 5 in (0, 2) else []
        return [k for k in (16 + 2 * (u - STEPS), 17 + 2 * (u - STEPS)) if k < TT * NPAIR]

    def sb(name, shape, dt=F32):
        return ctx.enter_context(nc.sbuf_tensor("l_" + name, shape, dt))

    bank, full, free = banks(nc, ctx, used, "l")
    outputs = bank[4]
    ident, identb = sb("ident", [P, P]), sb("identb", [P, P], BF16)
    mask_q, mask_k = sb("mask_q", [P, QW], BF16), sb("mask_k", [P, QW], BF16)
    w = {"tri": sb("tri", [P, P], BF16), "ones": sb("ones", [P, P], BF16),
         "rev": sb("rev", [P, TT, NE]), "base": sb("base", [P, TT, NE])}
    g1, b1, g2, b2 = (sb(n, [P, CT]) for n in ("g1", "b1", "g2", "b2"))
    wqkv, bqk = sb("wqkv", [P, CT, 3 * C]), sb("bqk", [P, 4])
    bv, bo, bf2 = sb("bv", [P, C]), sb("bo", [P, C]), sb("bf2", [P, C])
    wo = sb("wo", [P, CT, C])
    w1, bf1, w2 = sb("w1", [P, CT, FF]), sb("bf1", [P, FT]), sb("w2", [P, FT, C])
    wr, half = sb("wr", [P, CT, NE]), sb("half", [P, TT])
    st = {k: sb("st" + k, [P, TT, 6]) for k in "FOC"}
    mv = {k: sb("mv" + k, [P, TT, 2]) for k in "FOC"}
    rs = {k: sb("rs" + k, [P, 2, TT]) for k in "FOC"}
    rt = {k: sb("rt" + k, [P, 2, TT]) for k in "FOC"}
    x = sb("x", [P, TT, C])
    hT = sb("hT", [P, CT, KPAD])
    parts = [sb(f"parts{n}", [P, 2, T], F32R) for n in range(2)]
    QS, KS = ([sb(f"{n}{p}", [P, heads, width], F32R) for p in range(2)] for n, heads, width in
              (("QS", NH, T), ("KS", NPAIR, KPAD)))
    VP = [sb(f"VP{p}", [P, NKT, NH, 2 * HD]) for p in range(2)]
    nm, mT = sb("nm", [P, TT, NH]), sb("mT", [NH // 2, T], F32R)
    pr, oT = sb("pr", [P, 2, HG, QW]), sb("oT", [P, NG, T])
    sums = sb("sums", [P, TT, NH])
    on = hh = h2 = sb("rows", [P, TT, C])
    nT = sb("nT", [P, CT, T])
    y, res, z = sb("y", [P, TT, C]), sb("res", [P, TT, C]), sb("z", [P, TT, C])
    G = [parts[m // 2][:, m % 2, :].bitcast(F32) for m in range(4)]
    b = route_tiles(sb)
    zero = z
    masks, trif = y[:, 0:2, 0:QW], y[:, 2, 0:P]

    S = sems(nc, used, "l", """weights zeroed zero_ready cleared consts casts x_in statsF statsO statsC rstdF rstdO rstdC
        t0_ready hh_ready hi_ready bounced0 bounced1 stacked0 stacked1 m_in0 m_in1 pv_done sums_own
        t0_out y_in yb_ready h2_ready x_again res_ready x1_out z_ready gap_ready gap_exp picks_ready
        idx_ready sent f_own o_own c_own poolF_own poolR_own poolO_own poolC_own dve_passed pool_passed
        pe_passed sp_passed""")
    bounce, bounced = d["bounce"], [S["bounced0"], S["bounced1"]]
    stacked, m_in = [S["stacked0"], S["stacked1"]], [S["m_in0"], S["m_in1"]]

    def mat(m):
        return m.rearrange("(c p) n -> p c n", p=P)

    loads = [
        (ident[:], a["c_ident"]), (masks, a["c_masks"]), (trif, a["c_tri"]),
        (w["rev"][:], a["c_rev"]), (w["base"][:], a["c_base"]),
        (g1[:], a["ln1_g"]), (b1[:], a["ln1_b"]), (g2[:], a["ln2_g"]), (b2[:], a["ln2_b"]),
        (wqkv[:], mat(a["w_qkv"])), (bqk[:], a["b_qk"]), (wo[:], mat(a["w_out"])),
        (bv[:], a["b_v"].partition_broadcast(P)), (bo[:], a["b_out"].partition_broadcast(P)),
        (bf2[:], a["b2"].partition_broadcast(P)), (w1[:], mat(a["w1"])),
        (bf1[:], a["b1"]), (w2[:], mat(a["w2"])), (wr[:], mat(a["router"])),
    ]
    LOADED = 16 * len(loads)
    queue = d["queue"].rearrange("(n t p) c -> n p t c", t=TT, p=P)
    CLEAR_PERIODS = 2
    CLEARS = NE * CAP // T // CLEAR_PERIODS
    CLEARED = 16 * CLEARS * CLEAR_PERIODS
    block = ctx.enter_context(nc.Block())

    @block.sync
    def _(sp):
        sp.dma_start(x[:], rows(a["x"], 0)).then_inc(S["x_in"], 16)
        load_all(sp, S["weights"], loads)
        sp.wait_ge(S["zero_ready"], 1)
        sp.wait_ge(S["casts"], 32)

        def row_of_maxima(f, buf, s):
            sp.dma_start(QS[buf][STACK:STACK + 1, 8 * f:8 * f + 8, :].bitcast(F32), mT[:, :].bitcast(F32)).then_inc(m_in[f], 16)

        def drained(n, job):
            sp.wait_ge(free[JM.bank(job)], JM.drained(n, job))
            apart(sp, S["sp_passed"])

        def bounce_part(n, m):
            drained(n, ("qk", m))
            sp.dma_start(bounce["qk"[m // 2]][:, (m % 2) * P:(m % 2 + 1) * P, :].rearrange("s p n -> p s n"),
                         parts[m % 2][:].bitcast(F32)).then_inc(bounced[m % 2], 16)

        def period(i, p, on_now):
            n = i + 2
            if "C" in on_now:
                for q in range(2):
                    drained(n - 1, ("f2", q))
                sp.dma_start(rows(d["x1"], i - 2), res[:]).then_inc(S["x1_out"], 16)
            if "S" in on_now:
                after(sp, S["pv_done"], NG * NKT * i)
                apart(sp, S["sp_passed"])
                stack_half(sp, QS[1 - p], KS[1 - p], 1, bounce, stacked[1], BUCKET)
            if "A" in on_now:
                drained(n, ("mT", 1))
                row_of_maxima(1, p, i)
            if "O" in on_now:
                if isinstance(i, int) and i == 1:
                    sp.wait_ge(S["cleared"], CLEARED)
                after(sp, S["res_ready"], i - 1)
                apart(sp, S["sp_passed"])
                sp.dma_start(y[:], rows(d["x2"], i - 1)).then_inc(S["y_in"], 16)
            if "F" in on_now:
                sp.wait_ge(S["t0_ready"], i + 3)
                apart(sp, S["sp_passed"])
                sp.dma_start(rows(d["x2"], i + 2), x[:]).then_inc(S["t0_out"], 16)
            if "O" in on_now:
                after(sp, S["z_ready"], i - 1)
                apart(sp, S["sp_passed"])
                after(sp, S["x1_out"], 16 * (i - 1))
                apart(sp, S["sp_passed"])
                sp.dma_start(res[:], rows(a["x"], i - 1)).then_inc(S["x_again"], 16)
            if "F" in on_now:
                if not isinstance(i, int) or i + 3 < NB:
                    sp.wait_ge(S["hh_ready"], i + 3)
                    apart(sp, S["sp_passed"])
                    sp.wait_ge(S["t0_out"], 16 * (i + 3))
                    apart(sp, S["sp_passed"])
                    sp.dma_start(x[:], rows(a["x"], i + 3)).then_inc(S["x_in"], 16)
                after(sp, stacked[1], 16 * HALF_DMAS * (i + 2))
                apart(sp, S["sp_passed"])
                for m in range(4):
                    bounce_part(n, m)
                for k in range(2):
                    sp.wait_ge(bounced[k], 32 * (i + 3))
                    apart(sp, S["sp_passed"])
                after(sp, S["pv_done"], NG * NKT * i + 2 * NKT)
                apart(sp, S["sp_passed"])
                stack_half(sp, QS[p], KS[p], 0, bounce, stacked[0], BUCKET)
            if "S" in on_now:
                drained(n, ("mT", 0))
                row_of_maxima(0, 1 - p, i + 1)
            if isinstance(i, int) and i < CLEAR_PERIODS - 2:
                for t in range(n * CLEARS, (n + 1) * CLEARS):
                    sp.dma_start(queue[t], zero[:]).then_inc(S["cleared"], 16)

        periods(sp, period)
        sp.wait_ge(S["x1_out"], 16 * NB)
        sp.wait_ge(S["t0_out"], 16 * NB)
        sp.wait_ge(S["cleared"], CLEARED)
        for k in range(2):
            sp.wait_ge(bounced[k], 32 * NB)

    @block.gpsimd
    def _(pool):
        V = nc.gpsimd
        V.memset(half[:], -0.5)
        V.memset(QS[1][:].bitcast(F32), 0.0)
        V.memset(KS[1][:].bitcast(F32), 0.0)
        V.memset(VP[1][:], 0.0).then_inc(S["zeroed"], 1)
        pool.wait_ge(S["zeroed"], 2)
        for p in range(2):
            pool.dma_start(KS[p][STACK:STACK + 1, :, :], a["c_one"]).then_inc(S["casts"], 16)
        chain_f = Chain(S["poolF_own"], pool, 5, S["pool_passed"])
        chain_r = Chain(S["poolR_own"], pool, 1, S["pool_passed"])
        chain_o = Chain(S["poolO_own"], pool, 1, S["pool_passed"])
        chain_c = Chain(S["poolC_own"], pool, 1, S["pool_passed"])
        pool.wait_ge(S["weights"], LOADED)

        def everywhere(bias):
            return bias[:].unsqueeze(1).broadcast_to([P, TT, C])

        def period(i, p, on_now):
            if "C" in on_now:
                chain_c.start(i - 2)
                root(nc, pool, chain_c.link, mv["C"], rs["C"], rt["C"], half, S["statsC"], i - 1, S["rstdC"], S["pool_passed"])
            if "F" in on_now:
                chain_f.start(i + 2)
                pool.wait_ge(S["statsF"], i + 3)
                apart(pool, S["pool_passed"])
                r, u, v = rs["F"], rt["F"], mv["F"][:, :, 1]
                chain_f.link(V.tensor_scalar(u[:, 0, :], v, EPS, None, ALU.add))
                chain_f.link(V.tensor_tensor(r[:, 0, :], u[:, 0, :], half[:], ALU.pow))
                chain_f.link(V.tensor_tensor(u[:, 1, :], r[:, 0, :], r[:, 0, :], ALU.mult))
                chain_f.link(V.tensor_tensor(u[:, 1, :], u[:, 1, :], v, ALU.mult))
                apart(pool, S["pool_passed"])
                chain_f.link(V.tensor_scalar(u[:, 1, :], u[:, 1, :], EPS, None, ALU.add))
                V.tensor_tensor(r[:, 1, :], u[:, 1, :], half[:], ALU.pow).then_inc(S["rstdF"], 1)
            if "O" in on_now:
                pool.wait_ge(S["y_in"], 16 * i)
                V.tensor_tensor(y[:], y[:], everywhere(bo), ALU.add).then_inc(S["yb_ready"], 1)
            if "O" in on_now:
                chain_o.start(i - 1)
                chain_r.start(i - 1)
                root(nc, pool, chain_o.link, mv["O"], rs["O"], rt["O"], half, S["statsO"], i, S["rstdO"], S["pool_passed"])
                pool.wait_ge(S["x_again"], 16 * i)
                chain_r.link(V.tensor_tensor(res[:], res[:], everywhere(bf2), ALU.add))
                pool.wait_ge(S["h2_ready"], i)
                V.tensor_tensor(res[:], res[:], y[:], ALU.add).then_inc(S["res_ready"], 1)
            if "C" in on_now:
                send_rows(nc, pool, z, b, d, S, i - 2, tab)
            if isinstance(i, int) and i == 1:
                pool.wait_ge(S["cleared"], CLEARED)

        periods(pool, period)

    @block.scalar
    def _(act):
        A = nc.scalar
        act.wait_ge(S["weights"], LOADED)
        act.wait_ge(S["consts"], 1)

        def copy(n, job, dst, height=P, func=ACT.Copy, **more):
            k = JM.bank(job)
            act.wait_ge(full[k], JM.turn(n, job))
            A.activation(dst, bank[k][0:height, :], func, **more).then_inc(free[k], 1)

        def period(i, p, on_now):
            n = i + 2
            for u in range(STEPS + FT + 1):
                slot, e = u // 2, u % 2
                if "A" in on_now and u < STEPS:
                    q0, q1, _ = queries_of(slot % NKT)
                    nk, nq = min(P, KPAD - slot % NKT * P), q1 - q0
                    if e == 0:
                        after(act, S["pv_done"], NG * NKT * i + slot - 1)
                    act.wait_ge(full[e], JA.turn(i, ("st", u)))
                    A.activation(pr[0:nk, slot % 2, 2 * e:2 * e + 2, 0:nq],
                                 bank[e][0:nk, 0:2 * nq].rearrange("p (h q) -> p h q", h=2), ACT.Exp).then_inc(free[e], 1)
                if u == AT["mT", 1] and "A" in on_now:
                    act.wait_ge(m_in[0], 16 * (i + 1))
                    copy(n, ("mT", 1), mT[:, :], NH // 2)
                if u == AT["mT", 0] and "S" in on_now:
                    after(act, m_in[1], 16 * (i + 1))
                    copy(n, ("mT", 0), mT[:, :], NH // 2)
                for c in range(CT):
                    if u == AT["hT", c] and "F" in on_now:
                        copy(n, ("hT", c), hT[:, c, BUCKET:], func=ACT.Identity, bias=b1[:, c:c + 1], scale=g1[:, c:c + 1])
                    if u == AT["nT", c] and "O" in on_now:
                        copy(n, ("nT", c), nT[:, c, :])
                    if u == AT["zT", c] and "C" in on_now:
                        copy(n, ("zT", c), nT[:, c, :])
                    if u == AT["h2T", c] and "O" in on_now:
                        copy(n, ("h2T", c), nT[:, c, :], func=ACT.Identity, bias=b2[:, c:c + 1], scale=g2[:, c:c + 1])
                for m in range(4):
                    if u == AT["qk", m] and "F" in on_now:
                        k = JM.bank(("qk", m))
                        after(act, bounced[m % 2], 16 * (2 * (i + 2) + m // 2))
                        act.wait_ge(full[k], JM.turn(n, ("qk", m)))
                        A.activation(parts[m % 2][:, 0, :], bank[k][:], ACT.Identity, bias=bqk[:, m:m + 1]).then_inc(S["hi_ready"], 1)
                if u in (11, 21, 31, 41) and "A" in on_now:
                    g = u // 10 - 1
                    if g == 0:
                        act.wait_ge(full[JM.bank(("n", 3))], JM.turn(n, ("n", 3)))
                    act.wait_ge(S["pv_done"], NKT * (NG * i + g + 1))
                    A.activation(oT[:, g, :], outputs[:], ACT.Copy).then_inc(free[4], 1)
                if u == 22 and "C" in on_now:
                    act.wait_ge(S["gap_ready"], i - 1)
                    A.activation(b["e2"][:], b["gap"][:], ACT.Exp).then_inc(S["gap_exp"], 1)
                if STEPS <= u < STEPS + FT and "O" in on_now:
                    m = u - STEPS
                    if m < 2 and "F" in on_now:
                        act.wait_ge(bounced[m], 32 * (i + 3))
                    copy(n, ("f1", m), G[m % 4], func=ACT.Gelu, bias=bf1[:, m:m + 1])

        periods(act, period)

    @block.vector
    def _(dve):
        V = nc.vector
        chain_f = Chain(S["f_own"], dve, 1, S["dve_passed"])
        chain_o = Chain(S["o_own"], dve, 1, S["dve_passed"])
        chain_c = Chain(S["c_own"], dve, 1 + ROUTER_LINKS, S["dve_passed"])
        V.memset(zero[:], 0.0).then_inc(S["zero_ready"], 1)
        V.memset(QS[0][:].bitcast(F32), 0.0)
        V.memset(KS[0][:].bitcast(F32), 0.0)
        V.memset(VP[0][:], 0.0)
        V.memset(hT[:, :, 0:BUCKET], 0.0)
        V.memset(b["carry"][:], 0.0)
        V.memset(w["ones"][:], 1.0).then_inc(S["zeroed"], 1)
        dve.wait_ge(S["zeroed"], 2)
        for p in range(2):
            V.memset(VP[p][:, :, :, HD:HD + 1], 1.0)
        dve.wait_ge(S["weights"], LOADED)
        V.tensor_copy(identb[:], ident[:])
        V.tensor_copy(mask_q[:], masks[:, 0, :])
        V.tensor_copy(mask_k[:], masks[:, 1, :])
        V.tensor_copy(w["tri"][:], trif)
        V.tensor_scalar(wqkv[:, :, 0:C], wqkv[:, :, 0:C], HD ** -0.5, None, ALU.mult)
        V.tensor_scalar(bqk[:, 0:CT], bqk[:, 0:CT], HD ** -0.5, None, ALU.mult).then_inc(S["consts"], 1)
        dve.wait_ge(S["consts"], 1)

        def add_bias(i, p, q):
            k = JM.bank(("v", q))
            after(dve, S["pv_done"], NG * NKT * i)
            dve.wait_ge(full[k], JM.turn(i + 2, ("v", q)))
            tiles = [t for t in (2 * q, 2 * q + 1) if t < NKT]
            for t in tiles:
                lo, hi, at = (BUCKET if t == 0 else 0), min(P, KPAD - t * P), t % 2 * C
                ins = V.tensor_tensor(VP[p][lo:hi, t, :, 0:HD], bank[k][lo:hi, at:at + C].rearrange("p (h d) -> p h d", d=HD),
                                      bv[lo:hi, :].rearrange("p (h d) -> p h d", d=HD), ALU.add)
            ins.then_inc(free[k], 1)

        def period(i, p, on_now):
            n = i + 2
            for u in range(STEPS + FT + 1):
                for k in max_jobs(u) if "S" in on_now else ():
                    if k == 0 and "A" in on_now:
                        dve.wait_ge(full[JM.bank(("mT", 0))], JM.turn(n - 1, ("mT", 0)))
                    if k == 16 and "A" in on_now:
                        dve.wait_ge(full[JM.bank(("mT", 1))], JM.turn(n, ("mT", 1)))
                    at, hp, t = JS.bank(("s", k)), k // TT, k % TT
                    dve.wait_ge(full[at], JS.turn(i + 1, ("s", k)))
                    V.tensor_reduce(nm[:, t, 2 * hp:2 * hp + 2], bank[at][:, 0:2 * QW].rearrange("p (h k) -> p h k", h=2),
                                    AX.X, ALU.max, negate=True).then_inc(free[at], 1)
                for q in range(3):
                    if u == AT["v", q] and "S" in on_now:
                        add_bias(i, 1 - p, q)
                if "F" in on_now:
                    if u == 1:
                        chain_f.start(i + 2)
                        dve.wait_ge(S["x_in"], 16 * (i + 3))
                        statistics(nc, chain_f, x, st["F"], mv["F"], S["statsF"])
                    if u == 8:
                        dve.wait_ge(S["rstdF"], i + 3)
                        normalize(nc, x, x, mv["F"], rs["F"][:, 0, :]).then_inc(S["t0_ready"], 1)
                    if u == 11:
                        dve.wait_ge(S["t0_ready"], i + 3)
                        for c in range(CT):
                            dve.wait_ge(full[JM.bank(("nT", c))], JM.turn(n, ("nT", c)))
                        for t in range(TT):
                            ins = V.tensor_scalar(hh[:, t, :], x[:, t, :], rs["F"][:, 1, t:t + 1], None, ALU.mult)
                        ins.then_inc(S["hh_ready"], 1)
                    for m in range(4):
                        if u == AT["qk", m]:
                            at = JM.bank(("qk", m))
                            dve.wait_ge(S["hi_ready"], 4 * (i + 2) + m + 1)
                            V.scalar_tensor_tensor(parts[m % 2][:, 1, :], bank[at][:], bqk[:, m:m + 1],
                                                   parts[m % 2][:, 0, :].bitcast(F32), ALU.add, ALU.subtract).then_inc(free[at], 1)
                if "O" in on_now:
                    for t in range(TT):
                        if u == AT["n", t]:
                            at = JM.bank(("n", t))
                            if t == 0:
                                for c in range(CT):
                                    after(dve, full[JM.bank(("h2T", c))], JM.turn(n - 1, ("h2T", c)))
                            dve.wait_ge(full[at], JM.turn(n, ("n", t)))
                            by_head = bank[at][:].rearrange("p (h r) -> p h r", r=2 * HD)
                            V.reciprocal(sums[:, t, :], by_head[:, :, HD]).then_inc(S["sums_own"], 1)
                            dve.wait_ge(S["sums_own"], TT * (i - 1) + t + 1)
                            V.tensor_tensor(on[:, t, :].rearrange("p (h d) -> p h d", d=HD), by_head[:, :, 0:HD],
                                            sums[:, t, :].unsqueeze(2).broadcast_to([P, NH, HD]), ALU.mult).then_inc(free[at], 1)
                    for q in range(2):
                        if u == AT["y", q]:
                            at = JM.bank(("y", q))
                            dve.wait_ge(S["yb_ready"], i)
                            dve.wait_ge(full[at], JM.turn(n, ("y", q)))
                            V.tensor_tensor(y[:, 2 * q:2 * q + 2, :], bank[at][:].rearrange("p (t n) -> p t n", t=2),
                                            y[:, 2 * q:2 * q + 2, :], ALU.add).then_inc(free[at], 1)
                            dve.wait_ge(free[at], JM.drained(n, ("y", q)))
                    if u == AT["y", 1] + 1:
                        chain_o.start(i - 1)
                        statistics(nc, chain_o, y, st["O"], mv["O"], S["statsO"])
                    if u == 24:
                        dve.wait_ge(S["rstdO"], i)
                        normalize(nc, y, h2, mv["O"], rs["O"][:, 0, :]).then_inc(S["h2_ready"], 1)
                    if u == STEPS + FT:
                        dve.wait_ge(S["res_ready"], i)
                        for q in range(2):
                            at = JM.bank(("f2", q))
                            dve.wait_ge(full[at], JM.turn(n, ("f2", q)))
                            V.tensor_tensor(res[:, 2 * q:2 * q + 2, :], bank[at][:].rearrange("p (t n) -> p t n", t=2),
                                            res[:, 2 * q:2 * q + 2, :], ALU.add).then_inc(free[at], 1)
                            dve.wait_ge(free[at], JM.drained(n, ("f2", q)))
                if "C" in on_now:
                    if u == 0:
                        chain_c.start(i - 2)
                        statistics(nc, chain_c, res, st["C"], mv["C"], S["statsC"])
                    if u == 12:
                        dve.wait_ge(S["rstdC"], i - 1)
                        if not isinstance(i, int) or i > 2:
                            dve.wait_ge(S["sent"], 16 * TOPK * TT * (i - 2))
                        normalize(nc, res, z, mv["C"], rs["C"][:, 0, :]).then_inc(S["z_ready"], 1)
                    if u == AT["logit"]:
                        take_logits(nc, dve, b, JM, bank, full, free, n)
                    if u in (AT["logit"], AT["logit"] + 1):
                        route_top(nc, chain_c.link, b, w, u - AT["logit"])
                    if u == AT["logit"] + 2:
                        route_gap(nc, b, S)
                    if u == AT["logit"] + 4:
                        route_weights(nc, dve, chain_c.link, b, S, i - 2)
                    if AT["cum"] <= u < AT["cum"] + 3:
                        route_ranks(nc, dve, chain_c.link, b, w, JM, bank, full, free, n, S, i - 2, tab, u - AT["cum"])
            if isinstance(i, int) and i == 1:
                dve.wait_ge(S["cleared"], CLEARED)

        periods(dve, period)

    @block.tensor
    def _(pe):
        M = nc.tensor
        open_banks(pe, free)
        pe.wait_ge(S["weights"], LOADED)
        pe.wait_ge(S["consts"], 1)

        def drained(n, *some):
            for job in some:
                pe.wait_ge(free[JM.bank(job)], JM.drained(n, job))
                apart(pe, S["pe_passed"])

        def scores(i, p, u):
            g, kt, e = u // (2 * NKT), u // 2 % NKT, u % 2
            hp, (q0, q1, m0) = 2 * g + e, queries_of(kt)
            nk, nq = min(P, KPAD - kt * P), q1 - q0
            pe.wait_ge(free[e], JA.turn(i, ("st", u)))
            apart(pe, S["pe_passed"])
            to = bank[e][0:nk, 0:2 * nq].rearrange("p (h q) -> p h q", h=2)
            M.matmul(to, identb[0:nk, 0:nk], mask_k[0:nk, m0:m0 + nq].unsqueeze(1).broadcast_to([nk, 2, nq]),
                     start=True, stop=False)
            M.matmul(to, KS[p][0:STACK + 1, hp, kt * P:kt * P + nk], QS[p][0:STACK + 1, 2 * hp:2 * hp + 2, q0:q1],
                     start=False, stop=True).then_inc(full[e], 1)

        def products(i, p, slot):
            g, kt = slot // NKT, slot % NKT
            q0, q1, _ = queries_of(kt)
            nk, nq = min(P, KPAD - kt * P), q1 - q0
            if kt == 0:
                pe.wait_ge(free[4], JO.turn(i, ("o", g)))
            for e in range(2):
                pe.wait_ge(free[e], JA.drained(i, ("st", 2 * slot + e)))
            apart(pe, S["pe_passed"])
            for s in range(HG):
                ins = M.matmul(outputs[32 * s:32 * s + 32, q0:q1], VP[p][0:nk, kt, HG * g + s, :],
                               pr[0:nk, slot % 2, s, 0:nq], start=kt == 0, stop=kt == NKT - 1, skip_group_check=True)
            ins.then_inc(S["pv_done"], 1)

        def maxima(i, p, k):
            hp, t, at = k // TT, k % TT, JS.bank(("s", k))
            if k % 16 == 0:
                pe.wait_ge(stacked[k // 16], 16 * HALF_DMAS * (i + 1))
            pe.wait_ge(free[at], JS.turn(i, ("s", k)))
            M.matmul(bank[at][:, 0:2 * QW].rearrange("p (h k) -> p h k", h=2), identb[:],
                     mask_q[:].unsqueeze(1).broadcast_to([P, 2, QW]), start=True, stop=False)
            for e in range(2):
                ins = M.matmul(bank[at][:, e * QW:(e + 1) * QW], QS[p][0:STACK, 2 * hp + e, t * P:(t + 1) * P],
                               KS[p][0:STACK, hp, t * P:t * P + QW], start=False, stop=e == 1)
            ins.then_inc(full[at], 1)

        def second_product(n, m):
            drained(n, ("f1", m))
            for q in range(2):
                for t in (2 * q, 2 * q + 1):
                    ins = M.matmul(bank[5 + q][:, t % 2 * C:(t % 2 + 1) * C], G[m % 4][:, t * P:(t + 1) * P], w2[:, m, :],
                                   start=m == 0 and t % 2 == 0, stop=m == FT - 1, skip_group_check=True)
                if m == FT - 1:
                    ins.then_inc(full[5 + q], 1)

        def extra(i, p, job):
            n = i + 2
            kind, k = (job, 0) if isinstance(job, str) else job
            at = JM.bank(job)
            if kind == "cum":
                count_picks(nc, pe, b, w, JM, bank, full, free, S, i - 2, n)
                return
            if kind == "logit":
                drained(n, ("zT", 0), ("zT", 1))
                logits(nc, pe, nT, wr, JM, bank, full, free, n, S["pe_passed"])
                return
            to = bank[at]
            if kind == "f2":
                return
            if kind == "mT":
                s, last = (i + 1, 15) if k == 0 else (i, 31)
                for q in (last - 1, last):
                    pe.wait_ge(free[JS.bank(("s", q))], JS.drained(s, ("s", q)))
                for t in range(TT):
                    ins = M.transpose(to[0:NH // 2, t * P:(t + 1) * P], nm[:, t, 8 * k:8 * k + 8], ident[:])
            elif kind == "v":
                for t in (2 * k, 2 * k + 1):
                    if t < NKT:
                        width, where = min(P, KPAD - t * P), t % 2 * C
                        for c in range(CT):
                            ins = M.matmul(to[0:width, where:where + C], hT[:, c, t * P:t * P + width],
                                           wqkv[:, c, 2 * C:], start=c == 0, stop=c == CT - 1)
            elif kind == "hT":
                pe.wait_ge(S["hh_ready"], i + 3)
                ins = transposes(nc, to, hh, k, ident)
            elif kind == "qk":
                if k == 0:
                    drained(n, ("hT", 0), ("hT", 1))
                for c in range(CT):
                    ins = M.matmul(to[:], wqkv[:, c, k * P:(k + 1) * P], hT[:, c, BUCKET:], start=c == 0, stop=c == CT - 1)
            elif kind == "n":
                if k == 0:
                    pe.wait_ge(free[4], JO.drained(i - 1, ("o", NG - 1)))
                for g in range(NG):
                    ins = M.transpose(to[:, g * P:(g + 1) * P], oT[:, g, k * P:(k + 1) * P], ident[:])
            elif kind == "nT":
                if k == 0:
                    drained(n, *(("n", t) for t in range(TT)))
                ins = transposes(nc, to, on, k, ident)
            elif kind == "y":
                if k == 0:
                    drained(n, ("nT", 0), ("nT", 1))
                for t in (2 * k, 2 * k + 1):
                    for c in range(CT):
                        ins = M.matmul(to[:, t % 2 * C:(t % 2 + 1) * C], nT[:, c, t * P:(t + 1) * P], wo[:, c, :],
                                       start=c == 0, stop=c == CT - 1)
            elif kind == "zT":
                pe.wait_ge(S["z_ready"], i - 1)
                ins = transposes(nc, to, z, k, ident)
            elif kind == "h2T":
                pe.wait_ge(S["h2_ready"], i)
                ins = transposes(nc, to, h2, k, ident)
            else:
                if k == 0:
                    drained(n, ("h2T", 0), ("h2T", 1))
                for c in range(CT):
                    ins = M.matmul(to[:], w1[:, c, k * P:(k + 1) * P], nT[:, c, :], start=c == 0, stop=c == CT - 1)
            ins.then_inc(full[at], 1)

        def period(i, p, on_now):
            n = i + 2
            for u in range(STEPS + FT + 1):
                if "A" in on_now and u < STEPS:
                    if u % (STEPS // 2) == 0:
                        f = u // (STEPS // 2)
                        pe.wait_ge(m_in[f], 16 * (i + 1))
                        pe.wait_ge(stacked[f], 16 * HALF_DMAS * (i + 1))
                    scores(i, p, u)
                if "A" in on_now and u % 2 == 1 and 0 < u // 2 <= NG * NKT:
                    products(i, p, u // 2 - 1)
                for k in max_jobs(u) if "S" in on_now else ():
                    maxima(i + 1, 1 - p, k)
                for job, stage in ((job, stage) for at, job, stage in MISC if at == u):
                    if stage not in on_now or (job not in ("cum", "logit")):
                        pe.wait_ge(free[JM.bank(job)], JM.turn(n, job))
                        apart(pe, S["pe_passed"])
                    if stage in on_now:
                        extra(i, p, job)
                    else:
                        pe.sem_inc(full[JM.bank(job)], 1)
                        pe.sem_inc(free[JM.bank(job)], 1)
                if u > STEPS and "O" in on_now:
                    second_product(n, u - STEPS - 1)

        periods(pe, period)


def phase_experts(nc, ctx, used, a, d, prefix):
    chunks_of = CAP // T
    CHUNKS, IT = NE * chunks_of, EI // P
    jobs = [(("h", m), 2 + m) for m in range(IT)]
    jobs += [(("xT", c), c) for c in range(CT)]
    jobs += [(("o", q), 6 + q) for q in range(2)]
    J = Turns(jobs)
    HI, LO = 0, 1
    PASSES = ((HI, HI), (HI, LO), (LO, HI))

    def sb(name, shape, dt=F32):
        return ctx.enter_context(nc.sbuf_tensor(prefix + name, shape, dt))

    bank, full, free = banks(nc, ctx, used, prefix)
    ident = sb("ident", [P, P])
    x = [sb(f"x{p}", [P, TT, C]) for p in range(2)]
    whole = {"w1": sb("w1", [P, CT, EI]), "w2": sb("w2", [P, IT, C])}
    w1 = [sb(f"w1p{p}", [P, 2, CT, EI], F32R) for p in range(2)]
    w2 = [sb(f"w2p{p}", [P, 2, IT, C], F32R) for p in range(2)]
    xT, h = sb("xT", [P, 2, CT, T], F32R), sb("h", [P, 2, IT, T], F32R)
    y = [sb(f"y{p}", [P, TT, C]) for p in range(2)]
    S = sems(nc, used, prefix, "ident x_in0 x_in1 w_in w_hi w_lo x_hi h_hi y_out0 y_out1 sp_passed")
    x_in, y_out = ([S[n + str(p)] for p in range(2)] for n in ("x_in", "y_out"))
    block = ctx.enter_context(nc.Block())

    def chunks(engine, chunk):
        per = 2 * chunks_of
        with engine.Fori(0, NE // 2 - 1) as j:
            for q in range(per):
                chunk(per * j + q, j, q)
        for q in range(per):
            chunk(CHUNKS - per + q, NE // 2 - 1, q)

    def exists(n):
        return not isinstance(n, int) or n < CHUNKS

    def weights_next(j, q):
        return 2 * j + q // chunks_of + 1, 1 - q // chunks_of

    @block.sync
    def _(sp):
        sp.dma_start(ident[:], a["c_ident"]).then_inc(S["ident"], 16)

        def load_weights(e):
            sp.dma_start(whole["w1"][:], a["first"][bass.ds(e * C, C), :].rearrange("(c p) i -> p c i", p=P)).then_inc(S["w_in"], 16)
            sp.dma_start(whole["w2"][:], a["second"][bass.ds(e * EI, EI), :].rearrange("(m p) n -> p m n", p=P)).then_inc(S["w_in"], 16)

        def load_rows(n, p):
            sp.dma_start(x[p][:], rows(d["queue"], n)).then_inc(x_in[p], 16)

        def transposed(n):
            for c in range(CT):
                sp.wait_ge(full[J.bank(("xT", c))], J.turn(n, ("xT", c)))
                apart(sp, S["sp_passed"])

        load_rows(0, 0)
        load_weights(0)
        load_rows(1, 1)
        transposed(0)
        load_rows(2, 0)

        def chunk(n, j, q):
            if q % chunks_of == 0:
                e, _ = weights_next(j, q)
                if not isinstance(e, int) or e < NE:
                    sp.wait_ge(S["w_lo"], 2 * e)
                    apart(sp, S["sp_passed"])
                    load_weights(e)
            if exists(n + 3):
                transposed(n + 1)
                load_rows(n + 3, (q + 1) % 2)
            for k in range(2):
                sp.wait_ge(free[J.bank(("o", k))], J.drained(n, ("o", k)))
                apart(sp, S["sp_passed"])
            sp.dma_start(rows(d["done"], n), y[q % 2][:]).then_inc(y_out[q % 2], 16)

        chunks(sp, chunk)
        for p in range(2):
            sp.wait_ge(y_out[p], 16 * (CHUNKS // 2))

    def cut_high(act, e, at, k):
        name, dst = (("w1", w1), ("w2", w2))[k]
        act.wait_ge(S["w_in"], 32 * e + 32)
        nc.scalar.activation(dst[at][:, HI], whole[name][:], ACT.Copy).then_inc(S["w_hi"], 1)

    def cut_low(dve, e, at, k):
        name, dst = (("w1", w1), ("w2", w2))[k]
        dve.wait_ge(S["w_hi"], 2 * e + k + 1)
        nc.vector.tensor_tensor(dst[at][:, LO], whole[name][:], dst[at][:, HI].bitcast(F32), ALU.subtract).then_inc(S["w_lo"], 1)

    @block.scalar
    def _(act):
        def rows_high(n):
            for c in range(CT):
                k = J.bank(("xT", c))
                act.wait_ge(full[k], J.turn(n, ("xT", c)))
                nc.scalar.activation(xT[:, HI, c, :], bank[k][:], ACT.Copy).then_inc(S["x_hi"], 1)

        for k in range(2):
            cut_high(act, 0, 0, k)
        rows_high(0)

        def chunk(n, j, q):
            for m in range(IT):
                k = J.bank(("h", m))
                act.wait_ge(full[k], J.turn(n, ("h", m)))
                nc.scalar.activation(h[:, HI, m, :], bank[k][:], ACT.Relu).then_inc(S["h_hi"], 1)
            if exists(n + 1):
                rows_high(n + 1)
            k = J.bank(("o", 0))
            after(act, y_out[q % 2], 16 * (chunks_of * j + q // 2))
            act.wait_ge(full[k], J.turn(n, ("o", 0)))
            nc.scalar.activation(y[q % 2][:, 0:2, :], bank[k][:].rearrange("p (t c) -> p t c", t=2), ACT.Copy).then_inc(free[k], 1)
            e, at = weights_next(j, q)
            if q % chunks_of in (1, 2) and (not isinstance(e, int) or e < NE):
                cut_high(act, e, at, q % chunks_of - 1)

        chunks(act, chunk)

    @block.vector
    def _(dve):
        V = nc.vector

        def rows_low(n):
            for c in range(CT):
                k = J.bank(("xT", c))
                dve.wait_ge(S["x_hi"], CT * n + c + 1)
                V.tensor_tensor(xT[:, LO, c, :], bank[k][:], xT[:, HI, c, :].bitcast(F32), ALU.subtract).then_inc(free[k], 1)

        for k in range(2):
            cut_low(dve, 0, 0, k)
        rows_low(0)

        def chunk(n, j, q):
            for m in range(IT):
                k = J.bank(("h", m))
                dve.wait_ge(S["h_hi"], IT * n + m + 1)
                V.scalar_tensor_tensor(h[:, LO, m, :], bank[k][:], 0.0, h[:, HI, m, :].bitcast(F32), ALU.max,
                                       ALU.subtract).then_inc(free[k], 1)
            if exists(n + 1):
                rows_low(n + 1)
            k = J.bank(("o", 1))
            after(dve, y_out[q % 2], 16 * (chunks_of * j + q // 2))
            dve.wait_ge(full[k], J.turn(n, ("o", 1)))
            V.tensor_copy(y[q % 2][:, 2:4, :], bank[k][:].rearrange("p (t c) -> p t c", t=2)).then_inc(free[k], 1)
            e, at = weights_next(j, q)
            if q % chunks_of in (1, 2) and (not isinstance(e, int) or e < NE):
                cut_low(dve, e, at, q % chunks_of - 1)

        chunks(dve, chunk)

    @block.tensor
    def _(pe):
        M = nc.tensor
        open_banks(pe, free)
        pe.wait_ge(S["ident"], 16)

        def transpose_rows(n, p, arrived):
            pe.wait_ge(x_in[p], arrived)
            for c in range(CT):
                k = J.bank(("xT", c))
                pe.wait_ge(free[k], J.turn(n, ("xT", c)))
                transposes(nc, bank[k], x[p], c, ident).then_inc(full[k], 1)

        transpose_rows(0, 0, 16)

        def chunk(n, j, q):
            at = q // chunks_of
            if q % chunks_of == 0:
                pe.wait_ge(S["w_lo"], 2 * (2 * j + at) + 2)
            for c in range(CT):
                pe.wait_ge(free[J.bank(("xT", c))], J.drained(n, ("xT", c)))
            for m in range(IT):
                k = J.bank(("h", m))
                pe.wait_ge(free[k], J.turn(n, ("h", m)))
                parts = [(c, wp, xp) for c in range(CT) for wp, xp in PASSES]
                for c, wp, xp in parts:
                    ins = M.matmul(bank[k][:], w1[at][:, wp, c, m * P:(m + 1) * P], xT[:, xp, c, :],
                                   start=(c, wp, xp) == parts[0], stop=(c, wp, xp) == parts[-1])
                ins.then_inc(full[k], 1)
            if exists(n + 1):
                transpose_rows(n + 1, (q + 1) % 2, 16 * (chunks_of * j + (q + 1) // 2 + 1))
            for m in range(IT):
                pe.wait_ge(free[J.bank(("h", m))], J.drained(n, ("h", m)))
            for t in range(TT):
                k = J.bank(("o", t // 2))
                if t % 2 == 0:
                    pe.wait_ge(free[k], J.turn(n, ("o", t // 2)))
                parts = [(m, hp, wp) for m in range(IT) for hp, wp in PASSES]
                for m, hp, wp in parts:
                    ins = M.matmul(bank[k][:, t % 2 * C:(t % 2 + 1) * C], h[:, hp, m, t * P:(t + 1) * P],
                                   w2[at][:, wp, m, :], start=(m, hp, wp) == parts[0], stop=(m, hp, wp) == parts[-1])
                if t % 2 == 1:
                    ins.then_inc(full[k], 1)

        chunks(pe, chunk)


def fetch_rows(nc, pool, got, idx, d, S, tab, i, p, link):
    link(nc.gpsimd.tensor_copy(idx[p][:], tab["idx"][:, bass.ds(i * TOPK * TT, TOPK * TT)]))
    apart(pool, S["pool_passed"])
    for n in range(TOPK * TT):
        pool.indirect_dma_start(got[p][:, n, :], None, d["done"], bass.IndirectOffsetOnAxis(ap=idx[p][:, n:n + 1], axis=0),
                                bounds_check=NE * CAP - 1, oob_is_err=False).then_inc(S[f"got{p}"], 16)


def combine(nc, link, x, got, wt, tab, i):
    link(nc.vector.tensor_copy(wt[:], tab["w"][:, bass.ds(i * TOPK * TT, TOPK * TT)]))
    for k in range(TOPK):
        for t in range(TT):
            n = k * TT + t
            ins = nc.vector.scalar_tensor_tensor(x[:, t, :], got[:, n, :], wt[:, n:n + 1], x[:, t, :], ALU.mult, ALU.add)
        if k == 0:
            link(ins)
    return ins


def phase_alibi(nc, ctx, used, a, d, tab):
    ROWS = STACK + 6
    MISC = [(2, ("v", 0), "S"), (3, ("v", 1), "S"), (4, "cum", "C"), (5, ("n", 0), "O"), (6, ("n", 1), "O"), (7, ("n", 2), "O"),
            (8, ("mT", 1), "A"), (9, ("tT", 0), "F"), (10, ("n", 3), "O"), (11, ("tT", 1), "F"), (12, ("nT", 0), "O"),
            (13, ("qk", 0), "F"), (14, ("nT", 1), "O"), (15, ("qk", 1), "F"), (16, ("y", 0), "O"), (17, ("qk", 2), "F"),
            (18, ("y", 1), "O"), (19, ("qk", 3), "F"), (20, ("mT", 0), "S"), (26, ("zT", 0), "O"), (27, ("zT", 1), "O"),
            (29, "logit", "O")]
    AT = {job: u for u, job, _ in MISC}
    JM = Turns([(job, 6 + n % 2) for n, (_, job, _) in enumerate(MISC)])
    JS = Turns([(("s", n), 2 + n % 3) for n in range(2 * UNITS)])
    JA = Turns([(("st", n), n % 2) for n in range(2 * UNITS)])
    JO = Turns([(("o", g), 5) for g in range(NG)])

    def max_jobs(u):
        first, last, jobs = 8, 3, NH * TT
        rest = UNITS - first - last

        def before(v):
            busy = min(v, first) + max(0, v - (UNITS - last))
            return 3 * busy // 2 + (jobs - 3 * (first + last) // 2) * min(max(0, v - first), rest) // rest

        done = (before(u), before(u + 1))
        return range(*done)

    def sb(name, shape, dt=F32):
        return ctx.enter_context(nc.sbuf_tensor("b_" + name, shape, dt))

    bank, full, free = banks(nc, ctx, used, "b")
    outputs = bank[5]

    ident = sb("ident", [P, P])
    w = {"tri": sb("tri", [P, P], BF16), "ones": sb("ones", [P, P], BF16),
         "rev": sb("rev", [P, TT, NE]), "base": sb("base", [P, TT, NE])}
    wqk, bqk, wv = sb("wqk", [P, CT, 2 * C]), sb("bqk", [P, 4]), sb("wv", [P, CT, C])
    bv, bo, wo = sb("bv", [P, C]), sb("bo", [P, C]), sb("wo", [P, CT, C])
    wr, half = sb("wr", [P, CT, NE]), sb("half", [P, TT])
    x = sb("x", [P, TT, C])
    got = [sb(f"got{p}", [P, TOPK * TT, C]) for p in range(2)]
    idx = [sb(f"idx{p}", [P, TOPK * TT], U32) for p in range(2)]
    wt, t0, tT = sb("wt", [P, TOPK * TT]), sb("t0", [P, TT, C]), sb("tT", [P, CT, T])
    st = {k: sb("st" + k, [P, TT, 6]) for k in "FO"}
    mv = {k: sb("mv" + k, [P, TT, 2]) for k in "FO"}
    rs = {k: sb("rs" + k, [P, 1, TT]) for k in "FO"}
    rt = {k: sb("rt" + k, [P, 1, TT]) for k in "FO"}
    parts = [sb(f"parts{n}", [P, 2, T], F32R) for n in range(2)]
    QS, KS = ([sb(f"{n}{p}", [P, heads, T], F32R) for p in range(2)] for n, heads in (("QS", NH), ("KS", NPAIR)))
    VP = [sb(f"VP{p}", [P, TT, NH, 2 * HD]) for p in range(2)]
    nm, mT = sb("nm", [P, TT, NH]), [sb(f"mT{f}", [NH // 2, T], F32R) for f in range(2)]
    pr, oT = sb("pr", [P, 2, HG, T]), sb("oT", [P, NG, T])
    sums, on, nT = sb("sums", [P, TT, NH]), sb("on", [P, TT, C]), sb("nT", [P, CT, T])
    res, z = sb("res", [P, TT, C]), sb("z", [P, TT, C])
    b = route_tiles(sb)
    trif = z[:, 0, 0:P]
    S = sems(nc, used, "b", """weights zeroed got_zeroed casts consts x_in got0 got1 combined statsF statsO rstdF rstdO
        t0_ready hi_ready bounced0 bounced1 stacked0 stacked1 m_in0 m_in1 pv_done sums_own x2_out
        res_in res_ready x3_out z_ready gap_ready gap_exp picks_ready idx_ready sent fetch_own f_own
        o_own c_own poolF_own poolO_own dve_passed pool_passed pe_passed sp_passed""")
    bounce, bounced = d["bounce"], [S["bounced0"], S["bounced1"]]
    stacked, m_in, got_in = [S["stacked0"], S["stacked1"]], [S["m_in0"], S["m_in1"]], [S["got0"], S["got1"]]

    def mat(m):
        return m.rearrange("(c p) n -> p c n", p=P)

    loads = [
        (ident[:], a["c_ident"]), (trif, a["c_tri"]),
        (w["rev"][:], a["c_rev"]), (w["base"][:], a["c_base"]),
        (wqk[:, :, 0:C], mat(a["wq"])), (wqk[:, :, C:2 * C], mat(a["wk"])), (wv[:], mat(a["wv"])), (wo[:], mat(a["wo"])),
        (bqk[:, 0:CT], a["bq"]), (bqk[:, CT:2 * CT], a["bk"]),
        (bv[:], a["bv"].partition_broadcast(P)), (bo[:], a["bo"].partition_broadcast(P)),
        (wr[:], a["router"].rearrange("(c p) e -> p c e", p=P)),
    ]
    LOADED = 16 * len(loads)
    block = ctx.enter_context(nc.Block())

    def m_row(sp, f, buf, s):
        sp.dma_start(QS[buf][ROWS:ROWS + 1, 8 * f:8 * f + 8, :].bitcast(F32), mT[f][:, :].bitcast(F32)).then_inc(m_in[f], 16)

    @block.sync
    def _(sp):
        load_all(sp, S["weights"], loads)
        sp.dma_start(x[:], rows(d["x1"], 0)).then_inc(S["x_in"], 16)
        sp.wait_ge(S["casts"], 64)

        def period(i, p, on_now):
            n = i + 2
            if "O" in on_now:
                after(sp, S["z_ready"], i - 1)
                apart(sp, S["sp_passed"])
                after(sp, S["x3_out"], 16 * (i - 1))
                apart(sp, S["sp_passed"])
                sp.dma_start(res[:], rows(d["x2"], i - 1)).then_inc(S["res_in"], 16)
            if "S" in on_now:
                after(sp, S["pv_done"], NG * TT * i)
                apart(sp, S["sp_passed"])
                stack_half(sp, QS[1 - p], KS[1 - p], 1, bounce, stacked[1])
            if "F" in on_now:
                sp.wait_ge(S["combined"], i + 3)
                apart(sp, S["sp_passed"])
                sp.dma_start(rows(d["x2"], i + 2), x[:]).then_inc(S["x2_out"], 16)
                if not isinstance(i, int) or i + 3 < NB:
                    sp.wait_ge(S["t0_ready"], i + 3)
                    apart(sp, S["sp_passed"])
                    sp.wait_ge(S["x2_out"], 16 * (i + 3))
                    apart(sp, S["sp_passed"])
                    sp.dma_start(x[:], rows(d["x1"], i + 3)).then_inc(S["x_in"], 16)
            if "A" in on_now:
                sp.wait_ge(free[JM.bank(("mT", 1))], JM.drained(n, ("mT", 1)))
                apart(sp, S["sp_passed"])
                m_row(sp, 1, p, i)
            if "F" in on_now:
                after(sp, stacked[1], 16 * HALF_DMAS * (i + 2))
                apart(sp, S["sp_passed"])
                for m in range(4):
                    sp.wait_ge(free[JM.bank(("qk", m))], JM.drained(n, ("qk", m)))
                    apart(sp, S["sp_passed"])
                    sp.dma_start(bounce["qk"[m // 2]][:, (m % 2) * P:(m % 2 + 1) * P, :].rearrange("s p n -> p s n"),
                                 parts[m % 2][:].bitcast(F32)).then_inc(bounced[m % 2], 16)
                for k in range(2):
                    sp.wait_ge(bounced[k], 32 * (i + 3))
                    apart(sp, S["sp_passed"])
                after(sp, S["pv_done"], NG * TT * i + 8)
                apart(sp, S["sp_passed"])
                stack_half(sp, QS[p], KS[p], 0, bounce, stacked[0])
            if "S" in on_now:
                sp.wait_ge(free[JM.bank(("mT", 0))], JM.drained(n, ("mT", 0)))
                apart(sp, S["sp_passed"])
                m_row(sp, 0, 1 - p, i + 1)
            if "O" in on_now:
                for q in range(2):
                    sp.wait_ge(free[JM.bank(("y", q))], JM.drained(n, ("y", q)))
                    apart(sp, S["sp_passed"])
                sp.dma_start(rows(d["x3"], i - 1), res[:]).then_inc(S["x3_out"], 16)

        periods(sp, period)
        sp.wait_ge(S["x3_out"], 16 * NB)
        sp.wait_ge(S["x2_out"], 16 * NB)
        for k in range(2):
            sp.wait_ge(bounced[k], 32 * NB)

    @block.gpsimd
    def _(pool):
        V = nc.gpsimd
        V.memset(half[:], -0.5)
        fetch = Chain(S["fetch_own"], pool, 1, S["pool_passed"])
        fetch.start(0)
        pool.wait_ge(S["got_zeroed"], 2)
        fetch_rows(nc, pool, got, idx, d, S, tab, 0, 0, fetch.link)
        V.memset(QS[1][:].bitcast(F32), 0.0)
        V.memset(KS[1][:].bitcast(F32), 0.0)
        V.memset(VP[1][:], 0.0).then_inc(S["zeroed"], 1)
        pool.wait_ge(S["zeroed"], 2)
        for p in range(2):
            pool.dma_start(KS[p][STACK:ROWS + 1, :, :], a["c_alibi_k"]).then_inc(S["casts"], 16)
            pool.dma_start(QS[p][STACK:ROWS, :, :], a["c_alibi_q"]).then_inc(S["casts"], 16)
        chain_f = Chain(S["poolF_own"], pool, 1, S["pool_passed"])
        chain_o = Chain(S["poolO_own"], pool, 1, S["pool_passed"])
        pool.wait_ge(S["weights"], LOADED)

        def period(i, p, on_now):
            if "F" in on_now:
                chain_f.start(i + 2)
                root(nc, pool, chain_f.link, mv["F"], rs["F"], rt["F"], half, S["statsF"], i + 3, S["rstdF"], S["pool_passed"])
                pool.wait_ge(S["rstdF"], i + 3)
                apart(pool, S["pool_passed"])
                normalize_on(V, x, t0, mv["F"], rs["F"][:, 0, :]).then_inc(S["t0_ready"], 1)
            if "C" in on_now:
                issue_rows(nc, pool, z, b, d, S, i - 2, tab)
            if "F" in on_now and (not isinstance(i, int) or i + 3 < NB):
                fetch.start(i + 3)
                fetch_rows(nc, pool, got, idx, d, S, tab, i + 3, 1 - p, fetch.link)
            if "O" in on_now:
                pool.wait_ge(S["res_in"], 16 * i)
                apart(pool, S["pool_passed"])
                V.tensor_tensor(res[:], res[:], bo[:].unsqueeze(1).broadcast_to([P, TT, C]), ALU.add).then_inc(S["res_ready"], 1)
            if "C" in on_now:
                pool.wait_ge(S["sent"], 16 * TOPK * TT * (i - 1))
            if "O" in on_now:
                chain_o.start(i - 1)
                root(nc, pool, chain_o.link, mv["O"], rs["O"], rt["O"], half, S["statsO"], i, S["rstdO"], S["pool_passed"])

        periods(pool, period)

    @block.scalar
    def _(act):
        A = nc.scalar
        act.wait_ge(S["weights"], LOADED)
        act.wait_ge(S["consts"], 1)

        def copy(n, job, dst, height=P):
            k = JM.bank(job)
            act.wait_ge(full[k], JM.turn(n, job))
            A.activation(dst, bank[k][0:height, :], ACT.Copy).then_inc(free[k], 1)

        def copy_group(s, g):
            act.wait_ge(S["pv_done"], TT * (NG * s + g + 1))
            A.activation(oT[:, g, :], outputs[:], ACT.Copy).then_inc(free[5], 1)

        def period(i, p, on_now):
            n = i + 2
            for u in range(UNITS):
                slot = u // 2
                if "A" in on_now:
                    if u % 2 == 0:
                        after(act, S["pv_done"], NG * TT * i + slot - 1)
                    for s in range(2):
                        k = JA.bank(("st", 2 * u + s))
                        act.wait_ge(full[k], JA.turn(i, ("st", 2 * u + s)))
                        A.activation(pr[:, slot % 2, 2 * (u % 2) + s, :], bank[k][:], ACT.Exp).then_inc(free[k], 1)
                if u == AT["mT", 1] and "A" in on_now:
                    after(act, m_in[1], 16 * i)
                    copy(n, ("mT", 1), mT[1][:, :], NH // 2)
                if u == 1 and "O" in on_now:
                    copy_group(i - 1, NG - 1)
                for c in range(CT):
                    if u == AT["tT", c] and "F" in on_now:
                        copy(n, ("tT", c), tT[:, c, :])
                    if u == AT["nT", c] and "O" in on_now:
                        copy(n, ("nT", c), nT[:, c, :])
                    if u == AT["zT", c] and "O" in on_now:
                        copy(n, ("zT", c), nT[:, c, :])
                if u in (10, 17, 25) and "A" in on_now:
                    if u == 10:
                        after(act, full[JM.bank(("n", 3))], JM.turn(n, ("n", 3)))
                    copy_group(i, u // 8 - 1)
                for m in range(4):
                    if u == AT["qk", m] and "F" in on_now:
                        after(act, bounced[m % 2], 16 * (2 * (i + 2) + m // 2))
                        act.wait_ge(full[JM.bank(("qk", m))], JM.turn(n, ("qk", m)))
                        A.activation(parts[m % 2][:, 0, :], bank[JM.bank(("qk", m))][:], ACT.Identity,
                                     bias=bqk[:, m:m + 1]).then_inc(S["hi_ready"], 1)
                if u == AT["mT", 0] and "S" in on_now:
                    after(act, m_in[0], 16 * (i + 1))
                    copy(n, ("mT", 0), mT[0][:, :], NH // 2)
                if u == 0 and "C" in on_now:
                    act.wait_ge(S["gap_ready"], i - 1)
                    A.activation(b["e2"][:], b["gap"][:], ACT.Exp).then_inc(S["gap_exp"], 1)

        periods(act, period)

    @block.vector
    def _(dve):
        V = nc.vector
        chain_f = Chain(S["f_own"], dve, 3, S["dve_passed"])
        chain_o = Chain(S["o_own"], dve, 1 + TOP_LINKS, S["dve_passed"])
        chain_c = Chain(S["c_own"], dve, WEIGHT_LINKS + RANK_LINKS, S["dve_passed"])
        for p in range(2):
            V.memset(got[p][:], 0.0).then_inc(S["got_zeroed"], 1)
        V.memset(QS[0][:].bitcast(F32), 0.0)
        V.memset(KS[0][:].bitcast(F32), 0.0)
        V.memset(VP[0][:], 0.0)
        V.memset(b["carry"][:], 0.0)
        V.memset(w["ones"][:], 1.0).then_inc(S["zeroed"], 1)
        dve.wait_ge(S["zeroed"], 2)
        for p in range(2):
            V.memset(VP[p][:, :, :, HD:HD + 1], 1.0)
        dve.wait_ge(S["weights"], LOADED)
        V.tensor_copy(w["tri"][:], trif)
        V.tensor_scalar(wqk[:, :, 0:C], wqk[:, :, 0:C], HD ** -0.5, None, ALU.mult)
        V.tensor_scalar(bqk[:, 0:CT], bqk[:, 0:CT], HD ** -0.5, None, ALU.mult).then_inc(S["consts"], 1)
        dve.wait_ge(S["consts"], 1)

        def add_pick(f, k, buf):
            for t in range(TT):
                ins = V.scalar_tensor_tensor(x[:, t, :], got[buf][:, k * TT + t, :], wt[:, k * TT + t:k * TT + t + 1], x[:, t, :],
                                             ALU.mult, ALU.add)
            return ins

        def period(i, p, on_now):
            n = i + 2
            for u in range(UNITS):
                for k in max_jobs(u) if "S" in on_now else ():
                    if k == 0 and "A" in on_now:
                        dve.wait_ge(full[JM.bank(("mT", 0))], JM.turn(n - 1, ("mT", 0)))
                    if k == 32 and "A" in on_now:
                        dve.wait_ge(full[JM.bank(("mT", 1))], JM.turn(n, ("mT", 1)))
                    at, h, t = JS.bank(("s", k)), k // TT, k % TT
                    dve.wait_ge(full[at], JS.turn(i + 1, ("s", k)))
                    V.tensor_reduce(nm[:, t, h:h + 1], bank[at][:], AX.X, ALU.max, negate=True).then_inc(free[at], 1)
                if "F" in on_now:
                    if u == 0:
                        chain_f.start(i + 2)
                        dve.wait_ge(S["x_in"], 16 * (i + 3))
                        dve.wait_ge(got_in[p], 8 * TOPK * TT * (i - p + 4))
                        chain_f.link(V.tensor_copy(wt[:], tab["w"][:, bass.ds((i + 2) * TOPK * TT, TOPK * TT)]))
                        chain_f.link(add_pick(i + 2, 0, p))
                    if u == 1:
                        add_pick(i + 2, 1, p).then_inc(S["combined"], 1)
                        dve.wait_ge(S["combined"], i + 3)
                    if u == 3:
                        statistics(nc, chain_f, x, st["F"], mv["F"], S["statsF"])
                    for m in range(4):
                        if u == AT["qk", m]:
                            dve.wait_ge(S["hi_ready"], 4 * (i + 2) + m + 1)
                            at = JM.bank(("qk", m))
                            V.scalar_tensor_tensor(parts[m % 2][:, 1, :], bank[at][:], bqk[:, m:m + 1], parts[m % 2][:, 0, :].bitcast(F32),
                                                   ALU.add, ALU.subtract).then_inc(free[at], 1)
                for q in range(2):
                    if u == AT["v", q] and "S" in on_now:
                        after(dve, S["pv_done"], NG * TT * i)
                        dve.wait_ge(full[JM.bank(("v", q))], JM.turn(n, ("v", q)))
                        at = JM.bank(("v", q))
                        V.tensor_tensor(VP[1 - p][:, 2 * q:2 * q + 2, :, 0:HD], bank[at][:].rearrange("p (t h d) -> p t h d", t=2, d=HD),
                                        bv[:].rearrange("p (h d) -> p h d", d=HD).unsqueeze(1).broadcast_to([P, 2, NH, HD]),
                                        ALU.add).then_inc(free[at], 1)
                if "C" in on_now:
                    if u == 2:
                        chain_c.start(i - 2)
                        route_weights(nc, dve, chain_c.link, b, S, i - 2)
                    if u in (5, 6, 7):
                        route_ranks(nc, dve, chain_c.link, b, w, JM, bank, full, free, n, S, i - 2, tab, u - 5)
                if "O" in on_now:
                    if u == 0:
                        chain_o.start(i - 1)
                    for t in range(TT):
                        if u == AT["n", t]:
                            dve.wait_ge(full[JM.bank(("n", t))], JM.turn(n, ("n", t)))
                            at = JM.bank(("n", t))
                            by_head = bank[at][:].rearrange("p (h r) -> p h r", r=2 * HD)
                            V.reciprocal(sums[:, t, :], by_head[:, :, HD]).then_inc(S["sums_own"], 1)
                            dve.wait_ge(S["sums_own"], TT * (i - 1) + t + 1)
                            V.tensor_tensor(on[:, t, :].rearrange("p (h d) -> p h d", d=HD), by_head[:, :, 0:HD],
                                            sums[:, t, :].unsqueeze(2).broadcast_to([P, NH, HD]), ALU.mult).then_inc(free[at], 1)
                    for q in range(2):
                        if u == AT["y", q]:
                            dve.wait_ge(S["res_ready"], i)
                            dve.wait_ge(full[JM.bank(("y", q))], JM.turn(n, ("y", q)))
                            at = JM.bank(("y", q))
                            V.tensor_tensor(res[:, 2 * q:2 * q + 2, :], bank[at][:].rearrange("p (t n) -> p t n", t=2),
                                            res[:, 2 * q:2 * q + 2, :], ALU.add).then_inc(free[at], 1)
                            dve.wait_ge(free[JM.bank(("y", q))], JM.drained(n, ("y", q)))
                    if u == 20:
                        statistics(nc, chain_o, res, st["O"], mv["O"], S["statsO"])
                    if u == 23:
                        dve.wait_ge(S["rstdO"], i)
                        normalize(nc, res, z, mv["O"], rs["O"][:, 0, :]).then_inc(S["z_ready"], 1)
                    if u == AT["logit"]:
                        take_logits(nc, dve, b, JM, bank, full, free, n)
                        route_top(nc, chain_o.link, b, w, 0)
                    if u == AT["logit"] + 1:
                        route_top(nc, chain_o.link, b, w, 1)
                    if u == AT["logit"] + 2:
                        route_gap(nc, b, S)

        periods(dve, period)

    @block.tensor
    def _(pe):
        M = nc.tensor
        open_banks(pe, free)
        pe.wait_ge(S["weights"], LOADED)
        pe.wait_ge(S["consts"], 1)

        def products(i, p, slot):
            g, kt = slot // TT, slot % TT
            if slot == NG * TT - 1:
                for n in (4 * slot + 2, 4 * slot + 3):
                    pe.wait_ge(free[JA.bank(("st", n))], JA.drained(i, ("st", n)))
            if kt == 0:
                pe.wait_ge(free[5], JO.turn(i, ("o", g)))
            for s in range(HG):
                ins = M.matmul(outputs[32 * s:32 * s + 32, :], VP[p][:, kt, HG * g + s, :], pr[:, slot % 2, s, :],
                               start=kt == 0, stop=kt == TT - 1)
            ins.then_inc(S["pv_done"], 1)

        def drained(n, *some):
            for job in some:
                pe.wait_ge(free[JM.bank(job)], JM.drained(n, job))
                apart(pe, S["pe_passed"])

        def extra(i, p, job):
            n = i + 2
            kind, k = (job, 0) if isinstance(job, str) else job
            to = bank[JM.bank(job)]
            if kind == "cum":
                count_picks(nc, pe, b, w, JM, bank, full, free, S, i - 2, n)
            elif kind == "mT":
                s, last = (i + 1, 31) if k == 0 else (i, 63)
                for q in (last - 1, last):
                    pe.wait_ge(free[JS.bank(("s", q))], JS.drained(s, ("s", q)))
                for t in range(TT):
                    ins = M.transpose(to[0:NH // 2, t * P:(t + 1) * P], nm[:, t, 8 * k:8 * k + 8], ident[:])
            elif kind == "v":
                for t in (2 * k, 2 * k + 1):
                    for c in range(CT):
                        ins = M.matmul(to[:, (t % 2) * C:(t % 2 + 1) * C], tT[:, c, t * P:(t + 1) * P], wv[:, c, :],
                                       start=c == 0, stop=c == CT - 1)
            elif kind == "tT":
                pe.wait_ge(S["t0_ready"], i + 3)
                ins = transposes(nc, to, t0, k, ident)
            elif kind == "qk":
                if k == 0:
                    drained(n, ("tT", 0), ("tT", 1))
                for c in range(CT):
                    ins = M.matmul(to[:], wqk[:, c, k * P:(k + 1) * P], tT[:, c, :], start=c == 0, stop=c == CT - 1)
            elif kind == "n":
                pe.wait_ge(free[5], JO.drained(i - 1, ("o", NG - 1)))
                for g in range(NG):
                    ins = M.transpose(to[:, g * P:(g + 1) * P], oT[:, g, k * P:(k + 1) * P], ident[:])
            elif kind == "nT":
                if k == 0:
                    drained(n, *(("n", t) for t in range(TT)))
                ins = transposes(nc, to, on, k, ident)
            elif kind == "y":
                if k == 0:
                    drained(n, ("nT", 0), ("nT", 1))
                for t in (2 * k, 2 * k + 1):
                    for c in range(CT):
                        ins = M.matmul(to[:, (t % 2) * C:(t % 2 + 1) * C], nT[:, c, t * P:(t + 1) * P], wo[:, c, :],
                                       start=c == 0, stop=c == CT - 1)
            elif kind == "zT":
                pe.wait_ge(S["z_ready"], i)
                ins = transposes(nc, to, z, k, ident)
            else:
                drained(n, ("zT", 0), ("zT", 1))
                logits(nc, pe, nT, wr, JM, bank, full, free, n, S["pe_passed"])
            if kind not in ("cum", "logit"):
                ins.then_inc(full[JM.bank(job)], 1)

        def period(i, p, on_now):
            n = i + 2
            todo = {u: (job, stage) for u, job, stage in MISC}
            for u in range(UNITS):
                g, kt, e = u // 8, u % 8 // 2, u % 2
                if "A" in on_now:
                    if u % 16 == 0:
                        pe.wait_ge(m_in[u // 16], 16 * (i + 1))
                        if u == 16:
                            pe.wait_ge(stacked[1], 16 * HALF_DMAS * (i + 1))
                    for s in range(2):
                        k = JA.bank(("st", 2 * u + s))
                        pe.wait_ge(free[k], JA.turn(i, ("st", 2 * u + s)))
                        M.matmul(bank[k][:], KS[p][0:ROWS + 1, 2 * g + e, kt * P:(kt + 1) * P],
                                 QS[p][0:ROWS + 1, HG * g + 2 * e + s, :], start=True, stop=True).then_inc(full[k], 1)
                if u % 2 == 1:
                    if u > 1 and "A" in on_now:
                        products(i, p, u // 2 - 1)
                    if u == 1 and "O" in on_now:
                        products(i - 1, 1 - p, NG * TT - 1)
                for k in max_jobs(u) if "S" in on_now else ():
                    at, h, t = JS.bank(("s", k)), k // TT, k % TT
                    if k % 32 == 0:
                        pe.wait_ge(stacked[k // 32], 16 * HALF_DMAS * (i + 2))
                    pe.wait_ge(free[at], JS.turn(i + 1, ("s", k)))
                    M.matmul(bank[at][:], QS[1 - p][0:ROWS, h, t * P:(t + 1) * P], KS[1 - p][0:ROWS, h // 2, :],
                             start=True, stop=True).then_inc(full[at], 1)
                if u in todo:
                    job, stage = todo[u]
                    if stage not in on_now or job not in ("cum", "logit"):
                        pe.wait_ge(free[JM.bank(job)], JM.turn(n, job))
                        apart(pe, S["pe_passed"])
                    if stage in on_now:
                        extra(i, p, job)
                    else:
                        pe.sem_inc(full[JM.bank(job)], 1)
                        pe.sem_inc(free[JM.bank(job)], 1)

        periods(pe, period)


def phase_combine(nc, ctx, used, a, d, tab, out):
    def sb(name, shape, dt=F32):
        return ctx.enter_context(nc.sbuf_tensor("c_" + name, shape, dt))

    x = [sb(f"x{p}", [P, TT, C]) for p in range(2)]
    got = [sb(f"got{p}", [P, TOPK * TT, C]) for p in range(2)]
    idx = [sb(f"idx{p}", [P, TOPK * TT], U32) for p in range(2)]
    wt = sb("wt", [P, TOPK * TT])
    S = sems(nc, used, "c", """zeroed x_in0 x_in1 first got0 got1 sum_ready out0 out1 dve_own pool_own dve_passed pool_passed
        sp_passed""")
    x_in, left = [S["x_in0"], S["x_in1"]], [S["out0"], S["out1"]]
    block = ctx.enter_context(nc.Block())

    @block.sync
    def _(sp):
        for p in range(2):
            sp.dma_start(x[p][:], rows(d["x3"], p)).then_inc(x_in[p], 16)

        def sequence(i, j, p, last):
            sp.wait_ge(S["sum_ready"], i + 1)
            apart(sp, S["sp_passed"])
            sp.dma_start(rows(out, i), x[p][:]).then_inc(left[p], 16)
            if not last:
                sp.wait_ge(left[p], 16 * j + 16)
                apart(sp, S["sp_passed"])
                sp.dma_start(x[p][:], rows(d["x3"], i + 2)).then_inc(x_in[p], 16)

        with sp.Fori(0, NB // 2 - 1) as j:
            for p in range(2):
                sequence(2 * j + p, j, p, False)
        for p in range(2):
            sequence(NB - 2 + p, NB // 2 - 1, p, True)
        for p in range(2):
            sp.wait_ge(left[p], 16 * (NB // 2))

    @block.gpsimd
    def _(pool):
        pool.wait_ge(S["zeroed"], 1)
        chain = Chain(S["pool_own"], pool, 1, S["pool_passed"])
        first = S["first"]
        fetch_rows(nc, pool, got, idx, d, S, tab, 0, 0, lambda ins: (ins.then_inc(first, 1), pool.wait_ge(first, 1)))

        def sequence(i, p, last):
            chain.start(i)
            if not last:
                if last is not None:
                    pool.wait_ge(S["sum_ready"], i)
                fetch_rows(nc, pool, got, idx, d, S, tab, i + 1, 1 - p, chain.link)

        sequence(0, 0, None)
        sequence(1, 1, False)
        with pool.Fori(1, NB // 2 - 1) as j:
            for p in range(2):
                sequence(2 * j + p, p, False)
        sequence(NB - 2, 0, False)

    @block.vector
    def _(dve):
        for p in range(2):
            ins = nc.vector.memset(got[p][:], 0.0)
        ins.then_inc(S["zeroed"], 1)
        chain = Chain(S["dve_own"], dve, 2, S["dve_passed"])
        dve.wait_ge(S["zeroed"], 1)

        def sequence(i, j, p):
            chain.start(i)
            dve.wait_ge(x_in[p], 16 * j + 16)
            dve.wait_ge(S[f"got{p}"], 16 * TOPK * TT * (j + 1))
            combine(nc, chain.link, x[p], got[p], wt, tab, i).then_inc(S["sum_ready"], 1)
            dve.wait_ge(S["sum_ready"], i + 1)
            chain.end()

        with dve.Fori(0, NB // 2) as j:
            for p in range(2):
                sequence(2 * j + p, j, p)


def program(nc, a, out):
    d = {n: nc.dram_tensor(f"d_{n}", (NB * T, C), F32).ap() for n in ("x1", "x2", "x3", "queue", "done")}
    d["bounce"] = {n: nc.dram_tensor(f"d_{n}_parts", (2, C, T), F32).ap() for n in "qk"}
    with ExitStack() as ctx:
        tab = {"idx": ctx.enter_context(nc.sbuf_tensor("tab_idx", [P, NB * TOPK * TT], U32)),
               "w": ctx.enter_context(nc.sbuf_tensor("tab_w", [P, NB * TOPK * TT], F32))}
        for phase, *more in ((phase_local, tab), (phase_experts, "e1_"), (phase_alibi, tab), (phase_experts, "e2_"),
                             (phase_combine, tab, out)):
            with ExitStack() as own:
                used = []
                phase(nc, own, used, a, d, *more)
            nc.clear_and_free_semaphores(used)
            nc.all_engine_barrier()


def shape_constants():
    import numpy as np
    f = np.float32
    none = f(-1e30)
    q, k = np.arange(P), np.arange(QW)
    a, i = q[:, None] // BUCKET, q[:, None] % BUCKET
    b, j = k[None, :] // BUCKET, k[None, :] % BUCKET
    mask_q = np.where((b == a) | ((b == a + 1) & (j <= i)), f(0), none)
    kb, kj = a, i
    qb, qi = b, j
    mask_k = np.where((qb == kb + 1) | ((qb == kb) & (kj <= qi)), f(0), none)
    c = {"c_ident": np.eye(P, dtype=f), "c_masks": np.stack([mask_q, mask_k], 1).astype(f)}
    c["c_tri"] = (q[:, None] <= q[None, :]).astype(f)
    e = np.arange(NE)
    c["c_rev"] = np.broadcast_to((NE - e).astype(f), (P, TT, NE)).copy()
    c["c_base"] = np.broadcast_to((CAP * e - 1).astype(f), (P, TT, NE)).copy()
    c["c_one"] = np.ones((1, NPAIR, KPAD), f)

    def cut(v):
        v = v.astype(f)
        hi = ((v.view(np.uint32) + np.uint32(0x800)) & np.uint32(0xFFFFF000)).view(f)
        return hi, v - hi

    slope = (f(1) / np.power(f(2), np.arange(NH, dtype=f) / f(NH))).astype(f)
    pos = np.arange(T, dtype=f)
    KA, QA = np.zeros((7, NPAIR, T), f), np.zeros((6, NH, T), f)
    for h in range(NH):
        hi, lo = cut(slope[h] * pos)
        KA[2 * (h % 2), h // 2], KA[2 * (h % 2) + 1, h // 2] = hi, lo
        QA[2 * (h % 2), h], QA[2 * (h % 2) + 1, h] = 1, 1
        hi, lo = cut(-slope[h] * pos)
        QA[4, h], QA[5, h] = hi, lo
    KA[4:7] = 1
    return c | {"c_alibi_k": KA, "c_alibi_q": QA}


def kernel(L0_attn_a_x, L0_attn_a_ln1_g, L0_attn_a_ln1_b, L0_attn_a_w_qkv, L0_attn_a_b_qkv, L0_attn_a_w_out,
           L0_attn_a_b_out, L0_attn_a_ln2_g, L0_attn_a_ln2_b, L0_attn_a_w1, L0_attn_a_b1, L0_attn_a_w2, L0_attn_a_b2,
           L0_attn_b_Wq, L0_attn_b_bq, L0_attn_b_Wk, L0_attn_b_bk, L0_attn_b_Wv, L0_attn_b_bv, L0_attn_b_Wo,
           L0_attn_b_bo, L0_ffn_expert_embeddings, L0_ffn_first_linear, L0_ffn_second_linear):
    import numpy as np
    import concourse.bacc as bacc
    from concourse.bass_utils import run_bass_kernel_spmd

    def lay(v):
        return np.ascontiguousarray(v)

    def columns(v):
        return lay(np.transpose(np.reshape(v, (-1, P))))

    arrays = {
        "x": lay(np.reshape(L0_attn_a_x, (NB * T, C))), "ln1_g": columns(L0_attn_a_ln1_g), "ln1_b": columns(L0_attn_a_ln1_b),
        "w_qkv": lay(L0_attn_a_w_qkv), "b_qk": columns(L0_attn_a_b_qkv[0:2 * C]), "b_v": lay(L0_attn_a_b_qkv[2 * C:3 * C]),
        "w_out": lay(L0_attn_a_w_out),
        "b_out": lay(L0_attn_a_b_out), "ln2_g": columns(L0_attn_a_ln2_g), "ln2_b": columns(L0_attn_a_ln2_b),
        "w1": lay(L0_attn_a_w1), "b1": columns(L0_attn_a_b1), "w2": lay(L0_attn_a_w2), "b2": lay(L0_attn_a_b2),
        "wq": lay(L0_attn_b_Wq), "bq": columns(L0_attn_b_bq), "wk": lay(L0_attn_b_Wk), "bk": columns(L0_attn_b_bk),
        "wv": lay(L0_attn_b_Wv), "bv": lay(L0_attn_b_bv), "wo": lay(L0_attn_b_Wo), "bo": lay(L0_attn_b_bo),
        "router": lay(np.transpose(L0_ffn_expert_embeddings)),
        "first": lay(np.reshape(np.transpose(L0_ffn_first_linear, (0, 2, 1)), (NE * C, EI))),
        "second": lay(np.reshape(np.transpose(L0_ffn_second_linear, (0, 2, 1)), (NE * EI, C))),
    }
    arrays |= shape_constants()
    nc = bacc.Bacc("TRN2", target_bir_lowering=False, num_devices=1)
    a = {n: nc.dram_tensor(f"in_{n}", v.shape, mybir.dt.from_np(v.dtype), kind="ExternalInput").ap()
         for n, v in arrays.items()}
    out = nc.dram_tensor("out", (NB * T, C), F32, kind="ExternalOutput").ap()
    program(nc, a, out)
    r = run_bass_kernel_spmd(nc, [{f"in_{n}": v for n, v in arrays.items()}], core_ids=[0])
    return np.reshape(r.results[0]["out"], (NB, T, C))
```
